# Optimizing a Trainium2 kernel written in Bass

```python
import numpy as np
import jax
import jax.numpy as jnp

def _softmax(x, axis=-1):
    return jax.nn.softmax(x, axis=axis)

def _gelu(x):
    return jax.nn.gelu(x, approximate=True)

def _silu(x):
    return jax.nn.silu(x)

def _sigmoid(x):
    return jax.nn.sigmoid(x)

def _layernorm(x, axis=-1, eps=1e-05):
    m = jnp.mean(x, axis=axis, keepdims=True)
    v = jnp.var(x, axis=axis, keepdims=True)
    return (x - m) / jnp.sqrt(v + eps)

def _scatter_add(tgt, idx, src, axis=0):
    return tgt.at[idx].add(src)

def _segment_sum(src, seg, n):
    return jax.ops.segment_sum(src, seg, n)
kernel_name = 'mk_vit_tower_cls_d2_tok_img256_r4_427aee'

def setup_inputs(seed: int=0):
    np.random.seed(seed)
    _w = jnp.asarray

    def _rec_inputs():
        import jax
        import jax.numpy as jnp
        _rk = jax.random.key(seed)
        x = -0.00040386 + 0.999972 * jax.random.normal(jax.random.fold_in(_rk, 1), (4, 3, 64, 64), jnp.float32)
        cls_tok = 0.02 * jax.random.normal(jax.random.fold_in(_rk, 5), (1, 1, 64), jnp.float32)
        return (x, cls_tok)
    x, cls_tok = _rec_inputs()

    def _L0_tok_setup():
        import jax, jax.numpy as jnp
        import numpy as np
        EPS = 1e-05
        P = 8
        DIM = 64
        NUM_TOKENS = 64
        PATCH_DIM = 3 * P * P

        def layernorm(x, g, b):
            mu = jnp.mean(x, axis=-1, keepdims=True)
            var = jnp.mean(jnp.square(x - mu), axis=-1, keepdims=True)
            return (x - mu) * jax.lax.rsqrt(var + EPS) * g + b
        key = jax.random.key(seed)
        ks = jax.random.split(key, 8)
        b, c, h, w = (16, 3, 128, 128)
        x = jax.random.normal(ks[0], (b, c, h, w), dtype=jnp.float32)
        ln1_g = jnp.ones((PATCH_DIM,), jnp.float32)
        ln1_b = jnp.zeros((PATCH_DIM,), jnp.float32)
        W1 = jax.random.normal(ks[1], (PATCH_DIM, DIM), jnp.float32) * 0.02
        b1 = jnp.zeros((DIM,), jnp.float32)
        ln2_g = jnp.ones((DIM,), jnp.float32)
        ln2_b = jnp.zeros((DIM,), jnp.float32)
        Wp1 = jax.random.normal(ks[2], (DIM, DIM), jnp.float32) * 0.02
        bp1 = jnp.zeros((DIM,), jnp.float32)
        lnp_g = jnp.ones((DIM,), jnp.float32)
        lnp_b = jnp.zeros((DIM,), jnp.float32)
        Wp2 = jax.random.normal(ks[3], (DIM, NUM_TOKENS), jnp.float32) * 0.02
        bp2 = jnp.zeros((NUM_TOKENS,), jnp.float32)
        return {'x': x, 'ln1_g': ln1_g, 'ln1_b': ln1_b, 'W1': W1, 'b1': b1, 'ln2_g': ln2_g, 'ln2_b': ln2_b, 'Wp1': Wp1, 'bp1': bp1, 'lnp_g': lnp_g, 'lnp_b': lnp_b, 'Wp2': Wp2, 'bp2': bp2}
    _L0_tok_all = _L0_tok_setup()
    _L0_tok_in = {k: v for k, v in _L0_tok_all.items() if k in ('ln1_g', 'ln1_b', 'W1', 'b1', 'ln2_g', 'ln2_b', 'Wp1', 'bp1', 'lnp_g', 'lnp_b', 'Wp2', 'bp2')}
    del _L0_tok_all

    def _L0_attn_setup():
        import jax, jax.numpy as jnp
        import numpy as np
        import math
        key = jax.random.key(seed)
        ks = jax.random.split(key, 7)
        d_input, d_state, d_output = (64, 64, 64)
        B_, S_ = (8, 1024)
        x = jax.random.normal(ks[0], (B_, S_, d_input), dtype=jnp.float32)
        log_lambda_real = jax.random.normal(ks[1], (d_state,), dtype=jnp.float32)
        lambda_imag = jax.random.normal(ks[2], (d_state,), dtype=jnp.float32)
        dt = jnp.clip(0.01 + jax.random.normal(ks[3], (d_state,), dtype=jnp.float32) * 0.01, 0.005, 0.1)
        log_dt = jnp.log(dt)
        B = jax.random.normal(ks[4], (d_state, d_input), dtype=jnp.float32) / d_state ** 0.5
        C_real = jax.random.normal(ks[5], (d_output, d_state), dtype=jnp.float32) / d_state ** 0.5
        C_imag = jax.random.normal(ks[6], (d_output, d_state), dtype=jnp.float32) / d_state ** 0.5
        return {'x': x, 'log_lambda_real': log_lambda_real, 'lambda_imag': lambda_imag, 'log_dt': log_dt, 'B': B, 'C_real': C_real, 'C_imag': C_imag}
    _L0_attn_all = _L0_attn_setup()
    _L0_attn_in = {k: v for k, v in _L0_attn_all.items() if k in ('log_lambda_real', 'lambda_imag', 'log_dt', 'B', 'C_real', 'C_imag')}
    del _L0_attn_all

    def _L0_ffn_setup():
        import jax, jax.numpy as jnp
        import numpy as np
        DIM = 64
        HEADS = 8
        NUM_KEYS = 64
        NUM_KV = NUM_KEYS ** 2
        PK_TOPK = 16
        FINAL_TOPK = 16
        DIM_KEY = DIM // 2
        P = 2

        def _pk(x, Wq_pk, pk_keys):
            b, n, _ = x.shape
            q = (x @ Wq_pk).reshape(b, n, P, HEADS, DIM_KEY).transpose(2, 0, 1, 3, 4)
            sim = jnp.einsum('pbnhd,pkhd->pbnhk', q, pk_keys)
            scores, idx = jax.lax.top_k(sim, PK_TOPK)
            idx0 = idx[0]
            idx1 = idx[1] * NUM_KEYS
            index = (idx0[..., :, None] + idx1[..., None, :]).reshape(b, n, HEADS, PK_TOPK * PK_TOPK)
            score = (scores[0][..., :, None] + scores[1][..., None, :]).reshape(b, n, HEADS, PK_TOPK * PK_TOPK)
            final_scores, pk_idx = jax.lax.top_k(score, FINAL_TOPK)
            final_indices = jnp.take_along_axis(index, pk_idx, axis=-1)
            final_scores = jax.nn.softmax(final_scores, axis=-1)
            return (final_scores, final_indices)
        key = jax.random.key(seed)
        ks = jax.random.split(key, 7)
        b, n = (2, 256)
        std = 0.02
        x = jax.random.normal(ks[0], (b, n, DIM), dtype=jnp.float32)
        Wq_pk = jax.random.normal(ks[1], (DIM, P * HEADS * DIM_KEY), dtype=jnp.float32) * std
        pk_keys = jax.random.normal(ks[2], (P, NUM_KEYS, HEADS, DIM_KEY), dtype=jnp.float32) * std
        Wq = jax.random.normal(ks[3], (DIM, HEADS * DIM), dtype=jnp.float32) * std
        keys_table = jax.random.normal(ks[4], (NUM_KV * HEADS, DIM), dtype=jnp.float32) * std
        values_table = jax.random.normal(ks[5], (NUM_KV * HEADS, DIM), dtype=jnp.float32) * std
        Wo = jax.random.normal(ks[6], (DIM * HEADS, DIM), dtype=jnp.float32) * std
        return {'x': x, 'Wq_pk': Wq_pk, 'pk_keys': pk_keys, 'Wq': Wq, 'keys_table': keys_table, 'values_table': values_table, 'Wo': Wo}
    _L0_ffn_all = _L0_ffn_setup()
    _L0_ffn_in = {k: v for k, v in _L0_ffn_all.items() if k in ('Wq_pk', 'pk_keys', 'Wq', 'keys_table', 'values_table', 'Wo')}
    del _L0_ffn_all

    def _L1_attn_setup():
        import jax, jax.numpy as jnp
        import numpy as np
        MEMORY_SIZE = 40
        INPUT_SIZE = 64
        OUTPUT_SIZE = 64
        BATCH = 16
        SEQ = 1024
        key = jax.random.key(seed)
        k1, k2, k3, k4 = jax.random.split(key, 4)
        x = jax.random.normal(k1, (BATCH, SEQ, INPUT_SIZE), dtype=jnp.float32)
        lim_w = float(np.sqrt(6.0 / (INPUT_SIZE + OUTPUT_SIZE)))
        W1 = jax.random.uniform(k2, (INPUT_SIZE, OUTPUT_SIZE), minval=-lim_w, maxval=lim_w, dtype=jnp.float32)
        W2 = jax.random.uniform(k3, (INPUT_SIZE, OUTPUT_SIZE), minval=-lim_w, maxval=lim_w, dtype=jnp.float32)
        bias = jnp.ones((OUTPUT_SIZE,), dtype=jnp.float32)
        lim_m = float(np.sqrt(6.0 / (MEMORY_SIZE + 1 + INPUT_SIZE)))
        mw = jax.random.uniform(k4, (MEMORY_SIZE + 1, INPUT_SIZE), minval=-lim_m, maxval=lim_m, dtype=jnp.float32)
        mw = mw.at[0].set(0.0)
        return {'input_data': x, 'W1': W1, 'W2': W2, 'bias': bias, 'memory_weights': mw}
    _L1_attn_all = _L1_attn_setup()
    _L1_attn_in = {k: v for k, v in _L1_attn_all.items() if k in ('W1', 'W2', 'bias', 'memory_weights')}
    del _L1_attn_all

    def _L1_ffn_setup():
        import jax, jax.numpy as jnp
        import numpy as np
        BN_EPS = 0.001

        def _bn(h, g, b, m, v):
            return g * (h - m) * jax.lax.rsqrt(v + BN_EPS) + b
        key = jax.random.key(seed)
        ks = jax.random.split(key, 8)
        B, F, Df = (64, 64, 64)
        E, H, D = (8, 64, 64)
        s1 = 1.0 / np.sqrt(Df)
        s2 = 1.0 / np.sqrt(H)
        return {'x': jax.random.normal(ks[0], (B, F, Df), jnp.float32), 'Wr': jax.random.normal(ks[1], (Df, E), jnp.float32) * s1, 'br': jnp.zeros((E,), jnp.float32), 'W1': jax.random.normal(ks[2], (E, Df, H), jnp.float32) * s1, 'b1': jnp.zeros((E, H), jnp.float32), 'g1': jnp.ones((E, H), jnp.float32), 'be1': jnp.zeros((E, H), jnp.float32), 'm1': jnp.zeros((E, H), jnp.float32), 'v1': jnp.ones((E, H), jnp.float32), 'W2': jax.random.normal(ks[3], (E, H, H), jnp.float32) * s2, 'b2': jnp.zeros((E, H), jnp.float32), 'g2': jnp.ones((E, H), jnp.float32), 'be2': jnp.zeros((E, H), jnp.float32), 'm2': jnp.zeros((E, H), jnp.float32), 'v2': jnp.ones((E, H), jnp.float32), 'Wo': jax.random.normal(ks[4], (E, H, D), jnp.float32) * s2, 'bo': jnp.zeros((E, D), jnp.float32)}
    _L1_ffn_all = _L1_ffn_setup()
    _L1_ffn_in = {k: v for k, v in _L1_ffn_all.items() if k in ('Wr', 'br', 'W1', 'b1', 'g1', 'be1', 'm1', 'v1', 'W2', 'b2', 'g2', 'be2', 'm2', 'v2', 'Wo', 'bo')}
    del _L1_ffn_all
    return {'x': x, 'cls_tok': cls_tok, 'L0_tok_ln1_g': _L0_tok_in['ln1_g'], 'L0_tok_ln1_b': _L0_tok_in['ln1_b'], 'L0_tok_W1': _L0_tok_in['W1'], 'L0_tok_b1': _L0_tok_in['b1'], 'L0_tok_ln2_g': _L0_tok_in['ln2_g'], 'L0_tok_ln2_b': _L0_tok_in['ln2_b'], 'L0_tok_Wp1': _L0_tok_in['Wp1'], 'L0_tok_bp1': _L0_tok_in['bp1'], 'L0_tok_lnp_g': _L0_tok_in['lnp_g'], 'L0_tok_lnp_b': _L0_tok_in['lnp_b'], 'L0_tok_Wp2': _L0_tok_in['Wp2'], 'L0_tok_bp2': _L0_tok_in['bp2'], 'L0_attn_log_lambda_real': _L0_attn_in['log_lambda_real'], 'L0_attn_lambda_imag': _L0_attn_in['lambda_imag'], 'L0_attn_log_dt': _L0_attn_in['log_dt'], 'L0_attn_B': _L0_attn_in['B'], 'L0_attn_C_real': _L0_attn_in['C_real'], 'L0_attn_C_imag': _L0_attn_in['C_imag'], 'L0_ffn_Wq_pk': _L0_ffn_in['Wq_pk'], 'L0_ffn_pk_keys': _L0_ffn_in['pk_keys'], 'L0_ffn_Wq': _L0_ffn_in['Wq'], 'L0_ffn_keys_table': _L0_ffn_in['keys_table'], 'L0_ffn_values_table': _L0_ffn_in['values_table'], 'L0_ffn_Wo': _L0_ffn_in['Wo'], 'L1_attn_W1': _L1_attn_in['W1'], 'L1_attn_W2': _L1_attn_in['W2'], 'L1_attn_bias': _L1_attn_in['bias'], 'L1_attn_memory_weights': _L1_attn_in['memory_weights'], 'L1_ffn_Wr': _L1_ffn_in['Wr'], 'L1_ffn_br': _L1_ffn_in['br'], 'L1_ffn_W1': _L1_ffn_in['W1'], 'L1_ffn_b1': _L1_ffn_in['b1'], 'L1_ffn_g1': _L1_ffn_in['g1'], 'L1_ffn_be1': _L1_ffn_in['be1'], 'L1_ffn_m1': _L1_ffn_in['m1'], 'L1_ffn_v1': _L1_ffn_in['v1'], 'L1_ffn_W2': _L1_ffn_in['W2'], 'L1_ffn_b2': _L1_ffn_in['b2'], 'L1_ffn_g2': _L1_ffn_in['g2'], 'L1_ffn_be2': _L1_ffn_in['be2'], 'L1_ffn_m2': _L1_ffn_in['m2'], 'L1_ffn_v2': _L1_ffn_in['v2'], 'L1_ffn_Wo': _L1_ffn_in['Wo'], 'L1_ffn_bo': _L1_ffn_in['bo']}

def reference(x, cls_tok, L0_tok_ln1_g, L0_tok_ln1_b, L0_tok_W1, L0_tok_b1, L0_tok_ln2_g, L0_tok_ln2_b, L0_tok_Wp1, L0_tok_bp1, L0_tok_lnp_g, L0_tok_lnp_b, L0_tok_Wp2, L0_tok_bp2, L0_attn_log_lambda_real, L0_attn_lambda_imag, L0_attn_log_dt, L0_attn_B, L0_attn_C_real, L0_attn_C_imag, L0_ffn_Wq_pk, L0_ffn_pk_keys, L0_ffn_Wq, L0_ffn_keys_table, L0_ffn_values_table, L0_ffn_Wo, L1_attn_W1, L1_attn_W2, L1_attn_bias, L1_attn_memory_weights, L1_ffn_Wr, L1_ffn_br, L1_ffn_W1, L1_ffn_b1, L1_ffn_g1, L1_ffn_be1, L1_ffn_m1, L1_ffn_v1, L1_ffn_W2, L1_ffn_b2, L1_ffn_g2, L1_ffn_be2, L1_ffn_m2, L1_ffn_v2, L1_ffn_Wo, L1_ffn_bo):
    import jax
    import jax.numpy as jnp

    def _L0_tok_ref(x, ln1_g, ln1_b, W1, b1, ln2_g, ln2_b, Wp1, bp1, lnp_g, lnp_b, Wp2, bp2):
        import jax, jax.numpy as jnp
        import numpy as np
        EPS = 1e-05
        P = 8
        DIM = 64
        NUM_TOKENS = 64
        PATCH_DIM = 3 * P * P

        def layernorm(x, g, b):
            mu = jnp.mean(x, axis=-1, keepdims=True)
            var = jnp.mean(jnp.square(x - mu), axis=-1, keepdims=True)
            return (x - mu) * jax.lax.rsqrt(var + EPS) * g + b
        b, c, H, W = x.shape
        hp, wp = (H // P, W // P)
        patches = x.reshape(b, c, hp, P, wp, P)
        patches = jnp.transpose(patches, (0, 2, 4, 3, 5, 1))
        patches = patches.reshape(b, hp * wp, P * P * c)
        tokens = layernorm(patches, ln1_g, ln1_b)
        tokens = tokens @ W1 + b1
        tokens = layernorm(tokens, ln2_g, ln2_b)
        q = tokens
        k = tokens
        tokens = jnp.concatenate([q, k, tokens], axis=1)
        h1 = layernorm(tokens @ Wp1 + bp1, lnp_g, lnp_b)
        h1 = jax.nn.silu(h1)
        return h1 @ Wp2 + bp2

    def _L0_attn_ref(x, log_lambda_real, lambda_imag, log_dt, B, C_real, C_imag):
        import jax, jax.numpy as jnp
        import numpy as np
        import math
        batch, seq_len, _ = x.shape
        Lambda = -jnp.exp(log_lambda_real) + 1j * lambda_imag
        dt = jnp.clip(jnp.exp(log_dt), 0.005, 0.1)
        denom = 1.0 - 0.5 * dt * Lambda
        A_bar = (1.0 + 0.5 * dt * Lambda) / denom
        B_bar = (dt / denom)[:, None] * B
        u = jnp.matmul(x, B_bar.real.T) + 1j * jnp.matmul(x, B_bar.imag.T)
        A_poles = jnp.broadcast_to(A_bar[:, None], (A_bar.shape[0], seq_len))
        A_cp = jnp.cumprod(A_poles, axis=1)
        A_powers = jnp.concatenate([jnp.ones_like(A_cp[:, :1]), A_cp[:, :-1]], axis=1)
        n_fft = 2 ** math.ceil(math.log2(seq_len * 2 - 1))
        u_t = jnp.swapaxes(u, 1, 2)
        u_f = jnp.fft.fft(u_t, n=n_fft, axis=-1)
        A_f = jnp.fft.fft(A_powers, n=n_fft, axis=-1)
        h = jnp.fft.ifft(u_f * A_f[None], n=n_fft, axis=-1)[..., :seq_len]
        h = jnp.swapaxes(h, 1, 2)
        C_c = C_real + 1j * C_imag
        return jnp.matmul(h, C_c.T).real

    def _L0_ffn_ref(x, Wq_pk, pk_keys, Wq, keys_table, values_table, Wo):
        import jax, jax.numpy as jnp
        import numpy as np
        DIM = 64
        HEADS = 8
        NUM_KEYS = 64
        NUM_KV = NUM_KEYS ** 2
        PK_TOPK = 16
        FINAL_TOPK = 16
        DIM_KEY = DIM // 2
        P = 2

        def _pk(x, Wq_pk, pk_keys):
            b, n, _ = x.shape
            q = (x @ Wq_pk).reshape(b, n, P, HEADS, DIM_KEY).transpose(2, 0, 1, 3, 4)
            sim = jnp.einsum('pbnhd,pkhd->pbnhk', q, pk_keys)
            scores, idx = jax.lax.top_k(sim, PK_TOPK)
            idx0 = idx[0]
            idx1 = idx[1] * NUM_KEYS
            index = (idx0[..., :, None] + idx1[..., None, :]).reshape(b, n, HEADS, PK_TOPK * PK_TOPK)
            score = (scores[0][..., :, None] + scores[1][..., None, :]).reshape(b, n, HEADS, PK_TOPK * PK_TOPK)
            final_scores, pk_idx = jax.lax.top_k(score, FINAL_TOPK)
            final_indices = jnp.take_along_axis(index, pk_idx, axis=-1)
            final_scores = jax.nn.softmax(final_scores, axis=-1)
            return (final_scores, final_indices)
        b, n, d = x.shape
        q = (x @ Wq).reshape(b, n, HEADS, DIM) * DIM ** (-0.5)
        kv_scores, indices = _pk(x, Wq_pk, pk_keys)
        offsets = jnp.arange(HEADS, dtype=indices.dtype) * NUM_KV
        ind = indices + offsets[None, None, :, None]
        k = jnp.einsum('bnhk,bnhkd->bnhd', kv_scores, keys_table[ind])
        v = jnp.einsum('bnhk,bnhkd->bnhd', kv_scores, values_table[ind])
        sim = jnp.einsum('bihd,bjhd->bhij', q, k)
        neg = -jnp.finfo(sim.dtype).max
        causal = jnp.tril(jnp.ones((n, n), dtype=bool))
        sim = jnp.where(causal, sim, neg)
        attn = jax.nn.softmax(sim, axis=-1)
        out = jnp.einsum('bhij,bjhd->bhid', attn, v)
        out = out.transpose(0, 2, 1, 3).reshape(b, n, HEADS * DIM)
        return out @ Wo

    def _L1_attn_ref(input_data, W1, W2, bias, memory_weights):
        import jax, jax.numpy as jnp
        import numpy as np
        MEMORY_SIZE = 40
        INPUT_SIZE = 64
        OUTPUT_SIZE = 64
        BATCH = 16
        SEQ = 1024
        m = memory_weights.shape[0] - 1
        B, T, D = input_data.shape
        total = jnp.sum(input_data, axis=1, keepdims=True)
        h_hatt = jnp.zeros_like(input_data)
        win = jnp.zeros_like(input_data)
        for l in range(1, m + 1):
            shifted = jnp.pad(input_data[:, :T - l], ((0, 0), (l, 0), (0, 0)))
            h_hatt = h_hatt + memory_weights[l] * shifted
            win = win + shifted
        h_hatt = h_hatt + memory_weights[0] * (total - win)
        return input_data @ W1 + h_hatt @ W2 + bias

    def _L1_ffn_ref(x, Wr, br, W1, b1, g1, be1, m1, v1, W2, b2, g2, be2, m2, v2, Wo, bo):
        import jax, jax.numpy as jnp
        import numpy as np
        BN_EPS = 0.001

        def _bn(h, g, b, m, v):
            return g * (h - m) * jax.lax.rsqrt(v + BN_EPS) + b
        feat = jnp.mean(x, axis=0)
        w = jax.nn.softmax(feat @ Wr + br, axis=-1)
        h = jnp.einsum('bfd,edh->bfeh', x, W1) + b1
        h = jax.nn.relu(_bn(h, g1, be1, m1, v1))
        h = jnp.einsum('bfeh,ehk->bfek', h, W2) + b2
        h = jax.nn.relu(_bn(h, g2, be2, m2, v2))
        y = jnp.einsum('bfeh,ehd->bfed', h, Wo) + bo
        return jnp.einsum('bfed,fe->bfd', y, w)
    h = _L0_tok_ref(x, L0_tok_ln1_g, L0_tok_ln1_b, L0_tok_W1, L0_tok_b1, L0_tok_ln2_g, L0_tok_ln2_b, L0_tok_Wp1, L0_tok_bp1, L0_tok_lnp_g, L0_tok_lnp_b, L0_tok_Wp2, L0_tok_bp2)
    h = jnp.concatenate([jnp.broadcast_to(cls_tok, (h.shape[0], 1, h.shape[2])), h], axis=1)
    h = h + _L0_attn_ref(_layernorm(h, axis=-1), L0_attn_log_lambda_real, L0_attn_lambda_imag, L0_attn_log_dt, L0_attn_B, L0_attn_C_real, L0_attn_C_imag)
    h = h + _L0_ffn_ref(_layernorm(h, axis=-1), L0_ffn_Wq_pk, L0_ffn_pk_keys, L0_ffn_Wq, L0_ffn_keys_table, L0_ffn_values_table, L0_ffn_Wo)
    h = h + _L1_attn_ref(_layernorm(h, axis=-1), L1_attn_W1, L1_attn_W2, L1_attn_bias, L1_attn_memory_weights)
    h = h + _L1_ffn_ref(_layernorm(h, axis=-1), L1_ffn_Wr, L1_ffn_br, L1_ffn_W1, L1_ffn_b1, L1_ffn_g1, L1_ffn_be1, L1_ffn_m1, L1_ffn_v1, L1_ffn_W2, L1_ffn_b2, L1_ffn_g2, L1_ffn_be2, L1_ffn_m2, L1_ffn_v2, L1_ffn_Wo, L1_ffn_bo)
    return h

_drawn_inputs = setup_inputs


def setup_inputs(seed=0):
    import zlib

    import numpy as np

    out = dict(_drawn_inputs(seed))
    spreads = {'L0_tok_ln1_g': (1.0, 0.2),
     'L0_tok_ln1_b': (0.0, 0.1),
     'L0_tok_b1': (0.0, 0.1),
     'L0_tok_ln2_g': (1.0, 0.2),
     'L0_tok_ln2_b': (0.0, 0.1),
     'L0_tok_bp1': (0.0, 0.1),
     'L0_tok_lnp_g': (1.0, 0.2),
     'L0_tok_lnp_b': (0.0, 0.1),
     'L0_tok_bp2': (0.0, 0.1),
     'L1_attn_bias': (1.0, 0.2),
     'L1_ffn_br': (0.0, 0.8),
     'L1_ffn_b1': (0.0, 0.549),
     'L1_ffn_g1': (1.0, 0.562),
     'L1_ffn_be1': (0.0, 0.521),
     'L1_ffn_m1': (0.0, 0.646),
     'L1_ffn_v1': (1.0, 0.6),
     'L1_ffn_b2': (0.0, 0.29),
     'L1_ffn_g2': (1.0, 0.551),
     'L1_ffn_be2': (0.0, 0.308),
     'L1_ffn_m2': (0.0, 0.33),
     'L1_ffn_v2': (1.0, 0.6),
     'L1_ffn_bo': (0.0, 0.29)}
    factors = {'L0_ffn_Wq_pk': 8.0,
     'L0_ffn_pk_keys': 8.0,
     'L0_ffn_Wq': 64.0,
     'L0_ffn_keys_table': 64.0,
     'L0_ffn_values_table': 8.0,
     'L0_ffn_Wo': 8.0}
    for name, (base, spread) in spreads.items():
        noise = np.random.default_rng([zlib.crc32(name.encode()), seed]).standard_normal(out[name].shape)
        drawn = base * np.exp(spread * noise) if base else spread * noise
        out[name] = jnp.asarray(drawn.astype(out[name].dtype))
    for name, factor in factors.items():
        out[name] = (out[name] * factor).astype(out[name].dtype)
    return out
```

```python
from collections import namedtuple
from contextlib import ExitStack

import concourse.bass as bass
from concourse import mybir

ALU = mybir.AluOpType
ACT = mybir.ActivationFunctionType
AX = mybir.AxisListType.X
F32 = mybir.dt.float32
BF16 = mybir.dt.bfloat16

NB = 4
D = 64
SEG = 64
REP = 3
T = 1 + REP * SEG
TOK = NB * SEG
FLAT = NB * (T - 1) + 1
CLS = FLAT - 1
TIMED = NB * T
HALF_F = [(0, 2 * (T - 1)), (2 * (T - 1), FLAT)]
HALF_T = [(0, 2 * T), (2 * T, TIMED)]
PATCH = 192
PC = PATCH // 2
EPS = 1e-5
TOP_LINKS = 13
BN_EPS = 1e-3

H = 8
NK = 64
TOPK = 16
DK = 32
GUARD = 60.0
SLACK = float(2 ** -22)
NEG = -3.0e38
STAIR = [TOPK // (a + 1) for a in range(TOPK)]
NCAND = sum(STAIR)
WIDE = FLAT + FLAT % 2
WH = WIDE // 2
TILE = 128
NTILE = (FLAT - 1) // TILE
JH = 32
CH = 16
GRP = 4

NTG = 2 * CH // GRP
ND, NE, NW = 4, 2, 4

TAPS = 40
PAIRS = (TAPS + 2) // 2
E_ = 8
EP = E_ // 2

C64 = dict(tok_b1=0, ln2_g=1, ln2_b=2, bp1=3, lnp_g=4, lnp_b=5, bp2=6, cls=7, l1_bias=8, m0=9,
           Wp1=10, Wp2=74, BT2=138, W1=266, W2=330, Wr=394, end=402)
C128 = dict(lr=0, li=1, ldt=2, CriT=3, CirT=67, end=131)
CC = dict(ident=0, m0=TILE, m1=2 * TILE, end=2 * TILE + T)
MOE_P = 10
SEMS = """
in_x in_tokp in_p64 in_p128 in_const in_sel in_keys in_wqo in_moe in_moe_w in_fir
ones_ready pool_chain dve_chain top_chain
tok_mean tok_xc tok_sq tok_var tok_std tok_xn tok_z tok_zb tok_h tok_hb silu_e silu_out tok_o tok_ready cls_ready
ssm_exp ssm_n2 ssm_rn ssm_r2 ssm_r ssm_r0 ssm_rinv ssm_ri2 ssm_phase ssm_wc ssm_bx ssm_g ssm_q ssm_q2 ssm_y res_flat
pk_m pk_mc identb_ready sel_ready xst_ready sim_done sims_ready cut_e cut_es s0p_ready zinv_ready
s1h s1r s1m s1p_ready s0q_ready settled tr0_done tr0_read trz_done trz_read tr1_done tr1_read even_ready
b_ready d_ready e_ready w_ready w_used acc_read
tab0 tab1 tab2 tab3 tab4 tab5 tab6 tab7
timed_ready wst_ready kvh_ready q_done q_ready qk_done sc_ready nm_ready p_exp rec_ready p_ready pt_done pt_ready
vw_done vw_ready pv_done res_att
fir_w fir_pad fir_in fir_tot fir_tb fir_tbs fir_done res_fir
bn_sd bn_rec bn_ready
moe_feat moe_log moe_nm moe_le moe_gate moe_gt moe_gts moe_gb moe_gbs moe_h1 moe_a1 moe_h2 moe_a2 moe_w2g moe_y out_ready
out_done
""".split()


Semaphores = namedtuple("Semaphores", SEMS)
LN_SEMS = ("mean", "xc", "sq", "var", "std", "out")
LnSemaphores = namedtuple("LnSemaphores", LN_SEMS)


def tower(nc, xT, tokp, p64, p128, const, sel, pkw, table, wqo, fir, moe, moe_w, out):
    with ExitStack() as ctx:
        def sb(name, shape, dt=F32):
            return ctx.enter_context(nc.sbuf_tensor(name, shape, dt))

        ps = ctx.enter_context(nc.psum_tensor("ps", [128, 8, 512], F32))
        s = Semaphores(*[ctx.enter_context(nc.semaphore(n)) for n in SEMS])
        LN_BASE = dict(ln2=0, lnp=1, lns=2, lnf=3, lna=5, lnm=7)
        ln = LnSemaphores(*[ctx.enter_context(nc.semaphore("ln_" + n)) for n in LN_SEMS])

        kv = sb("kv", [128, H, WIDE])
        zbc = sb("zbc", [128, H, WIDE])
        rings = sb("rings", [128, (ND + NE + NW) * WIDE])
        taken = {}

        def part(region, shape, dt=F32, stage=0):
            flat = region.rearrange("p a b -> p (a b)") if region.ndim == 3 else region
            flat = flat if region.dtype == F32 else flat.bitcast(F32)
            n = 1
            for x in shape[1:]:
                n *= x
            words = n if dt == F32 else n // 2
            at = taken.get((region.name, stage), 0)
            taken[region.name, stage] = at + words
            assert at + words <= flat.shape[1]
            v = flat[0:shape[0], at:at + words]
            v = v if dt == F32 else v.bitcast(dt)
            names = "abcde"[:len(shape) - 1]
            if len(names) > 1:
                v = v.rearrange(f"p ({' '.join(names)}) -> p {' '.join(names)}",
                                **dict(zip(names[1:], shape[2:])))
            return v

        x_sb = part(zbc[:], [PC, 2, TOK])
        tokp_sb = sb("tokp_sb", [PC, 4 + 2 * D])
        p64_sb = sb("p64_sb", [D, C64["end"]])
        p128_sb = sb("p128_sb", [128, C128["end"]])
        const_sb = sb("const_sb", [128, CC["end"]])
        sel_sb = sb("sel_sb", [3 * JH, CH, 128], BF16)
        pkw_sb = part(zbc[:], [128, 2, 4, 64])
        fir_sb = sb("fir_sb", [128, PAIRS + 1 + 2 * D])
        moe_sb = sb("moe_sb", [128, 4, MOE_P])
        onesp = sb("onesp", [PC, PC])
        ones64 = sb("ones64", [D, D])
        four = sb("four", [1, 128])
        bn = sb("bn", [128, 4, EP, 2])
        eps_sb = sb("eps_sb", [128, 2])

        def col(name, n=1):
            return p64_sb[:, C64[name]:C64[name] + n]

        def par(name, n=1):
            return p128_sb[:, C128[name]:C128[name] + n]

        ident = const_sb[:, CC["ident"]:CC["ident"] + 128]
        mask0 = const_sb[:, CC["m0"]:CC["m0"] + TILE]
        mask1 = const_sb[0:T - TILE, CC["m1"]:CC["m1"] + T]

        tk = part(kv[:], [PC, 4, 2, TOK])
        u_sb = part(zbc[:], [D, TOK + 1])
        lnw = part(zbc[:], [D, 3, TIMED])
        tz = part(kv[:], [D, 6, TOK])
        sp_ = sb("sp_", [128, 32])
        ph = sb("ph", [128, 2, T])
        pht = part(zbc[:], [128, 2, SEG * 2])
        pin = part(zbc[:], [128, T])
        pin2 = part(zbc[:], [128, T])
        wcs = sb("wcs", [128, 2, D])
        vq = part(kv[:], [128, 2, FLAT + 3])
        g_sb = part(kv[:], [128, NB, T])
        res = sb("res", [D, FLAT])
        x1 = part(zbc[:], [D, TOK + 1])
        x2 = sb("x2", [D, FLAT])

        m_sb = sb("m_sb", [D, 2 * H * NK])
        identb = sb("identb", [128, 128], BF16)
        xst = sb("xst", [D, 2, TILE])
        sim = part(rings[:], [128, 2, 2 * H, NK])
        rest_sims = part(kv[:], [128, 2 * H, NK], stage=1)
        top = part(rings[:], [128, 2 * H, TOPK])
        cand = part(kv[:], [128, 2, H, NCAND], stage=1)
        best = sb("best", [128, H, TOPK])
        cut = sb("cut", [128, 3, H])
        ez = sb("ez", [128, 2, H, TOPK])
        zinv = sb("zinv", [128, 2, H])
        s0p = part(rings[:], [128, 2, H, 2, NK])
        s1p = part(rings[:], [128, 2, 2 * H, 3, JH], BF16)
        s1r = part(rings[:], [128, 2 * H, JH])
        s0t = sb("s0t", [128, H, WIDE])
        s1t_all = sb("s1t", [128, 2 * H, WIDE], BF16)
        s1t = s1t_all[0:3 * JH]
        tab_sb = sb("tab_sb", [128, NTG, GRP, 128])
        ring = rings[:].rearrange("p (a n) -> p a n", n=WIDE)
        d_sb, e_sb, w_sb = ring[:, 0:ND], ring[:, ND:ND + NE], ring[:, ND + NE:ND + NE + NW]
        tab_in = [s.tab0, s.tab1, s.tab2, s.tab3, s.tab4, s.tab5, s.tab6, s.tab7]
        x2t = sb("x2t", [D, TIMED])
        rest = sb("rest", [D, TIMED])
        wqo_sb = sb("wqo_sb", [128, H, D])
        wst = sb("wst", [128, D])
        kvh = sb("kvh", [128, NB, T])
        q_sb = sb("q_sb", [D, NB, T])
        a0 = sb("a0", [TILE, NB, TILE])
        a1 = sb("a1", [T - TILE, NB, T])
        amax = sb("amax", [TILE, 2, NB])
        asum = sb("asum", [TILE, 2, NB])
        arec = sb("arec", [TILE, 2, NB])
        pt0 = sb("pt0", [TILE, NB, TILE])
        pt1 = sb("pt1", [TILE, NB, T - TILE])
        pt2 = sb("pt2", [T - TILE, NB, T - TILE])
        vw0 = sb("vw0", [TILE, NB, D])
        vw1 = sb("vw1", [T - TILE, NB, D])

        def settle(eng):
            eng.sem_inc(s.settled, 1)

        sel_in = part(rings[:], [3 * JH, CH, 128], stage=1)

        moew = part(s0t[:], [128, 5, E_ * D])
        xpad = part(s0t[:], [128, NB, TAPS + T])
        firw = part(s0t[:], [128, PAIRS, D])
        firm = part(s0t[:], [128, PAIRS])
        xl = part(s1t_all[:], [D, TIMED])
        h1 = part(s1t_all[:], [128, 2, NB, T])
        h2 = part(s1t_all[:], [128, 2, NB, T])
        gb = part(s1t_all[:], [128, EP, T])
        tot = sb("tot", [D, 3, NB])
        feat = sb("feat", [D, T])
        lg = sb("lg", [TILE, 3, 2, E_])
        lsum = sb("lsum", [TILE, 3, 2])
        gt = sb("gt", [E_, T])
        w1m, w2m, wom = moew[0:D, 0], moew[:, 1].rearrange("p (a k) -> p a k", a=EP), moew[:, 2].rearrange("p (a k) -> p a k", a=EP)
        bom, brm, e8m = moew[0:E_, 3, 0:D], moew[0:1, 3, D:D + E_], moew[0:E_, 4].rearrange("p (a k) -> p a k", a=EP)

        pe = act = dve = None
        nlink = [0]

        def link(ins):
            nlink[0] += 1
            ins.then_inc(s.dve_chain, 1)
            dve.wait_ge(s.dve_chain, nlink[0])

        def ln_pe(k, src, ready, need, parts, banks):
            for i, (a, b) in enumerate(parts):
                pe.wait_ge(ready, need[i])
                nc.tensor.matmul(ps[0:D, banks[0] + i, 0:b - a], ones64[:], src[:, a:b],
                                 start=True, stop=True).then_inc(ln.mean, 1)
            for i, (a, b) in enumerate(parts):
                pe.wait_ge(ln.sq, LN_BASE[k] + i + 1)
                nc.tensor.matmul(ps[0:D, banks[1] + i, 0:b - a], ones64[:], lnw[:, 1, a:b],
                                 start=True, stop=True).then_inc(ln.var, 1)

        def ln_act(k, parts, banks):
            for i, (a, b) in enumerate(parts):
                act.wait_ge(ln.xc, LN_BASE[k] + i + 1)
                nc.scalar.activation(lnw[:, 1, a:b], lnw[:, 0, a:b], ACT.Square).then_inc(ln.sq, 1)
            for i, (a, b) in enumerate(parts):
                act.wait_ge(ln.var, LN_BASE[k] + i + 1)
                nc.scalar.activation(lnw[:, 2, a:b], ps[0:D, banks[1] + i, 0:b - a], ACT.Sqrt,
                                     bias=eps_sb[0:D, 0:1]).then_inc(ln.std, 1)

        def ln_dve(k, src, dst, parts, banks, affine=None):
            for i, (a, b) in enumerate(parts):
                dve.wait_ge(ln.mean, LN_BASE[k] + i + 1)
                nc.vector.tensor_tensor(lnw[:, 0, a:b], src[:, a:b], ps[0:D, banks[0] + i, 0:b - a],
                                        ALU.subtract).then_inc(ln.xc, 1)
            for i, (a, b) in enumerate(parts):
                dve.wait_ge(ln.std, LN_BASE[k] + i + 1)
                link(nc.vector.reciprocal(lnw[:, 2, a:b], lnw[:, 2, a:b]))
                last = nc.vector.tensor_tensor(dst[:, a:b], lnw[:, 0, a:b], lnw[:, 2, a:b], ALU.mult)
                if affine:
                    link(last)
                    last = nc.vector.tensor_scalar(dst[:, a:b], dst[:, a:b], affine[0], affine[1],
                                                   ALU.mult, ALU.add)
                last.then_inc(ln.out, 1)

        block = ctx.enter_context(nc.Block())

        @block.sync
        def _(sp):
            for dst, src, done in (
                (x_sb[:], xT, s.in_x), (tokp_sb[:], tokp, s.in_tokp), (p64_sb[:], p64, s.in_p64),
                (p128_sb[:], p128, s.in_p128), (const_sb[:], const, s.in_const), (pkw_sb[:], pkw, s.in_keys),
                (sel_in, sel, s.in_sel), (wqo_sb[:], wqo, s.in_wqo),
                (moe_sb[:], moe, s.in_moe), (fir_sb[:], fir, s.in_fir),
            ):
                sp.dma_start(dst, src).then_inc(done, 16)
            for g in range(NTG):
                sp.dma_start(tab_sb[:, g], table[g]).then_inc(tab_in[g], 16)
            with sp.Fori(0, H - 1) as h:
                for g in range(NTG):
                    sp.wait_ge(s.w_used, NW + h * 2 * CH + (g + 1) * GRP)
                    sp.dma_start(tab_sb[:, g], table[bass.ds((h + 1) * NTG + g, 1)]
                                 .rearrange("o p c k -> (o p) c k")).then_inc(tab_in[g], 16)
            sp.wait_ge(s.w_used, NW + H * 2 * CH)
            sp.dma_start(moew, moe_w).then_inc(s.in_moe_w, 16)
            for a, (lo, hi) in enumerate(HALF_T):
                sp.wait_ge(s.out_ready, a + 1)
                sp.dma_start(out[:, lo:hi], rest[:, lo:hi]).then_inc(s.out_done, 16)
            sp.wait_ge(s.out_done, 32)

        @block.gpsimd
        def _(pool):
            n = [0]

            def pl(ins):
                n[0] += 1
                ins.then_inc(s.pool_chain, 1)
                pool.wait_ge(s.pool_chain, n[0])

            nc.gpsimd.memset(onesp[:], 1.0 / PATCH)
            nc.gpsimd.memset(ones64[:], 1.0 / D)
            nc.gpsimd.memset(four[:], float(NB))
            nc.gpsimd.memset(eps_sb[:, 1:2], BN_EPS)
            nc.gpsimd.memset(eps_sb[:, 0:1], EPS).then_inc(s.ones_ready, 1)

            EL, DT, AR, AI, OM, AI2, AR2, N2, RN, T1, ARE, AIM, R2, R, RI, C1, S1, BRE, BIM, P2 = range(20)

            def c(k):
                return sp_[:, k:k + 1]

            tt, ts, stt = nc.gpsimd.tensor_tensor, nc.gpsimd.tensor_scalar, nc.gpsimd.scalar_tensor_tensor
            pool.wait_ge(s.in_p128, 16)
            pool.wait_ge(s.ssm_exp, 2)
            pl(ts(c(DT), c(DT), 0.005, 0.1, ALU.max, ALU.min))
            pl(tt(c(AR), c(DT), c(EL), ALU.mult))
            pl(ts(c(AR), c(AR), -0.5, None, ALU.mult))
            pl(tt(c(AI), c(DT), par("li"), ALU.mult))
            pl(ts(c(AI), c(AI), 0.5, None, ALU.mult))
            pl(ts(c(OM), c(AR), -1.0, 1.0, ALU.mult, ALU.add))
            pl(tt(c(AI2), c(AI), c(AI), ALU.mult))
            pl(tt(c(AR2), c(AR), c(AR), ALU.mult))
            pl(tt(c(N2), c(OM), c(OM), ALU.mult))
            tt(c(N2), c(N2), c(AI2), ALU.add).then_inc(s.ssm_n2, 1)
            pl(tt(c(T1), c(AR2), c(AI2), ALU.add))
            pl(ts(c(T1), c(T1), -1.0, 1.0, ALU.mult, ALU.add))
            pl(tt(c(BRE), c(DT), c(OM), ALU.mult))
            pl(tt(c(BIM), c(DT), c(AI), ALU.mult))
            pool.wait_ge(s.ssm_rn, 1)
            pl(tt(c(ARE), c(T1), c(RN), ALU.mult))
            pl(tt(c(AIM), c(AI), c(RN), ALU.mult))
            pl(ts(c(AIM), c(AIM), 2.0, None, ALU.mult))
            pl(tt(c(BRE), c(BRE), c(RN), ALU.mult))
            pl(tt(c(BIM), c(BIM), c(RN), ALU.mult))
            pl(tt(c(R2), c(ARE), c(ARE), ALU.mult))
            pl(tt(c(T1), c(AIM), c(AIM), ALU.mult))
            tt(c(R2), c(R2), c(T1), ALU.add).then_inc(s.ssm_r2, 1)
            pool.wait_ge(s.ssm_rinv, 1)
            pl(tt(c(T1), c(R2), c(RI), ALU.mult))
            pl(tt(c(R), c(R), c(T1), ALU.add))
            ts(c(R), c(R), 0.5, None, ALU.mult).then_inc(s.ssm_r, 1)
            pool.wait_ge(s.ssm_ri2, 1)
            pl(nc.gpsimd.memset(ph[:, 0, 0:1], 1.0))
            pl(nc.gpsimd.memset(ph[:, 1, 0:1], 0.0))
            pl(tt(ph[:, 0, 1:2], c(ARE), c(RI), ALU.mult))
            pl(tt(ph[:, 1, 1:2], c(AIM), c(RI), ALU.mult))
            m = 1
            while m < T - 1:
                w = min(m, T - 1 - m)
                cm, sm = ph[:, 0, m:m + 1], ph[:, 1, m:m + 1]
                cs, ss = ph[:, 0, 1:1 + w], ph[:, 1, 1:1 + w]
                ts(pht[:, 0, 0:w], ss, sm, None, ALU.mult)
                pl(ts(pht[:, 1, 0:w], ss, cm, None, ALU.mult))
                ts(ph[:, 0, m + 1:m + 1 + w], cs, cm, None, ALU.mult)
                pl(ts(ph[:, 1, m + 1:m + 1 + w], cs, sm, None, ALU.mult))
                tt(ph[:, 0, m + 1:m + 1 + w], ph[:, 0, m + 1:m + 1 + w], pht[:, 0, 0:w], ALU.subtract)
                pl(tt(ph[:, 1, m + 1:m + 1 + w], ph[:, 1, m + 1:m + 1 + w], pht[:, 1, 0:w], ALU.add))
                m += w
            for lo, a, b, neg in ((0, BRE, BIM, False), (D, BIM, BRE, True)):
                q = slice(lo, lo + D)
                pl(ts(pin[q, :], ph[q, 0, :], sp_[q, a:a + 1], None, ALU.mult))
                pl(ts(pin2[q, :], ph[q, 1, :], sp_[q, b:b + 1], None, ALU.mult))
                last = tt(pin[q, :], pin[q, :], pin2[q, :], ALU.subtract if neg else ALU.add)
                pl(last) if lo == 0 else last.then_inc(s.ssm_phase, 1)
            pool.wait_ge(s.ssm_phase, 1)
            pl(ts(wcs[0:D, 0, :], p128_sb[0:D, C128["CriT"]:C128["CriT"] + D], 1.0, None, ALU.mult))
            pl(ts(wcs[D:128, 0, :], p128_sb[D:128, C128["CriT"]:C128["CriT"] + D], -1.0, None, ALU.mult))
            ts(wcs[:, 1, :], par("CirT", D), -1.0, None, ALU.mult).then_inc(s.ssm_wc, 1)
            pool.wait_ge(s.ssm_g, NB)
            nc.gpsimd.memset(vq[:, 1, CLS:CLS + 1], 0.0)
            tt(vq[:, 1, 0:CLS].rearrange("p (b t) -> p b t", b=NB), g_sb[:, :, 1:T],
               ph[:, 1, 1:T].unsqueeze(1).broadcast_to([128, NB, T - 1]), ALU.mult).then_inc(s.ssm_q2, 1)
            nc.gpsimd.memset(s0t[:, :, FLAT:WIDE], -1.0)
            nc.gpsimd.memset(s1t[:, :, FLAT:WIDE], 0.0).then_inc(s.even_ready, 1)

            def pieces(u, n, rows):
                pool.wait_ge(s.s1h, n + 1)
                pool.wait_ge(s.s1p_ready, n + 1)
                tt(s1r[0:rows], sim[0:rows, u, H:2 * H].rearrange("p h (j k) -> p (h j) k", j=2),
                   s1p[0:rows, u, :, 0], ALU.subtract).then_inc(s.s1r, 1)
                pool.wait_ge(s.s1m, n + 1)
                tt(s1p[0:rows, u, :, 2], s1r[0:rows], s1p[0:rows, u, :, 1], ALU.subtract).then_inc(s.s1p_ready, 1)
                pool.wait_ge(s.s0p_ready, n + 1)
                tt(s0p[0:rows, u, :, 1], sim[0:rows, u, 0:H], cut[0:rows, 2].unsqueeze(2).broadcast_to([rows, H, NK]),
                   ALU.subtract).then_inc(s.s0q_ready, 1)

            pool.sem_inc(s.s1p_ready, 1)
            with pool.Fori(0, NTILE // 2) as i:
                for u in range(2):
                    pieces(u, 2 * i + u, TILE)
            pieces(0, NTILE, 1)
            pool.wait_ge(s.bn_rec, 1)
            prm = moe_sb[:].rearrange("p a (l k) -> p a l k", l=2)
            pl(tt(bn[:, 0], prm[:, :, :, 1], bn[:, 0], ALU.mult))
            pl(tt(bn[:, 2], prm[:, :, :, 0], prm[:, :, :, 3], ALU.subtract))
            pl(tt(bn[:, 2], bn[:, 2], bn[:, 0], ALU.mult))
            tt(bn[:, 1], bn[:, 2], prm[:, :, :, 2], ALU.add).then_inc(s.bn_ready, 1)
            pool.wait_ge(s.in_fir, 16)
            pool.wait_ge(s.w_used, NW + H * 2 * CH)
            nc.gpsimd.memset(xpad[:, :, 0:TAPS + 1], 0.0)
            pl(ts(firm, fir_sb[:, 0:PAIRS], fir_sb[:, PAIRS:PAIRS + 1], None, ALU.subtract))
            pl(tt(firw, firm.unsqueeze(2).broadcast_to([128, PAIRS, D]),
                  fir_sb[:, PAIRS + 1:PAIRS + 1 + D].unsqueeze(1).broadcast_to([128, PAIRS, D]), ALU.mult))
            pl(nc.gpsimd.memset(firw[D:128, PAIRS - 1], 0.0))
            nc.gpsimd.tensor_copy(firw[0:D, 0], fir_sb[0:D, PAIRS + 1 + D:PAIRS + 1 + 2 * D]).then_inc(s.fir_w, 1)

        @block.scalar
        def _(act_):
            nonlocal act
            act = act_
            act.wait_ge(s.ones_ready, 1)
            act.wait_ge(s.tok_xc, 1)
            nc.scalar.activation(tk[:, 1], tk[:, 0], ACT.Square).then_inc(s.tok_sq, 1)
            act.wait_ge(s.in_p128, 16)
            nc.scalar.activation(sp_[:, 0:1], par("lr"), ACT.Exp).then_inc(s.ssm_exp, 1)
            nc.scalar.activation(sp_[:, 1:2], par("ldt"), ACT.Exp).then_inc(s.ssm_exp, 1)
            act.wait_ge(s.tok_var, 1)
            nc.scalar.activation(tk[:, 2, 0], ps[0:PC, 1, 0:TOK], ACT.Sqrt, bias=eps_sb[0:PC, 0:1]).then_inc(s.tok_std, 1)
            act.wait_ge(s.in_p64, 16)
            act.wait_ge(s.tok_z, 1)
            nc.scalar.activation(tz[:, 0], ps[0:D, 2, 0:TOK], ACT.Identity, bias=col("tok_b1")).then_inc(s.tok_zb, 1)
            nc.scalar.copy(u_sb[:, TOK:TOK + 1], col("cls")).then_inc(s.cls_ready, 1)
            act.wait_ge(s.ssm_r2, 1)
            nc.scalar.activation(sp_[:, 13:14], sp_[:, 12:13], ACT.Sqrt).then_inc(s.ssm_r0, 1)
            ln_act("ln2", [(0, TOK)], (3, 4))
            act.wait_ge(s.tok_h, 1)
            nc.scalar.activation(tz[:, 2], ps[0:D, 5, 0:TOK], ACT.Identity, bias=col("bp1")).then_inc(s.tok_hb, 1)
            ln_act("lnp", [(0, TOK)], (6, 7))
            act.wait_ge(ln.out, LN_BASE["lnp"] + 1)
            nc.scalar.activation(tz[:, 4], tz[:, 3], ACT.Exp, scale=-1.0).then_inc(s.silu_e, 1)
            act.wait_ge(s.tok_o, 1)
            nc.scalar.activation(u_sb[:, 0:TOK], ps[0:D, 0, 0:TOK], ACT.Identity, bias=col("bp2")).then_inc(s.tok_ready, 1)
            ln_act("lns", [(0, TOK + 1)], (1, 2))
            act.wait_ge(s.in_sel, 16)
            nc.scalar.copy(sel_sb[:], sel_in).then_inc(s.sel_ready, 1)
            act.wait_ge(s.in_moe, 16)
            nc.scalar.activation(bn[:, 3], moe_sb[:].rearrange("p a (l k) -> p a l k", l=2)[:, :, :, 4], ACT.Sqrt,
                                 bias=eps_sb[:, 1:2]).then_inc(s.bn_sd, 1)
            act.wait_ge(s.in_const, 16)
            nc.scalar.copy(identb[:], ident).then_inc(s.identb_ready, 1)
            mv = m_sb[:].rearrange("p (g q k) -> p g q k", g=4, q=4)
            for q in range(4):
                act.wait_ge(s.pk_m, q + 1)
                nc.scalar.copy(mv[:, :, q], ps[0:D, 4 * (q % 2) + q // 2, 0:4 * NK].rearrange("p (g k) -> p g k", g=4)
                               ).then_inc(s.pk_mc, 1)

            ln_act("lnf", HALF_F, (3, 5))

            def stage_tile(u, lo, rows):
                nc.scalar.copy(xst[:, u, 0:rows], x2[:, lo]).then_inc(s.xst_ready, 1)

            def scores_out(u, n, rows):
                act.wait_ge(s.sim_done, n + 1)
                for k in range(2):
                    nc.scalar.copy(sim[0:rows, u, 8 * k:8 * k + 8], ps[0:rows, k, :].rearrange("p (h k) -> p h k", k=NK)
                                   ).then_inc(s.sims_ready, 1)
                act.wait_ge(s.sims_ready, 2 * n + 2)
                nc.scalar.copy(s1p[0:rows, u, :, 0], sim[0:rows, u, H:2 * H].rearrange("p h (j k) -> p (h j) k", j=2)
                               ).then_inc(s.s1h, 1)
                act.wait_ge(s.s1r, n + 1)
                nc.scalar.copy(s1p[0:rows, u, :, 1], s1r[0:rows]).then_inc(s.s1m, 1)

            def turned_out(n, lo, rows):
                act.wait_ge(s.cut_e, n + 1)
                nc.scalar.activation(ez[0:rows, 1], ez[0:rows, 0], ACT.Exp).then_inc(s.cut_es, 1)
                act.wait_ge(s.tr0_done, n + 1)
                nc.scalar.copy(s0t[:, :, lo], ps[:, 2:4, :].rearrange("p a (h k) -> p (a h) k", h=4)[:, :, 0:rows]
                               ).then_inc(s.tr0_read, 1)
                act.wait_ge(s.tr1_done, n + 1)
                nc.scalar.copy(s1t[:, :, lo], ps[0:3 * JH, 6:8, :].bitcast(BF16).rearrange("p a (h k) -> p (a h) k", h=8)[:, :, 0:rows]
                               ).then_inc(s.tr1_read, 1)
                act.wait_ge(s.trz_done, n + 1)
                nc.scalar.copy(zbc[:, :, lo], ps[:, 4:6, :].rearrange("p a (h k) -> p (a h) k", h=4)[:, :, 0:rows]
                               ).then_inc(s.trz_read, 1)

            act.wait_ge(ln.out, LN_BASE["lnf"] + 2)
            stage_tile(0, slice(0, TILE), TILE)
            scores_out(0, 0, TILE)
            with act.Fori(0, NTILE // 2 - 1) as i:
                for u in range(2):
                    n = 2 * i + u
                    stage_tile(1 - u, bass.ds((n + 1) * TILE, TILE), TILE)
                    scores_out(1 - u, n + 1, TILE)
                    turned_out(n, bass.ds(n * TILE, TILE), TILE)
            n = NTILE - 2
            stage_tile(1, slice(n * TILE + TILE, CLS), TILE)
            scores_out(1, n + 1, TILE)
            turned_out(n, slice(n * TILE, n * TILE + TILE), TILE)
            stage_tile(0, slice(CLS, FLAT), 1)
            scores_out(0, NTILE, 1)
            turned_out(n + 1, slice(n * TILE + TILE, CLS), TILE)
            turned_out(NTILE, slice(CLS, FLAT), 1)

            with act.Fori(0, H) as h:
                for c in range(2 * CH):
                    act.wait_ge(s.d_ready, h * 2 * CH + c + 1)
                    nc.scalar.activation(e_sb[:, c % NE], d_sb[:, c % ND], ACT.Exp).then_inc(s.e_ready, 1)
                act.wait_ge(s.w_used, NW + (h + 1) * 2 * CH)
                nc.scalar.copy(kv[:, bass.ds(h, 1), :].rearrange("p o (a n) -> p (o a) n", a=2),
                               ps[:, 4:6, 0:WH]).then_inc(s.acc_read, 1)

            act.wait_ge(s.in_wqo, 16)
            act.sem_inc(s.vw_done, 1)
            with act.Fori(0, H) as h:
                act.wait_ge(s.vw_done, h + 1)
                nc.scalar.copy(wst[:].unsqueeze(1), wqo_sb[:, bass.ds(h, 1), :]).then_inc(s.wst_ready, 1)
                act.wait_ge(s.q_done, h + 1)
                nc.scalar.mul(q_sb[:].rearrange("p b t -> p (b t)").rearrange("p (a n) -> p a n", a=2),
                              ps[0:D, 0:2, 0:2 * T], float(D) ** -0.5).then_inc(s.q_ready, 1)
                act.wait_ge(s.nm_ready, h + 1)
                for b in range(NB):
                    nc.scalar.activation(a0[:, b], a0[:, b], ACT.Exp, bias=amax[:, 0, b:b + 1],
                                         accum_out=asum[:, 0, b:b + 1])
                    last = nc.scalar.activation(a1[:, b], a1[:, b], ACT.Exp, bias=amax[0:T - TILE, 1, b:b + 1],
                                                accum_out=asum[0:T - TILE, 1, b:b + 1])
                last.then_inc(s.p_exp, 1)
                act.wait_ge(s.pt_done, h + 1)
                nc.scalar.copy(pt0[:], ps[:, 5, :].rearrange("p (b i) -> p b i", b=NB))
                nc.scalar.copy(pt1[:], ps[:, 6, 0:NB * (T - TILE)].rearrange("p (b i) -> p b i", b=NB))
                nc.scalar.copy(pt2[:], ps[0:T - TILE, 7, 0:NB * (T - TILE)].rearrange("p (b i) -> p b i", b=NB)
                               ).then_inc(s.pt_ready, 1)

            ln_act("lna", HALF_T, (2, 4))
            act.wait_ge(s.fir_w, 1)
            for a in range(2):
                act.wait_ge(ln.out, LN_BASE["lna"] + a + 1)
                nc.scalar.copy(xpad[0:D, 2 * a:2 * a + 2, TAPS:TAPS + T],
                               xl[:, 2 * a * T:(2 * a + 2) * T].rearrange("p (b t) -> p b t", b=2)).then_inc(s.fir_in, 1)
            act.wait_ge(s.fir_tb, 1)
            nc.scalar.activation(tot[:, 2], ps[0:D, 6, 0:NB], ACT.Identity, bias=col("l1_bias")).then_inc(s.fir_tbs, 1)

            ln_act("lnm", HALF_T, (2, 4))
            act.wait_ge(s.moe_nm, 1)
            for f, rows in ((0, TILE), (1, T - TILE)):
                last = nc.scalar.activation(lg[0:rows, 1, f], lg[0:rows, 0, f], ACT.Exp, bias=lsum[0:rows, 0, f:f + 1],
                                            accum_out=lsum[0:rows, 1, f:f + 1])
            last.then_inc(s.moe_le, 1)
            act.wait_ge(s.bn_ready, 1)
            for p in range(EP):
                for l, (done, hid) in enumerate(((s.moe_h1, h1), (s.moe_h2, h2))):
                    act.wait_ge(done, p + 1)
                    if l == 1 and p >= 2:
                        act.wait_ge(s.moe_y, p - 1)
                    nc.scalar.activation(hid[:, p % 2].rearrange("p b t -> p (b t)").rearrange("p (a n) -> p a n", a=2),
                                         ps[:, 2 * l:2 * l + 2, 0:2 * T], ACT.Relu, bias=bn[:, 1, p, l:l + 1],
                                         scale=bn[:, 0, p, l:l + 1]).then_inc((s.moe_a1, s.moe_a2)[l], 1)
                if p == 0:
                    act.wait_ge(s.moe_gt, 1)
                    nc.scalar.copy(gt[:], ps[0:E_, 7, 0:T]).then_inc(s.moe_gts, 1)
                    act.wait_ge(s.moe_gb, 1)
                    nc.scalar.copy(gb.rearrange("p (c a) t -> p c (a t)", c=2), ps[:, 6:8, 0:2 * T]).then_inc(s.moe_gbs, 1)

        @block.vector
        def _(dve_):
            nonlocal dve
            dve = dve_
            dve.wait_ge(s.in_x, 16)
            dve.wait_ge(s.tok_mean, 1)
            nc.vector.tensor_tensor(tk[:, 0], x_sb[:], ps[0:PC, 0, 0:TOK].unsqueeze(1).broadcast_to([PC, 2, TOK]),
                                    ALU.subtract).then_inc(s.tok_xc, 1)
            dve.wait_ge(s.tok_std, 1)
            link(nc.vector.reciprocal(tk[:, 2, 1], tk[:, 2, 0]))
            dve.wait_ge(s.in_tokp, 16)
            for c in range(2):
                link(nc.vector.tensor_tensor(tk[:, 3, c], tk[:, 0, c], tk[:, 2, 1], ALU.mult))
            for c in range(2):
                nc.vector.tensor_scalar(tk[:, 3, c], tk[:, 3, c], tokp_sb[:, c:c + 1], tokp_sb[:, 2 + c:3 + c],
                                        ALU.mult, ALU.add).then_inc(s.tok_xn, 1)
            dve.wait_ge(s.ssm_n2, 1)
            nc.vector.reciprocal(sp_[:, 8:9], sp_[:, 7:8]).then_inc(s.ssm_rn, 1)
            dve.wait_ge(s.in_p64, 16)
            ln_dve("ln2", tz[:, 0], tz[:, 1], [(0, TOK)], (3, 4), (col("ln2_g"), col("ln2_b")))
            dve.wait_ge(s.ssm_r0, 1)
            link(nc.vector.tensor_scalar(sp_[:, 20:21], sp_[:, 13:14], 1e-30, None, ALU.max))
            nc.vector.reciprocal(sp_[:, 14:15], sp_[:, 20:21]).then_inc(s.ssm_rinv, 1)
            ln_dve("lnp", tz[:, 2], tz[:, 3], [(0, TOK)], (6, 7), (col("lnp_g"), col("lnp_b")))
            dve.wait_ge(s.ssm_r, 1)
            link(nc.vector.tensor_scalar(sp_[:, 20:21], sp_[:, 13:14], 1e-30, None, ALU.max))
            nc.vector.reciprocal(sp_[:, 14:15], sp_[:, 20:21]).then_inc(s.ssm_ri2, 1)
            dve.wait_ge(s.silu_e, 1)
            link(nc.vector.tensor_scalar(tz[:, 4], tz[:, 4], 1.0, None, ALU.add))
            link(nc.vector.reciprocal(tz[:, 5], tz[:, 4]))
            nc.vector.tensor_tensor(tz[:, 4], tz[:, 3], tz[:, 5], ALU.mult).then_inc(s.silu_out, 1)
            ln_dve("lns", u_sb, x1, [(0, TOK + 1)], (1, 2))
            dve.wait_ge(s.ssm_bx, 1)
            dve.wait_ge(s.ssm_phase, 1)
            v = vq[:, 0, 0:TIMED].rearrange("p (b t) -> p b t", b=NB)
            bx = ps[:, 0, 0:TOK + 1]
            nc.vector.tensor_scalar(v[:, :, 0], bx[:, TOK:TOK + 1].broadcast_to([128, NB]), pin[:, 0:1], None, ALU.mult)
            for b in range(NB):
                last = nc.vector.tensor_tensor(
                    v[:, b, 1:T].rearrange("p (s j) -> p s j", s=REP),
                    bx[:, b * SEG:(b + 1) * SEG].unsqueeze(1).broadcast_to([128, REP, SEG]),
                    pin[:, 1:T].rearrange("p (s j) -> p s j", s=REP), ALU.mult)
                if b < NB - 1:
                    last.then_inc(s.dve_chain, 1)
                    nlink[0] += 1
            link(last)
            dve.wait_ge(s.ssm_r, 1)
            for b in range(NB):
                nc.vector.tensor_tensor_scan(g_sb[:, b], sp_[:, 13:14].broadcast_to([128, T]), v[:, b], 0.0,
                                             ALU.mult, ALU.add).then_inc(s.ssm_g, 1)
            dve.wait_ge(s.ssm_g, NB)
            nc.vector.tensor_copy(vq[:, 0, CLS:CLS + 1], g_sb[:, 0, 0:1])
            nc.vector.tensor_tensor(vq[:, 0, 0:CLS].rearrange("p (b t) -> p b t", b=NB), g_sb[:, :, 1:T],
                                    ph[:, 0, 1:T].unsqueeze(1).broadcast_to([128, NB, T - 1]),
                                    ALU.mult).then_inc(s.ssm_q, 1)
            for i, (a, b) in enumerate(HALF_F):
                dve.wait_ge(s.ssm_y, i + 1)
                for bb in (2 * i, 2 * i + 1):
                    last = nc.vector.tensor_tensor(
                        res[:, bb * (T - 1):(bb + 1) * (T - 1)].rearrange("p (s j) -> p s j", s=REP),
                        ps[0:D, 1 + i, (bb % 2) * (T - 1):(bb % 2 + 1) * (T - 1)].rearrange("p (s j) -> p s j", s=REP),
                        u_sb[:, bb * SEG:(bb + 1) * SEG].unsqueeze(1).broadcast_to([D, REP, SEG]), ALU.add)
                    if bb == 3:
                        link(last)
                        last = nc.vector.tensor_tensor(res[:, CLS:CLS + 1], ps[0:D, 2, b - 1 - a:b - a],
                                                       u_sb[:, TOK:TOK + 1], ALU.add)
                last.then_inc(s.res_flat, 1)
            ln_dve("lnf", res, x2, HALF_F, (3, 5))
            dve.wait_ge(s.bn_sd, 1)
            nc.vector.reciprocal(bn[:, 0], bn[:, 3]).then_inc(s.bn_rec, 1)

            def shaped(ap):
                return ap.rearrange("p (b t) -> p b t", b=NB)

            dve.wait_ge(ln.out, LN_BASE["lnf"] + 2)
            for dst, src in ((rest, res), (x2t, x2)):
                nc.vector.tensor_copy(shaped(dst[:])[:, :, 1:T], shaped(src[:, 0:CLS]))
                nc.vector.tensor_copy(shaped(dst[:])[:, :, 0], src[:, CLS:FLAT].broadcast_to([D, NB])
                                      ).then_inc(s.timed_ready, 1)

            def best_tile(u, n, rows):
                k = [0]
                sm, tp = sim[0:rows, u], top[0:rows]

                def lk(ins):
                    k[0] += 1
                    ins.then_inc(s.top_chain, 1)
                    dve.wait_ge(s.top_chain, n * TOP_LINKS + k[0])
                    settle(dve)

                dve.wait_ge(s.sims_ready, 2 * n + 2)
                settle(dve)
                for f in range(2 * H):
                    last = nc.vector.max(tp[:, f, 0:8], sm[:, f])
                lk(last)
                for f in range(2 * H):
                    last = nc.vector.match_replace(rest_sims[0:rows, f], tp[:, f, 0:8], sm[:, f], NEG)
                lk(last)
                for f in range(2 * H):
                    last = nc.vector.max(tp[:, f, 8:16], rest_sims[0:rows, f])
                lk(last)
                cd = [cand[0:rows, v] for v in range(2)]
                f0, f1 = tp[:, 0:H], tp[:, H:2 * H]
                at = 0
                a = 0
                while a < TOPK:
                    m = STAIR[a]
                    e = a
                    while e < TOPK and STAIR[e] == m:
                        e += 1
                    shape = [rows, H, e - a, m]
                    last = nc.vector.tensor_tensor(
                        cd[0][:, :, at:at + (e - a) * m].rearrange("p h (x y) -> p h x y", y=m),
                        f0[:, :, a:e].unsqueeze(3).broadcast_to(shape),
                        f1[:, :, 0:m].unsqueeze(2).broadcast_to(shape), ALU.add)
                    at += (e - a) * m
                    a = e
                lk(last)
                for r in range(2):
                    for h in range(H):
                        last = nc.vector.max(best[0:rows, h, 8 * r:8 * r + 8], cd[r][:, h])
                    lk(last)
                    if r < 1:
                        for h in range(H):
                            last = nc.vector.match_replace(cd[r + 1][:, h], best[0:rows, h, 8 * r:8 * r + 8], cd[r][:, h], NEG)
                        lk(last)
                v16 = best[0:rows, :, TOPK - 1]
                stt = nc.vector.scalar_tensor_tensor
                lk(stt(cut[0:rows, 0], f1[:, :, TOPK - 1], -1.0, f1[:, :, 0], ALU.mult, ALU.max))
                lk(stt(cut[0:rows, 1], v16, -1.0, cut[0:rows, 0], ALU.mult, ALU.max))
                lk(nc.vector.tensor_tensor(cut[0:rows, 1], cut[0:rows, 1], v16, ALU.max))
                lk(nc.vector.scalar_tensor_tensor(cut[0:rows, 0], cut[0:rows, 1], -SLACK, v16, ALU.mult, ALU.add))
                lk(nc.vector.scalar_tensor_tensor(cut[0:rows, 2], best[0:rows, :, 0], -GUARD, cut[0:rows, 0], ALU.add, ALU.max))
                nc.vector.tensor_tensor(ez[0:rows, 0], best[0:rows, :, 0:TOPK],
                                        cut[0:rows, 2].unsqueeze(2).broadcast_to([rows, H, TOPK]),
                                        ALU.subtract).then_inc(s.cut_e, 1)
                nc.vector.tensor_tensor(s0p[0:rows, u, :, 0], sm[:, 0:H],
                                        cut[0:rows, 2].unsqueeze(2).broadcast_to([rows, H, NK]),
                                        ALU.subtract).then_inc(s.s0p_ready, 1)
                dve.wait_ge(s.cut_es, n + 1)
                lk(nc.vector.reduce_sum(cut[0:rows, 0], ez[0:rows, 1], AX))
                nc.vector.reciprocal(zinv[0:rows, u], cut[0:rows, 0]).then_inc(s.zinv_ready, 1)
                assert k[0] == TOP_LINKS

            with dve.Fori(0, NTILE // 2) as i:
                for u in range(2):
                    best_tile(u, 2 * i + u, TILE)
            best_tile(0, NTILE, 1)

            dve.sem_inc(s.w_used, NW)
            dve.wait_ge(s.even_ready, 1)
            dve.wait_ge(s.tr0_read, NTILE + 2)

            def add(h, c):
                dve.wait_ge(s.b_ready, h * 2 * CH + c + 1)
                nc.vector.tensor_tensor(d_sb[:, c % ND].rearrange("p (a n) -> p a n", a=2),
                                        ps[:, 2 * (c % 2):2 * (c % 2) + 2, 0:WH],
                                        s0t[:, bass.ds(h, 1), :].rearrange("p o (a n) -> p (o a) n", a=2),
                                        ALU.add).then_inc(s.d_ready, 1)

            def weigh(h, c):
                dve.wait_ge(s.e_ready, h * 2 * CH + c + 1)
                dve.wait_ge(s.w_used, h * 2 * CH + c + 1)
                nc.vector.scalar_tensor_tensor(w_sb[:, c % NW], d_sb[:, c % ND], 0.0, e_sb[:, c % NE],
                                               ALU.is_ge, ALU.mult).then_inc(s.w_ready, 1)

            def head(h, last):
                for c in range(2 * CH):
                    if c < 2 * CH - 1:
                        add(h, c + 1)
                    elif not last:
                        add(h + 1, 0)
                    weigh(h, c)

            add(0, 0)
            with dve.Fori(0, H - 1) as h:
                head(h, False)
            head(H - 1, True)

            with dve.Fori(0, H) as h:
                dve.wait_ge(s.acc_read, h + 2)
                dve.wait_ge(s.trz_read, NTILE + 2)
                kh, zh = kv[:, bass.ds(h, 1), :], zbc[:, bass.ds(h, 1), :]
                nc.vector.tensor_tensor(kvh[:, :, 1:T], kh[:, :, 0:CLS].rearrange("p o (b t) -> p (o b) t", b=NB),
                                        zh[:, :, 0:CLS].rearrange("p o (b t) -> p (o b) t", b=NB), ALU.mult)
                nc.vector.tensor_tensor(kvh[:, :, 0:1], kh[:, :, CLS:FLAT].broadcast_to([128, NB, 1]),
                                        zh[:, :, CLS:FLAT].broadcast_to([128, NB, 1]), ALU.mult).then_inc(s.kvh_ready, 1)
                dve.wait_ge(s.qk_done, h + 1)
                nc.vector.tensor_tensor(a0[:], ps[:, 2, :].rearrange("p (b j) -> p b j", b=NB),
                                        mask0.unsqueeze(1).broadcast_to([TILE, NB, TILE]), ALU.add)
                n1 = T - TILE
                nc.vector.tensor_tensor(a1[:].rearrange("p (a b) j -> p a b j", a=2),
                                        ps[0:n1, 3:5, 0:2 * T].rearrange("p a (b j) -> p a b j", b=2),
                                        mask1.unsqueeze(1).unsqueeze(1).broadcast_to([n1, 2, 2, T]),
                                        ALU.add).then_inc(s.sc_ready, 1)
                dve.wait_ge(s.sc_ready, h + 1)
                nc.vector.tensor_reduce(amax[:, 0], a0[:], AX, ALU.max, negate=True)
                nc.vector.tensor_reduce(amax[0:n1, 1], a1[:], AX, ALU.max, negate=True).then_inc(s.nm_ready, 1)
                dve.wait_ge(s.p_exp, h + 1)
                nc.vector.reciprocal(arec[:, 0], asum[:, 0])
                nc.vector.reciprocal(arec[0:n1, 1], asum[0:n1, 1]).then_inc(s.rec_ready, 1)
                dve.wait_ge(s.rec_ready, h + 1)
                nc.vector.tensor_tensor(a0[:], a0[:], arec[:, 0].unsqueeze(2).broadcast_to([TILE, NB, TILE]), ALU.mult)
                nc.vector.tensor_tensor(a1[:], a1[:], arec[0:n1, 1].unsqueeze(2).broadcast_to([n1, NB, T]),
                                        ALU.mult).then_inc(s.p_ready, 1)
                dve.wait_ge(s.vw_done, h + 2)
                nc.vector.tensor_copy(vw0[:], ps[:, 2, 0:NB * D].rearrange("p (b e) -> p b e", b=NB))
                nc.vector.tensor_copy(vw1[:], ps[0:n1, 3, 0:NB * D].rearrange("p (b e) -> p b e", b=NB)
                                      ).then_inc(s.vw_ready, 1)
                dve.wait_ge(s.pv_done, h + 1)
                rv = rest[:].rearrange("p (a n) -> p a n", a=2)
                nc.vector.tensor_tensor(rv, rv, ps[0:D, 0:2, 0:2 * T], ALU.add).then_inc(s.res_att, 1)

            ln_dve("lna", rest, xl, HALF_T, (2, 4))
            dve.wait_ge(s.fir_w, 1)
            for a in range(2):
                dve.wait_ge(ln.out, LN_BASE["lna"] + a + 1)
                nc.vector.tensor_copy(xpad[D:128, 2 * a:2 * a + 2, TAPS + 1:TAPS + T],
                                      xl[:, 2 * a * T:(2 * a + 2) * T].rearrange("p (b t) -> p b t", b=2)[:, :, 0:T - 1]
                                      ).then_inc(s.fir_pad, 1)
            link(nc.vector.reduce_sum(tot[:, 0], shaped(xl), AX))
            nc.vector.tensor_scalar(tot[:, 1], tot[:, 0], col("m0"), None, ALU.mult).then_inc(s.fir_tot, 1)
            dve.wait_ge(s.fir_tbs, 1)
            for b in range(NB):
                if b % 2 == 0:
                    dve.wait_ge(s.fir_done, b // 2 + 1)
                r = rest[:, b * T:(b + 1) * T]
                nc.vector.scalar_tensor_tensor(r, ps[0:D, b // 2, (b % 2) * T:(b % 2 + 1) * T], tot[:, 2, b:b + 1], r,
                                               ALU.add, ALU.add).then_inc(s.res_fir, 1)

            ln_dve("lnm", rest, xl, HALF_T, (2, 4))
            dve.wait_ge(ln.out, LN_BASE["lnm"] + 2)
            nc.vector.reduce_sum(feat[:], shaped(xl).rearrange("p b t -> p t b"), AX).then_inc(s.moe_feat, 1)
            dve.wait_ge(s.moe_log, 1)
            for f, rows in ((0, TILE), (1, T - TILE)):
                link(nc.vector.tensor_scalar(lg[0:rows, 0, f], ps[0:rows, 6, f * E_:(f + 1) * E_], 1.0 / NB, None, ALU.mult))
                last = nc.vector.tensor_reduce(lsum[0:rows, 0, f:f + 1], lg[0:rows, 0, f], AX, ALU.max, negate=True)
            last.then_inc(s.moe_nm, 1)
            dve.wait_ge(s.moe_le, 1)
            for f, rows in ((0, TILE), (1, T - TILE)):
                link(nc.vector.reciprocal(lsum[0:rows, 2, f:f + 1], lsum[0:rows, 1, f:f + 1]))
                nc.vector.tensor_scalar(lg[0:rows, 2, f], lg[0:rows, 1, f], lsum[0:rows, 2, f:f + 1], None,
                                        ALU.mult).then_inc(s.moe_gate, 1)
            dve.wait_ge(s.moe_gbs, 1)
            for p in range(EP):
                dve.wait_ge(s.moe_a2, p + 1)
                nc.vector.tensor_tensor(h2[:, p % 2], h2[:, p % 2], gb[:, p].unsqueeze(1).broadcast_to([128, NB, T]),
                                        ALU.mult).then_inc(s.moe_w2g, 1)
            dve.wait_ge(s.moe_y, EP)
            for a, (lo, hi) in enumerate(HALF_T):
                nc.vector.tensor_tensor(rest[:, lo:hi], rest[:, lo:hi], ps[0:D, 4 + a, 0:2 * T], ALU.add
                                        ).then_inc(s.out_ready, 1)

        @block.tensor
        def _(pe_):
            nonlocal pe
            pe = pe_
            mm = nc.tensor.matmul
            pe.wait_ge(s.ones_ready, 1)
            pe.wait_ge(s.in_x, 16)
            for c in range(2):
                last = mm(ps[0:PC, 0, 0:TOK], onesp[:], x_sb[:, c], start=(c == 0), stop=(c == 1))
            last.then_inc(s.tok_mean, 1)
            pe.wait_ge(s.tok_sq, 1)
            for c in range(2):
                last = mm(ps[0:PC, 1, 0:TOK], onesp[:], tk[:, 1, c], start=(c == 0), stop=(c == 1))
            last.then_inc(s.tok_var, 1)
            pe.wait_ge(s.tok_xn, 2)
            for c in range(2):
                last = mm(ps[0:D, 2, 0:TOK], tokp_sb[:, 4 + c * D:4 + (c + 1) * D], tk[:, 3, c],
                          start=(c == 0), stop=(c == 1))
            last.then_inc(s.tok_z, 1)
            ln_pe("ln2", tz[:, 0], s.tok_zb, [1], [(0, TOK)], (3, 4))
            pe.wait_ge(ln.out, LN_BASE["ln2"] + 1)
            mm(ps[0:D, 5, 0:TOK], col("Wp1", D), tz[:, 1], start=True, stop=True).then_inc(s.tok_h, 1)
            ln_pe("lnp", tz[:, 2], s.tok_hb, [1], [(0, TOK)], (6, 7))
            pe.wait_ge(s.silu_out, 1)
            mm(ps[0:D, 0, 0:TOK], col("Wp2", D), tz[:, 4], start=True, stop=True).then_inc(s.tok_o, 1)
            pe.wait_ge(s.cls_ready, 1)
            ln_pe("lns", u_sb, s.tok_ready, [1], [(0, TOK + 1)], (1, 2))
            pe.wait_ge(ln.out, LN_BASE["lns"] + 1)
            mm(ps[:, 0, 0:TOK + 1], col("BT2", 128), x1[:], start=True, stop=True).then_inc(s.ssm_bx, 1)
            pe.wait_ge(s.ssm_wc, 1)
            pe.wait_ge(s.ssm_q, 1)
            pe.wait_ge(s.ssm_q2, 1)
            for i, (a, b) in enumerate(HALF_F):
                mm(ps[0:D, 1 + i, 0:b - a], wcs[:, 0, :], vq[:, 0, a:b], start=True, stop=False)
                mm(ps[0:D, 1 + i, 0:b - a], wcs[:, 1, :], vq[:, 1, a:b], start=False, stop=True).then_inc(s.ssm_y, 1)
            pe.wait_ge(s.in_keys, 16)
            pe.wait_ge(s.silu_out, 1)
            for q in range(4):
                if q == 2:
                    pe.wait_ge(s.res_flat, 2)
                for g in range(4):
                    last = mm(ps[0:D, 4 * (q % 2) + q // 2, g * NK:(g + 1) * NK], pkw_sb[DK * q:DK * q + DK, 0, g],
                              pkw_sb[DK * q:DK * q + DK, 1, g], start=True, stop=True)
                last.then_inc(s.pk_m, 1)
            pe.wait_ge(s.pk_mc, 4)
            ln_pe("lnf", res, s.res_flat, [1, 2], HALF_F, (3, 5))

            def scores(u, n, rows):
                pe.wait_ge(s.xst_ready, n + 1)
                pe.wait_ge(s.sims_ready, 2 * n)
                for k in range(2):
                    last = mm(ps[0:rows, k, :], xst[:, u, 0:rows], m_sb[:, 512 * k:512 * k + 512], start=True, stop=True)
                last.then_inc(s.sim_done, 1)

            def turn(u, n, rows):
                pe.wait_ge(s.s1p_ready, n + 2)
                pe.wait_ge(s.tr1_read, n + 1)
                for f in range(2 * H):
                    last = nc.tensor.transpose(ps[0:3 * JH, 6 + f // 8, :].bitcast(BF16)[:, (f % 8) * 128:(f % 8) * 128 + rows],
                                               s1p[0:rows, u, f].rearrange("p a k -> p (a k)"), identb[0:rows, 0:rows])
                last.then_inc(s.tr1_done, 1)
                pe.wait_ge(s.s0p_ready, n + 1)
                pe.wait_ge(s.s0q_ready, n + 1)
                pe.wait_ge(s.tr0_read, n + 1)
                for h in range(H):
                    last = nc.tensor.transpose(ps[:, 2 + h // 4, (h % 4) * 128:(h % 4) * 128 + rows],
                                               s0p[0:rows, u, h].rearrange("p a k -> p (a k)"),
                                               ident[0:rows, 0:rows])
                last.then_inc(s.tr0_done, 1)
                pe.wait_ge(s.zinv_ready, n + 1)
                pe.wait_ge(s.trz_read, n + 1)
                for h in range(H):
                    last = mm(ps[:, 4 + h // 4, (h % 4) * 128:(h % 4) * 128 + rows],
                              zinv[0:rows, u, h:h + 1].broadcast_to([rows, 128]), ident[0:rows, 0:rows],
                              start=True, stop=True)
                last.then_inc(s.trz_done, 1)

            pe.wait_ge(s.identb_ready, 1)
            for read in (s.tr0_read, s.tr1_read, s.trz_read):
                pe.sem_inc(read, 1)
            scores(0, 0, TILE)
            with pe.Fori(0, NTILE // 2 - 1) as i:
                for u in range(2):
                    scores(1 - u, 2 * i + u + 1, TILE)
                    turn(u, 2 * i + u, TILE)
            scores(1, NTILE - 1, TILE)
            turn(0, NTILE - 2, TILE)
            scores(0, NTILE, 1)
            turn(1, NTILE - 1, TILE)
            turn(0, NTILE, 1)

            pe.wait_ge(s.sel_ready, 1)
            pe.wait_ge(s.even_ready, 1)
            pe.wait_ge(s.trz_read, NTILE + 2)

            def spread(h, c, free):
                if free:
                    pe.wait_ge(s.d_ready, h * 2 * CH + c - 1)
                for a in range(2):
                    last = mm(ps[:, 2 * (c % 2) + a, 0:WH], sel_sb[:, c % CH],
                              s1t[:, bass.ds(2 * h + c // CH, 1), a * WH:(a + 1) * WH], start=True, stop=True)
                last.then_inc(s.b_ready, 1)

            def gather(h, c):
                if c == 0:
                    pe.wait_ge(s.acc_read, h + 1)
                if c % GRP == 0:
                    pe.wait_ge(tab_in[c // GRP], 16 * (h + 1))
                pe.wait_ge(s.w_ready, h * 2 * CH + c + 1)
                for a in range(2):
                    last = mm(ps[:, 4 + a, 0:WH], tab_sb[:, c // GRP, c % GRP], w_sb[:, c % NW, a * WH:(a + 1) * WH],
                              start=(c == 0), stop=(c == 2 * CH - 1))
                last.then_inc(s.w_used, 1)

            def pe_head(h, last):
                for c in range(2 * CH):
                    if c < 2 * CH - 2:
                        spread(h, c + 2, True)
                    elif not last:
                        spread(h + 1, c - (2 * CH - 2), True)
                    gather(h, c)

            pe.sem_inc(s.acc_read, 1)
            spread(0, 0, False)
            spread(0, 1, False)
            with pe.Fori(0, H - 1) as h:
                pe_head(h, False)
            pe_head(H - 1, True)

            n1 = T - TILE
            pe.wait_ge(s.timed_ready, 2)
            pe.sem_inc(s.res_att, 1)
            with pe.Fori(0, H) as h:
                pe.wait_ge(s.wst_ready, h + 1)
                pe.wait_ge(s.res_att, h + 1)
                settle(pe)
                for a, (lo, hi) in enumerate(HALF_T):
                    last = mm(ps[0:D, a, 0:2 * T], wst[0:D], x2t[:, lo:hi], start=True, stop=True)
                last.then_inc(s.q_done, 1)
                pe.wait_ge(s.q_ready, h + 1)
                pe.wait_ge(s.kvh_ready, h + 1)
                for b in range(NB):
                    mm(ps[:, 2, b * TILE:(b + 1) * TILE], q_sb[:, b, 0:TILE], kvh[0:D, b, 0:TILE], start=True, stop=True)
                for b in range(NB):
                    last = mm(ps[0:n1, 3 + b // 2, (b % 2) * T:(b % 2) * T + T], q_sb[:, b, TILE:T], kvh[0:D, b],
                              start=True, stop=True)
                last.then_inc(s.qk_done, 1)
                pe.wait_ge(s.sc_ready, h + 1)
                for b in range(NB):
                    mm(ps[:, 2, b * D:(b + 1) * D], kvh[D:128, b, 0:TILE], wst[D:128], start=True, stop=True)
                for b in range(NB):
                    last = mm(ps[0:n1, 3, b * D:(b + 1) * D], kvh[D:128, b, TILE:T], wst[D:128], start=True, stop=True)
                last.then_inc(s.vw_done, 1)
                pe.wait_ge(s.p_ready, h + 1)
                for b in range(NB):
                    nc.tensor.transpose(ps[:, 5, b * TILE:(b + 1) * TILE], a0[:, b], ident)
                    nc.tensor.transpose(ps[:, 6, b * n1:(b + 1) * n1], a1[:, b, 0:TILE], ident[0:n1, 0:n1])
                    last = nc.tensor.transpose(ps[0:n1, 7, b * n1:(b + 1) * n1], a1[:, b, TILE:T], ident[0:n1, 0:n1])
                last.then_inc(s.pt_done, 1)
                pe.wait_ge(s.pt_ready, h + 1)
                pe.wait_ge(s.vw_ready, h + 1)
                settle(pe)
                for b in range(NB):
                    y = ps[0:D, b // 2, (b % 2) * T:(b % 2) * T + T]
                    mm(y[:, 0:TILE], vw0[:, b], pt0[:, b], start=True, stop=True)
                    mm(y[:, TILE:T], vw0[:, b], pt1[:, b], start=True, stop=False)
                    last = mm(y[:, TILE:T], vw1[:, b], pt2[:, b], start=False, stop=True)
                last.then_inc(s.pv_done, 1)

            ln_pe("lna", rest, s.res_att, [H + 1, H + 1], HALF_T, (2, 4))
            pe.wait_ge(s.fir_w, 1)
            for a in range(2):
                pe.wait_ge(s.fir_in, a + 1)
                pe.wait_ge(s.fir_pad, a + 1)
                for k in range(PAIRS):
                    last = mm(ps[0:D, a, 0:2 * T], firw[:, k], xpad[:, 2 * a:2 * a + 2, TAPS - 2 * k:TAPS - 2 * k + T],
                              start=(k == 0), stop=(k == PAIRS - 1))
                last.then_inc(s.fir_done, 1)
                if a == 0:
                    pe.wait_ge(s.fir_tot, 1)
                    mm(ps[0:D, 6, 0:NB], col("W2", D), tot[:, 1], start=True, stop=True).then_inc(s.fir_tb, 1)

            ln_pe("lnm", rest, s.res_fir, [2, 4], HALF_T, (2, 4))
            pe.wait_ge(s.in_moe_w, 16)
            pe.wait_ge(ln.out, LN_BASE["lnm"] + 2)

            def layer1(p):
                if p:
                    pe.wait_ge(s.moe_a1, p)
                for a, (lo, hi) in enumerate(HALF_T):
                    last = mm(ps[:, a, 0:2 * T], w1m[:, p * 128:(p + 1) * 128], xl[:, lo:hi], start=True, stop=True)
                last.then_inc(s.moe_h1, 1)

            layer1(0)
            pe.wait_ge(s.moe_feat, 1)
            for f, rows in ((0, TILE), (1, T - TILE)):
                lo = f * TILE
                mm(ps[0:rows, 6, f * E_:(f + 1) * E_], feat[:, lo:lo + rows], col("Wr", E_), start=True, stop=False)
                last = mm(ps[0:rows, 6, f * E_:(f + 1) * E_], four[:, 0:rows], brm, start=False, stop=True)
            last.then_inc(s.moe_log, 1)
            for p in range(EP):
                pe.wait_ge(s.moe_a1, p + 1)
                if p:
                    pe.wait_ge(s.moe_a2, p)
                for a in range(2):
                    last = mm(ps[:, 2 + a, 0:2 * T], w2m[:, p], h1[:, p % 2, 2 * a:2 * a + 2], start=True, stop=True)
                last.then_inc(s.moe_h2, 1)
                if p < EP - 1:
                    layer1(p + 1)
                if p == 0:
                    pe.wait_ge(s.moe_gate, 2)
                    for f, rows in ((0, TILE), (1, T - TILE)):
                        last = nc.tensor.transpose(ps[0:E_, 7, f * TILE:f * TILE + rows], lg[0:rows, 2, f], ident[0:rows, 0:rows])
                    last.then_inc(s.moe_gt, 1)
                    pe.wait_ge(s.moe_gts, 1)
                    for q in range(EP):
                        last = mm(ps[:, 6 + q // 2, (q % 2) * T:(q % 2 + 1) * T], e8m[:, q], gt[:], start=True, stop=True)
                    last.then_inc(s.moe_gb, 1)
                    for a in range(2):
                        mm(ps[0:D, 4 + a, 0:2 * T], bom, gt[:].unsqueeze(1).broadcast_to([E_, 2, T]), start=True, stop=False)
                pe.wait_ge(s.moe_w2g, p + 1)
                for a in range(2):
                    last = mm(ps[0:D, 4 + a, 0:2 * T], wom[:, p, 0:D], h2[:, p % 2, 2 * a:2 * a + 2],
                              start=False, stop=(p == EP - 1))
                last.then_inc(s.moe_y, 1)


def layouts(inp):
    import numpy as np
    f = {k: np.asarray(v) for k, v in inp.items()}
    a = {}
    x = f["x"].reshape(NB, 3, 8, 8, 8, 8)
    a["xT"] = x.transpose(3, 5, 1, 0, 2, 4).reshape(2, PC, TOK).transpose(1, 0, 2)
    two = lambda v: v.reshape(2, PC, -1).transpose(1, 0, 2).reshape(PC, -1)
    a["tokp"] = np.concatenate([two(f["L0_tok_ln1_g"]), two(f["L0_tok_ln1_b"]), two(f["L0_tok_W1"])], axis=1)
    c1 = lambda v: v.reshape(D, 1)
    BT = f["L0_attn_B"].T
    a["p64"] = np.concatenate(
        [c1(f[k]) for k in ("L0_tok_b1", "L0_tok_ln2_g", "L0_tok_ln2_b", "L0_tok_bp1", "L0_tok_lnp_g",
                            "L0_tok_lnp_b", "L0_tok_bp2", "cls_tok", "L1_attn_bias")]
        + [c1(f["L1_attn_memory_weights"][0]), f["L0_tok_Wp1"], f["L0_tok_Wp2"], BT, BT,
           f["L1_attn_W1"], f["L1_attn_W2"], f["L1_ffn_Wr"]], axis=1)
    d2 = lambda v: np.concatenate([v, v]).reshape(128, 1)
    Cr, Ci = f["L0_attn_C_real"].T, f["L0_attn_C_imag"].T
    a["p128"] = np.concatenate([d2(f["L0_attn_log_lambda_real"]), d2(f["L0_attn_lambda_imag"]), d2(f["L0_attn_log_dt"]),
                                np.concatenate([Cr, Ci]), np.concatenate([Ci, Cr])], axis=1)
    const = np.zeros((128, CC["end"]), np.float32)
    const[:, :128] = np.eye(128)
    i, j = np.arange(TILE)[:, None], np.arange(T)[None, :]
    const[:, CC["m0"]:CC["m0"] + TILE] = np.where(j[:, :TILE] <= i, 0.0, NEG)
    const[:T - TILE, CC["m1"]:CC["m1"] + T] = np.where(j <= TILE + i[:T - TILE], 0.0, NEG)
    a["const"] = const
    sel = np.zeros((3, JH, CH, 2, NK), np.float32)
    for n in range(JH):
        sel[:, n, n // 2, n % 2, :] = 1.0
    a["sel"] = sel.reshape(3 * JH, CH, 128)
    wq = f["L0_ffn_Wq_pk"].T.reshape(4, 4, DK, D).transpose(1, 2, 0, 3)
    kk = f["L0_ffn_pk_keys"].transpose(0, 2, 3, 1).reshape(4, 4, DK, NK).transpose(1, 2, 0, 3)
    a["pkw"] = np.stack([wq.reshape(128, 4, D), kk.reshape(128, 4, NK)], axis=1)
    tab = np.concatenate([f["L0_ffn_keys_table"], f["L0_ffn_values_table"]], axis=1)
    a["table"] = tab.reshape(H * 8, GRP, 128, 128).transpose(0, 2, 1, 3)
    a["wqo"] = np.concatenate([f["L0_ffn_Wq"].reshape(D, H, D).transpose(1, 0, 2), f["L0_ffn_Wo"].reshape(H, D, D)],
                              axis=1).transpose(1, 0, 2)
    mw = np.zeros((2 * PAIRS, D), np.float32)
    mw[:TAPS + 1] = f["L1_attn_memory_weights"]
    both = lambda v: np.concatenate([v, v])
    a["fir"] = np.concatenate([mw.reshape(PAIRS, 2, D).transpose(1, 2, 0).reshape(128, PAIRS), d2(f["L1_attn_memory_weights"][0]),
                               both(f["L1_attn_W2"]), both(f["L1_attn_W1"])], axis=1)
    prm = np.stack([f["L1_ffn_" + k] for k in ("b1", "g1", "be1", "m1", "v1", "b2", "g2", "be2", "m2", "v2")])
    a["moe"] = prm.reshape(MOE_P, 4, 128).transpose(2, 1, 0)
    e8 = np.zeros((E_, 4, 2, D), np.float32)
    for e in range(E_):
        e8[e, e // 2, e % 2] = 1.0
    w = np.zeros((5, 128, E_ * D), np.float32)
    w[0, :D] = f["L1_ffn_W1"].transpose(1, 0, 2).reshape(D, E_ * D)
    w2 = f["L1_ffn_W2"].reshape(4, 2, D, D)
    for q in range(2):
        w[1].reshape(128, 4, 128)[q * D:(q + 1) * D, :, q * D:(q + 1) * D] = w2[:, q].transpose(1, 0, 2)
    w[2].reshape(128, 4, 128)[:, :, :D] = f["L1_ffn_Wo"].reshape(4, 128, D).transpose(1, 0, 2)
    w[3, :E_, :D] = f["L1_ffn_bo"]
    w[3, 0, D:D + E_] = f["L1_ffn_br"]
    w[4, :E_] = e8.reshape(E_, 512)
    a["moe_w"] = w.transpose(1, 0, 2)
    return {k: np.ascontiguousarray(v) for k, v in a.items()}


def kernel(**inputs):
    import numpy as _np
    import concourse.bacc as _bacc
    from concourse import mybir as _mybir
    from concourse.bass_utils import run_bass_kernel_spmd as _run

    nc = _bacc.Bacc("TRN2", target_bir_lowering=False, num_devices=1)
    arrays, args = {}, {}
    for name, a in layouts(inputs).items():
        arrays[f"in_{name}"] = a
        args[name] = nc.dram_tensor(f"in_{name}", a.shape, _mybir.dt.from_np(a.dtype), kind="ExternalInput").ap()
    out = nc.dram_tensor("out", (D, TIMED), F32, kind="ExternalOutput").ap()
    tower(nc, out=out, **args)
    r = _run(nc, [arrays], core_ids=[0])
    return _np.ascontiguousarray(r.results[0]["out"].T).reshape(NB, T, D)
```

```python
from collections import namedtuple
from contextlib import ExitStack

import concourse.bass as bass
from concourse import mybir

ALU = mybir.AluOpType
ACT = mybir.ActivationFunctionType
AX = mybir.AxisListType.X
F32 = mybir.dt.float32
BF16 = mybir.dt.bfloat16

NB = 4
D = 64
SEG = 64
REP = 3
T = 1 + REP * SEG
TOK = NB * SEG
FLAT = NB * (T - 1) + 1
CLS = FLAT - 1
TIMED = NB * T
HALF_F = [(0, 2 * (T - 1)), (2 * (T - 1), FLAT)]
HALF_T = [(0, 2 * T), (2 * T, TIMED)]
PATCH = 192
PC = PATCH // 2
EPS = 1e-5
TOP_LINKS = 13
BN_EPS = 1e-3

H = 8
NK = 64
TOPK = 16
DK = 32
GUARD = 60.0
SLACK = float(2 ** -22)
NEG = -3.0e38
STAIR = [TOPK // (a + 1) for a in range(TOPK)]
NCAND = sum(STAIR)
WIDE = FLAT + FLAT % 2
WH = WIDE // 2
TILE = 128
NTILE = (FLAT - 1) // TILE
JH = 32
CH = 16
GRP = 4

NTG = 2 * CH // GRP
ND, NE, NW = 4, 2, 4

HALF_CH = CH
Q_AT, QK_AT, VW_AT, PT_AT, Y_AT = 0, 2, 6, 10, 12
QS_AT, EXP_AT, VS_AT, PTS_AT = 2, 7, 9, 12
MASK_AT, REC_AT, RES_AT = 4, 8, 14

TAPS = 40
PAIRS = (TAPS + 2) // 2
E_ = 8
EP = E_ // 2

C64 = dict(tok_b1=0, ln2_g=1, ln2_b=2, bp1=3, lnp_g=4, lnp_b=5, bp2=6, cls=7, l1_bias=8, m0=9,
           Wp1=10, Wp2=74, BT2=138, W1=266, W2=330, Wr=394, end=402)
C128 = dict(lr=0, li=1, ldt=2, CriT=3, CirT=67, end=131)
CC = dict(ident=0, m0=TILE, m1=2 * TILE, end=2 * TILE + T)
MOE_P = 10
SEMS = """
in_x in_tokp in_p64 in_p128 in_const in_sel in_keys in_wqo in_moe in_moe_w in_fir
ones_ready pool_chain dve_chain top_chain
tok_mean tok_xc tok_sq tok_var tok_std tok_xn tok_z tok_zb tok_h tok_hb silu_e silu_out tok_o tok_ready cls_ready
ssm_exp ssm_n2 ssm_rn ssm_r2 ssm_r ssm_r0 ssm_rinv ssm_ri2 ssm_phase ssm_wc ssm_bx ssm_g ssm_q ssm_q2 ssm_y res_flat
pk_m pk_mc identb_ready sel_ready xst_ready sim_done sims_ready cut_e cut_es s0p_ready zinv_ready
s1h s1r s1m s1p_ready s0q_ready settled tr0_done tr0_read trz_done trz_read tr1_done tr1_read even_ready
b_ready d_ready e_ready w_ready w_used acc_read
tab0 tab1 tab2 tab3 tab4 tab5 tab6 tab7
timed_ready wst_ready kvh_ready q_done q_ready qk_done sc_ready nm_ready p_exp rec_ready p_ready pt_done pt_ready
vw_done vw_ready pv_done res_att
fir_w fir_pad fir_in fir_tot fir_tb fir_tbs fir_done res_fir
bn_sd bn_rec bn_ready
moe_feat moe_log moe_nm moe_le moe_gate moe_gt moe_gts moe_gb moe_gbs moe_h1 moe_a1 moe_h2 moe_a2 moe_w2g moe_y out_ready
out_done
""".split()


Semaphores = namedtuple("Semaphores", SEMS)
LN_SEMS = ("mean", "xc", "sq", "var", "std", "out")
LnSemaphores = namedtuple("LnSemaphores", LN_SEMS)


def tower(nc, xT, tokp, p64, p128, const, sel, pkw, table, wqo, fir, moe, moe_w, out):
    with ExitStack() as ctx:
        def sb(name, shape, dt=F32):
            return ctx.enter_context(nc.sbuf_tensor(name, shape, dt))

        ps = ctx.enter_context(nc.psum_tensor("ps", [128, 8, 512], F32))
        s = Semaphores(*[ctx.enter_context(nc.semaphore(n)) for n in SEMS])
        LN_BASE = dict(ln2=0, lnp=1, lns=2, lnf=3, lna=5, lnm=7)
        ln = LnSemaphores(*[ctx.enter_context(nc.semaphore("ln_" + n)) for n in LN_SEMS])

        kv = sb("kv", [128, H, WIDE])
        zbc = sb("zbc", [128, H, WIDE])
        rings = sb("rings", [128, (ND + NE + NW) * WIDE])
        taken = {}

        def part(region, shape, dt=F32, stage=0):
            flat = region.rearrange("p a b -> p (a b)") if region.ndim == 3 else region
            flat = flat if region.dtype == F32 else flat.bitcast(F32)
            n = 1
            for x in shape[1:]:
                n *= x
            words = n if dt == F32 else n // 2
            at = taken.get((region.name, stage), 0)
            taken[region.name, stage] = at + words
            assert at + words <= flat.shape[1]
            v = flat[0:shape[0], at:at + words]
            v = v if dt == F32 else v.bitcast(dt)
            names = "abcde"[:len(shape) - 1]
            if len(names) > 1:
                v = v.rearrange(f"p ({' '.join(names)}) -> p {' '.join(names)}",
                                **dict(zip(names[1:], shape[2:])))
            return v

        x_sb = part(zbc[:], [PC, 2, TOK])
        tokp_sb = sb("tokp_sb", [PC, 4 + 2 * D])
        p64_sb = sb("p64_sb", [D, C64["end"]])
        p128_sb = sb("p128_sb", [128, C128["end"]])
        const_sb = sb("const_sb", [128, CC["end"]])
        sel_sb = sb("sel_sb", [3 * JH, CH, 128], BF16)
        pkw_sb = part(zbc[:], [128, 2, 4, 64])
        fir_sb = sb("fir_sb", [128, PAIRS + 1 + 2 * D])
        moe_sb = sb("moe_sb", [128, 4, MOE_P])
        onesp = sb("onesp", [PC, PC])
        ones64 = sb("ones64", [D, D])
        four = sb("four", [1, 128])
        bn = sb("bn", [128, 4, EP, 2])
        eps_sb = sb("eps_sb", [128, 2])

        def col(name, n=1):
            return p64_sb[:, C64[name]:C64[name] + n]

        def par(name, n=1):
            return p128_sb[:, C128[name]:C128[name] + n]

        ident = const_sb[:, CC["ident"]:CC["ident"] + 128]
        mask0 = const_sb[:, CC["m0"]:CC["m0"] + TILE]
        mask1 = const_sb[0:T - TILE, CC["m1"]:CC["m1"] + T]

        tk = part(kv[:], [PC, 4, 2, TOK])
        u_sb = part(zbc[:], [D, TOK + 1])
        lnw = part(zbc[:], [D, 3, TIMED])
        tz = part(kv[:], [D, 6, TOK])
        sp_ = sb("sp_", [128, 32])
        ph = sb("ph", [128, 2, T])
        pht = part(zbc[:], [128, 2, SEG * 2])
        pin = part(zbc[:], [128, T])
        pin2 = part(zbc[:], [128, T])
        wcs = sb("wcs", [128, 2, D])
        vq = part(kv[:], [128, 2, FLAT + 3])
        g_sb = part(kv[:], [128, NB, T])
        res = sb("res", [D, FLAT])
        x1 = part(zbc[:], [D, TOK + 1])
        x2 = sb("x2", [D, FLAT])

        m_sb = sb("m_sb", [D, 2 * H * NK])
        identb = sb("identb", [128, 128], BF16)
        xst = sb("xst", [D, 2, TILE])
        sim = part(rings[:], [128, 2, 2 * H, NK])
        rest_sims = part(kv[:], [128, 2 * H, NK], stage=1)
        top = part(rings[:], [128, 2 * H, TOPK])
        cand = part(kv[:], [128, 2, H, NCAND], stage=1)
        best = sb("best", [128, H, TOPK])
        cut = sb("cut", [128, 3, H])
        ez = sb("ez", [128, 2, H, TOPK])
        zinv = sb("zinv", [128, 2, H])
        s0p = part(rings[:], [128, 2, H, 2, NK])
        s1p = part(rings[:], [128, 2, 2 * H, 3, JH], BF16)
        s1r = part(rings[:], [128, 2 * H, JH])
        s0t = sb("s0t", [128, H, WIDE])
        s1t_all = sb("s1t", [128, 2 * H, WIDE], BF16)
        s1t = s1t_all[0:3 * JH]
        tab_sb = sb("tab_sb", [128, NTG, GRP, 128])
        ring = rings[:].rearrange("p (a n) -> p a n", n=WIDE)
        d_sb, e_sb, w_sb = ring[:, 0:ND], ring[:, ND:ND + NE], ring[:, ND + NE:ND + NE + NW]
        tab_in = [s.tab0, s.tab1, s.tab2, s.tab3, s.tab4, s.tab5, s.tab6, s.tab7]
        x2t = sb("x2t", [D, TIMED])
        rest = sb("rest", [D, TIMED])
        wqo_sb = sb("wqo_sb", [128, H, D])
        wst = sb("wst", [128, D])
        kvh = sb("kvh", [128, NB, T])
        q_sb = sb("q_sb", [D, NB, T])
        a0 = sb("a0", [TILE, NB, TILE])
        a1 = sb("a1", [T - TILE, NB, T])
        amax = sb("amax", [TILE, 2, NB])
        asum = sb("asum", [TILE, 2, NB])
        arec = sb("arec", [TILE, 2, NB])
        pt0 = sb("pt0", [TILE, NB, TILE])
        pt1 = sb("pt1", [TILE, NB, T - TILE])
        pt2 = sb("pt2", [T - TILE, NB, T - TILE])
        vw0 = sb("vw0", [TILE, NB, D])
        vw1 = sb("vw1", [T - TILE, NB, D])

        def settle(eng):
            eng.sem_inc(s.settled, 1)

        sel_in = part(rings[:], [3 * JH, CH, 128], stage=1)

        moew = part(s0t[:], [128, 5, E_ * D])
        xpad = part(s0t[:], [128, NB, TAPS + T])
        firw = part(s0t[:], [128, PAIRS, D])
        firm = part(s0t[:], [128, PAIRS])
        xl = part(s1t_all[:], [D, TIMED])
        h1 = part(s1t_all[:], [128, 2, NB, T])
        h2 = part(s1t_all[:], [128, 2, NB, T])
        gb = part(s1t_all[:], [128, EP, T])
        tot = sb("tot", [D, 3, NB])
        feat = sb("feat", [D, T])
        lg = sb("lg", [TILE, 3, 2, E_])
        lsum = sb("lsum", [TILE, 3, 2])
        gt = sb("gt", [E_, T])
        w1m, w2m, wom = moew[0:D, 0], moew[:, 1].rearrange("p (a k) -> p a k", a=EP), moew[:, 2].rearrange("p (a k) -> p a k", a=EP)
        bom, brm, e8m = moew[0:E_, 3, 0:D], moew[0:1, 3, D:D + E_], moew[0:E_, 4].rearrange("p (a k) -> p a k", a=EP)

        pe = act = dve = None
        nlink = [0]

        def link(ins):
            nlink[0] += 1
            ins.then_inc(s.dve_chain, 1)
            dve.wait_ge(s.dve_chain, nlink[0])

        def ln_pe(k, src, ready, need, parts, banks):
            for i, (a, b) in enumerate(parts):
                pe.wait_ge(ready, need[i])
                nc.tensor.matmul(ps[0:D, banks[0] + i, 0:b - a], ones64[:], src[:, a:b],
                                 start=True, stop=True).then_inc(ln.mean, 1)
            for i, (a, b) in enumerate(parts):
                pe.wait_ge(ln.sq, LN_BASE[k] + i + 1)
                nc.tensor.matmul(ps[0:D, banks[1] + i, 0:b - a], ones64[:], lnw[:, 1, a:b],
                                 start=True, stop=True).then_inc(ln.var, 1)

        def ln_act(k, parts, banks):
            for i, (a, b) in enumerate(parts):
                act.wait_ge(ln.xc, LN_BASE[k] + i + 1)
                nc.scalar.activation(lnw[:, 1, a:b], lnw[:, 0, a:b], ACT.Square).then_inc(ln.sq, 1)
            for i, (a, b) in enumerate(parts):
                act.wait_ge(ln.var, LN_BASE[k] + i + 1)
                nc.scalar.activation(lnw[:, 2, a:b], ps[0:D, banks[1] + i, 0:b - a], ACT.Sqrt,
                                     bias=eps_sb[0:D, 0:1]).then_inc(ln.std, 1)

        def ln_dve(k, src, dst, parts, banks, affine=None):
            for i, (a, b) in enumerate(parts):
                dve.wait_ge(ln.mean, LN_BASE[k] + i + 1)
                nc.vector.tensor_tensor(lnw[:, 0, a:b], src[:, a:b], ps[0:D, banks[0] + i, 0:b - a],
                                        ALU.subtract).then_inc(ln.xc, 1)
            for i, (a, b) in enumerate(parts):
                dve.wait_ge(ln.std, LN_BASE[k] + i + 1)
                link(nc.vector.reciprocal(lnw[:, 2, a:b], lnw[:, 2, a:b]))
                last = nc.vector.tensor_tensor(dst[:, a:b], lnw[:, 0, a:b], lnw[:, 2, a:b], ALU.mult)
                if affine:
                    link(last)
                    last = nc.vector.tensor_scalar(dst[:, a:b], dst[:, a:b], affine[0], affine[1],
                                                   ALU.mult, ALU.add)
                last.then_inc(ln.out, 1)

        block = ctx.enter_context(nc.Block())

        @block.sync
        def _(sp):
            for dst, src, done in (
                (x_sb[:], xT, s.in_x), (tokp_sb[:], tokp, s.in_tokp), (p64_sb[:], p64, s.in_p64),
                (p128_sb[:], p128, s.in_p128), (const_sb[:], const, s.in_const), (pkw_sb[:], pkw, s.in_keys),
                (sel_in, sel, s.in_sel), (wqo_sb[:], wqo, s.in_wqo),
                (moe_sb[:], moe, s.in_moe), (fir_sb[:], fir, s.in_fir),
            ):
                sp.dma_start(dst, src).then_inc(done, 16)
            for g in range(NTG):
                sp.dma_start(tab_sb[:, g], table[g]).then_inc(tab_in[g], 16)
            with sp.Fori(0, H - 1) as h:
                for g in range(NTG):
                    sp.wait_ge(s.w_used, NW + h * 2 * CH + (g + 1) * GRP)
                    sp.dma_start(tab_sb[:, g], table[bass.ds((h + 1) * NTG + g, 1)]
                                 .rearrange("o p c k -> (o p) c k")).then_inc(tab_in[g], 16)
            sp.wait_ge(s.w_used, NW + H * 2 * CH)
            sp.dma_start(moew, moe_w).then_inc(s.in_moe_w, 16)
            for a, (lo, hi) in enumerate(HALF_T):
                sp.wait_ge(s.out_ready, a + 1)
                sp.dma_start(out[:, lo:hi], rest[:, lo:hi]).then_inc(s.out_done, 16)
            sp.wait_ge(s.out_done, 32)

        @block.gpsimd
        def _(pool):
            n = [0]

            def pl(ins):
                n[0] += 1
                ins.then_inc(s.pool_chain, 1)
                pool.wait_ge(s.pool_chain, n[0])

            nc.gpsimd.memset(onesp[:], 1.0 / PATCH)
            nc.gpsimd.memset(ones64[:], 1.0 / D)
            nc.gpsimd.memset(four[:], float(NB))
            nc.gpsimd.memset(eps_sb[:, 1:2], BN_EPS)
            nc.gpsimd.memset(eps_sb[:, 0:1], EPS).then_inc(s.ones_ready, 1)

            EL, DT, AR, AI, OM, AI2, AR2, N2, RN, T1, ARE, AIM, R2, R, RI, C1, S1, BRE, BIM, P2 = range(20)

            def c(k):
                return sp_[:, k:k + 1]

            tt, ts, stt = nc.gpsimd.tensor_tensor, nc.gpsimd.tensor_scalar, nc.gpsimd.scalar_tensor_tensor
            pool.wait_ge(s.in_p128, 16)
            pool.wait_ge(s.ssm_exp, 2)
            pl(ts(c(DT), c(DT), 0.005, 0.1, ALU.max, ALU.min))
            pl(tt(c(AR), c(DT), c(EL), ALU.mult))
            pl(ts(c(AR), c(AR), -0.5, None, ALU.mult))
            pl(tt(c(AI), c(DT), par("li"), ALU.mult))
            pl(ts(c(AI), c(AI), 0.5, None, ALU.mult))
            pl(ts(c(OM), c(AR), -1.0, 1.0, ALU.mult, ALU.add))
            pl(tt(c(AI2), c(AI), c(AI), ALU.mult))
            pl(tt(c(AR2), c(AR), c(AR), ALU.mult))
            pl(tt(c(N2), c(OM), c(OM), ALU.mult))
            tt(c(N2), c(N2), c(AI2), ALU.add).then_inc(s.ssm_n2, 1)
            pl(tt(c(T1), c(AR2), c(AI2), ALU.add))
            pl(ts(c(T1), c(T1), -1.0, 1.0, ALU.mult, ALU.add))
            pl(tt(c(BRE), c(DT), c(OM), ALU.mult))
            pl(tt(c(BIM), c(DT), c(AI), ALU.mult))
            pool.wait_ge(s.ssm_rn, 1)
            pl(tt(c(ARE), c(T1), c(RN), ALU.mult))
            pl(tt(c(AIM), c(AI), c(RN), ALU.mult))
            pl(ts(c(AIM), c(AIM), 2.0, None, ALU.mult))
            pl(tt(c(BRE), c(BRE), c(RN), ALU.mult))
            pl(tt(c(BIM), c(BIM), c(RN), ALU.mult))
            pl(tt(c(R2), c(ARE), c(ARE), ALU.mult))
            pl(tt(c(T1), c(AIM), c(AIM), ALU.mult))
            tt(c(R2), c(R2), c(T1), ALU.add).then_inc(s.ssm_r2, 1)
            pool.wait_ge(s.ssm_rinv, 1)
            pl(tt(c(T1), c(R2), c(RI), ALU.mult))
            pl(tt(c(R), c(R), c(T1), ALU.add))
            ts(c(R), c(R), 0.5, None, ALU.mult).then_inc(s.ssm_r, 1)
            pool.wait_ge(s.ssm_ri2, 1)
            pl(nc.gpsimd.memset(ph[:, 0, 0:1], 1.0))
            pl(nc.gpsimd.memset(ph[:, 1, 0:1], 0.0))
            pl(tt(ph[:, 0, 1:2], c(ARE), c(RI), ALU.mult))
            pl(tt(ph[:, 1, 1:2], c(AIM), c(RI), ALU.mult))
            m = 1
            while m < T - 1:
                w = min(m, T - 1 - m)
                cm, sm = ph[:, 0, m:m + 1], ph[:, 1, m:m + 1]
                cs, ss = ph[:, 0, 1:1 + w], ph[:, 1, 1:1 + w]
                ts(pht[:, 0, 0:w], ss, sm, None, ALU.mult)
                pl(ts(pht[:, 1, 0:w], ss, cm, None, ALU.mult))
                ts(ph[:, 0, m + 1:m + 1 + w], cs, cm, None, ALU.mult)
                pl(ts(ph[:, 1, m + 1:m + 1 + w], cs, sm, None, ALU.mult))
                tt(ph[:, 0, m + 1:m + 1 + w], ph[:, 0, m + 1:m + 1 + w], pht[:, 0, 0:w], ALU.subtract)
                pl(tt(ph[:, 1, m + 1:m + 1 + w], ph[:, 1, m + 1:m + 1 + w], pht[:, 1, 0:w], ALU.add))
                m += w
            for lo, a, b, neg in ((0, BRE, BIM, False), (D, BIM, BRE, True)):
                q = slice(lo, lo + D)
                pl(ts(pin[q, :], ph[q, 0, :], sp_[q, a:a + 1], None, ALU.mult))
                pl(ts(pin2[q, :], ph[q, 1, :], sp_[q, b:b + 1], None, ALU.mult))
                last = tt(pin[q, :], pin[q, :], pin2[q, :], ALU.subtract if neg else ALU.add)
                pl(last) if lo == 0 else last.then_inc(s.ssm_phase, 1)
            pool.wait_ge(s.ssm_phase, 1)
            pl(ts(wcs[0:D, 0, :], p128_sb[0:D, C128["CriT"]:C128["CriT"] + D], 1.0, None, ALU.mult))
            pl(ts(wcs[D:128, 0, :], p128_sb[D:128, C128["CriT"]:C128["CriT"] + D], -1.0, None, ALU.mult))
            ts(wcs[:, 1, :], par("CirT", D), -1.0, None, ALU.mult).then_inc(s.ssm_wc, 1)
            pool.wait_ge(s.ssm_g, NB)
            nc.gpsimd.memset(vq[:, 1, CLS:CLS + 1], 0.0)
            tt(vq[:, 1, 0:CLS].rearrange("p (b t) -> p b t", b=NB), g_sb[:, :, 1:T],
               ph[:, 1, 1:T].unsqueeze(1).broadcast_to([128, NB, T - 1]), ALU.mult).then_inc(s.ssm_q2, 1)
            nc.gpsimd.memset(s0t[:, :, FLAT:WIDE], -1.0)
            nc.gpsimd.memset(s1t[:, :, FLAT:WIDE], 0.0).then_inc(s.even_ready, 1)

            def pieces(u, n, rows):
                pool.wait_ge(s.s1h, n + 1)
                pool.wait_ge(s.s1p_ready, n + 1)
                tt(s1r[0:rows], sim[0:rows, u, H:2 * H].rearrange("p h (j k) -> p (h j) k", j=2),
                   s1p[0:rows, u, :, 0], ALU.subtract).then_inc(s.s1r, 1)
                pool.wait_ge(s.s1m, n + 1)
                tt(s1p[0:rows, u, :, 2], s1r[0:rows], s1p[0:rows, u, :, 1], ALU.subtract).then_inc(s.s1p_ready, 1)
                pool.wait_ge(s.s0p_ready, n + 1)
                tt(s0p[0:rows, u, :, 1], sim[0:rows, u, 0:H], cut[0:rows, 2].unsqueeze(2).broadcast_to([rows, H, NK]),
                   ALU.subtract).then_inc(s.s0q_ready, 1)

            pool.sem_inc(s.s1p_ready, 1)
            with pool.Fori(0, NTILE // 2) as i:
                for u in range(2):
                    pieces(u, 2 * i + u, TILE)
            pieces(0, NTILE, 1)
            with pool.Fori(0, H) as h:
                pool.wait_ge(s.acc_read, h + 2)
                pool.wait_ge(s.vw_done, 2 * h + 1)
                kh, zh = kv[:, bass.ds(h, 1), :], zbc[:, bass.ds(h, 1), :]
                tt(kvh[:, :, 1:T], kh[:, :, 0:CLS].rearrange("p o (b t) -> p (o b) t", b=NB),
                   zh[:, :, 0:CLS].rearrange("p o (b t) -> p (o b) t", b=NB), ALU.mult)
                tt(kvh[:, :, 0:1], kh[:, :, CLS:FLAT].broadcast_to([128, NB, 1]),
                   zh[:, :, CLS:FLAT].broadcast_to([128, NB, 1]), ALU.mult).then_inc(s.kvh_ready, 1)
                for a in range(2):
                    b2 = slice(2 * a, 2 * a + 2)
                    pool.wait_ge(s.rec_ready, 2 * h + a + 1)
                    tt(a0[:, b2], a0[:, b2], arec[:, 0, b2].unsqueeze(2).broadcast_to([TILE, 2, TILE]), ALU.mult)
                    tt(a1[:, b2], a1[:, b2], arec[0:T - TILE, 1, b2].unsqueeze(2).broadcast_to([T - TILE, 2, T]),
                       ALU.mult).then_inc(s.p_ready, 1)
            pool.wait_ge(s.bn_rec, 1)
            prm = moe_sb[:].rearrange("p a (l k) -> p a l k", l=2)
            pl(tt(bn[:, 0], prm[:, :, :, 1], bn[:, 0], ALU.mult))
            pl(tt(bn[:, 2], prm[:, :, :, 0], prm[:, :, :, 3], ALU.subtract))
            pl(tt(bn[:, 2], bn[:, 2], bn[:, 0], ALU.mult))
            tt(bn[:, 1], bn[:, 2], prm[:, :, :, 2], ALU.add).then_inc(s.bn_ready, 1)
            pool.wait_ge(s.in_fir, 16)
            pool.wait_ge(s.w_used, NW + H * 2 * CH)
            nc.gpsimd.memset(xpad[:, :, 0:TAPS + 1], 0.0)
            pl(ts(firm, fir_sb[:, 0:PAIRS], fir_sb[:, PAIRS:PAIRS + 1], None, ALU.subtract))
            pl(tt(firw, firm.unsqueeze(2).broadcast_to([128, PAIRS, D]),
                  fir_sb[:, PAIRS + 1:PAIRS + 1 + D].unsqueeze(1).broadcast_to([128, PAIRS, D]), ALU.mult))
            pl(nc.gpsimd.memset(firw[D:128, PAIRS - 1], 0.0))
            nc.gpsimd.tensor_copy(firw[0:D, 0], fir_sb[0:D, PAIRS + 1 + D:PAIRS + 1 + 2 * D]).then_inc(s.fir_w, 1)

        @block.scalar
        def _(act_):
            nonlocal act
            act = act_
            act.wait_ge(s.ones_ready, 1)
            act.wait_ge(s.tok_xc, 1)
            nc.scalar.activation(tk[:, 1], tk[:, 0], ACT.Square).then_inc(s.tok_sq, 1)
            act.wait_ge(s.in_p128, 16)
            nc.scalar.activation(sp_[:, 0:1], par("lr"), ACT.Exp).then_inc(s.ssm_exp, 1)
            nc.scalar.activation(sp_[:, 1:2], par("ldt"), ACT.Exp).then_inc(s.ssm_exp, 1)
            act.wait_ge(s.tok_var, 1)
            nc.scalar.activation(tk[:, 2, 0], ps[0:PC, 1, 0:TOK], ACT.Sqrt, bias=eps_sb[0:PC, 0:1]).then_inc(s.tok_std, 1)
            act.wait_ge(s.in_p64, 16)
            act.wait_ge(s.tok_z, 1)
            nc.scalar.activation(tz[:, 0], ps[0:D, 2, 0:TOK], ACT.Identity, bias=col("tok_b1")).then_inc(s.tok_zb, 1)
            nc.scalar.copy(u_sb[:, TOK:TOK + 1], col("cls")).then_inc(s.cls_ready, 1)
            act.wait_ge(s.ssm_r2, 1)
            nc.scalar.activation(sp_[:, 13:14], sp_[:, 12:13], ACT.Sqrt).then_inc(s.ssm_r0, 1)
            ln_act("ln2", [(0, TOK)], (3, 4))
            act.wait_ge(s.tok_h, 1)
            nc.scalar.activation(tz[:, 2], ps[0:D, 5, 0:TOK], ACT.Identity, bias=col("bp1")).then_inc(s.tok_hb, 1)
            ln_act("lnp", [(0, TOK)], (6, 7))
            act.wait_ge(ln.out, LN_BASE["lnp"] + 1)
            nc.scalar.activation(tz[:, 4], tz[:, 3], ACT.Exp, scale=-1.0).then_inc(s.silu_e, 1)
            act.wait_ge(s.tok_o, 1)
            nc.scalar.activation(u_sb[:, 0:TOK], ps[0:D, 0, 0:TOK], ACT.Identity, bias=col("bp2")).then_inc(s.tok_ready, 1)
            ln_act("lns", [(0, TOK + 1)], (1, 2))
            act.wait_ge(s.in_sel, 16)
            nc.scalar.copy(sel_sb[:], sel_in).then_inc(s.sel_ready, 1)
            act.wait_ge(s.in_moe, 16)
            nc.scalar.activation(bn[:, 3], moe_sb[:].rearrange("p a (l k) -> p a l k", l=2)[:, :, :, 4], ACT.Sqrt,
                                 bias=eps_sb[:, 1:2]).then_inc(s.bn_sd, 1)
            act.wait_ge(s.in_const, 16)
            nc.scalar.copy(identb[:], ident).then_inc(s.identb_ready, 1)
            mv = m_sb[:].rearrange("p (g q k) -> p g q k", g=4, q=4)
            for q in range(4):
                act.wait_ge(s.pk_m, q + 1)
                nc.scalar.copy(mv[:, :, q], ps[0:D, 4 * (q % 2) + q // 2, 0:4 * NK].rearrange("p (g k) -> p g k", g=4)
                               ).then_inc(s.pk_mc, 1)

            ln_act("lnf", HALF_F, (3, 5))

            def stage_tile(u, lo, rows):
                nc.scalar.copy(xst[:, u, 0:rows], x2[:, lo]).then_inc(s.xst_ready, 1)

            def scores_out(u, n, rows):
                act.wait_ge(s.sim_done, n + 1)
                for k in range(2):
                    nc.scalar.copy(sim[0:rows, u, 8 * k:8 * k + 8], ps[0:rows, k, :].rearrange("p (h k) -> p h k", k=NK)
                                   ).then_inc(s.sims_ready, 1)
                act.wait_ge(s.sims_ready, 2 * n + 2)
                nc.scalar.copy(s1p[0:rows, u, :, 0], sim[0:rows, u, H:2 * H].rearrange("p h (j k) -> p (h j) k", j=2)
                               ).then_inc(s.s1h, 1)
                act.wait_ge(s.s1r, n + 1)
                nc.scalar.copy(s1p[0:rows, u, :, 1], s1r[0:rows]).then_inc(s.s1m, 1)

            def turned_out(n, lo, rows):
                act.wait_ge(s.cut_e, n + 1)
                nc.scalar.activation(ez[0:rows, 1], ez[0:rows, 0], ACT.Exp).then_inc(s.cut_es, 1)
                act.wait_ge(s.tr0_done, n + 1)
                nc.scalar.copy(s0t[:, :, lo], ps[:, 2:4, :].rearrange("p a (h k) -> p (a h) k", h=4)[:, :, 0:rows]
                               ).then_inc(s.tr0_read, 1)
                act.wait_ge(s.tr1_done, n + 1)
                nc.scalar.copy(s1t[:, :, lo], ps[0:3 * JH, 6:8, :].bitcast(BF16).rearrange("p a (h k) -> p (a h) k", h=8)[:, :, 0:rows]
                               ).then_inc(s.tr1_read, 1)
                act.wait_ge(s.trz_done, n + 1)
                nc.scalar.copy(zbc[:, :, lo], ps[:, 4:6, :].rearrange("p a (h k) -> p (a h) k", h=4)[:, :, 0:rows]
                               ).then_inc(s.trz_read, 1)

            act.wait_ge(ln.out, LN_BASE["lnf"] + 2)
            stage_tile(0, slice(0, TILE), TILE)
            scores_out(0, 0, TILE)
            with act.Fori(0, NTILE // 2 - 1) as i:
                for u in range(2):
                    n = 2 * i + u
                    stage_tile(1 - u, bass.ds((n + 1) * TILE, TILE), TILE)
                    scores_out(1 - u, n + 1, TILE)
                    turned_out(n, bass.ds(n * TILE, TILE), TILE)
            n = NTILE - 2
            stage_tile(1, slice(n * TILE + TILE, CLS), TILE)
            scores_out(1, n + 1, TILE)
            turned_out(n, slice(n * TILE, n * TILE + TILE), TILE)
            stage_tile(0, slice(CLS, FLAT), 1)
            scores_out(0, NTILE, 1)
            turned_out(n + 1, slice(n * TILE + TILE, CLS), TILE)
            turned_out(NTILE, slice(CLS, FLAT), 1)

            def head_weights(h):
                act.wait_ge(s.vw_done, 2 * h + 1)
                nc.scalar.copy(wst[:].unsqueeze(1), wqo_sb[:, bass.ds(h, 1), :]).then_inc(s.wst_ready, 1)

            def queries_out(h, a):
                act.wait_ge(s.q_done, 2 * h + a + 1)
                nc.scalar.mul(q_sb[:, 2 * a:2 * a + 2].rearrange("p b t -> p (b t)"), ps[0:D, 6, 0:2 * T],
                              float(D) ** -0.5).then_inc(s.q_ready, 1)

            def values_out(h, a):
                act.wait_ge(s.vw_done, 2 * h + a + 2)
                nc.scalar.copy(vw0[:, 2 * a:2 * a + 2], ps[:, 6, 0:2 * D].rearrange("p (b e) -> p b e", b=2))
                nc.scalar.copy(vw1[:, 2 * a:2 * a + 2],
                               ps[0:T - TILE, 6, 2 * D:4 * D].rearrange("p (b e) -> p b e", b=2)
                               ).then_inc(s.vw_ready, 1)

            def prob_exps(h, a):
                act.wait_ge(s.nm_ready, 2 * h + a + 1)
                for b in range(2 * a, 2 * a + 2):
                    nc.scalar.activation(a0[:, b], a0[:, b], ACT.Exp, bias=amax[:, 0, b:b + 1],
                                         accum_out=asum[:, 0, b:b + 1])
                    last = nc.scalar.activation(a1[:, b], a1[:, b], ACT.Exp, bias=amax[0:T - TILE, 1, b:b + 1],
                                                accum_out=asum[0:T - TILE, 1, b:b + 1])
                last.then_inc(s.p_exp, 1)

            def probs_out(h, a):
                n1, b2 = T - TILE, slice(2 * a, 2 * a + 2)
                act.wait_ge(s.pt_done, 2 * h + a + 1)
                nc.scalar.copy(pt0[:, b2], ps[:, 6, 0:2 * TILE].rearrange("p (b i) -> p b i", b=2))
                nc.scalar.copy(pt1[:, b2], ps[:, 6, 2 * TILE:2 * T].rearrange("p (b i) -> p b i", b=2))
                nc.scalar.copy(pt2[:, b2], ps[0:n1, 7, 0:2 * n1].rearrange("p (b i) -> p b i", b=2)
                               ).then_inc(s.pt_ready, 1)

            def attend(h, c):
                a, k = c // HALF_CH, c % HALF_CH
                if c == 0:
                    head_weights(h)
                for at, step in ((QS_AT, queries_out), (EXP_AT, prob_exps), (VS_AT, values_out), (PTS_AT, probs_out)):
                    if k == at:
                        step(h, a)

            def sums_out(h):
                act.wait_ge(s.w_used, NW + (h + 1) * 2 * CH)
                nc.scalar.copy(kv[:, bass.ds(h, 1), :].rearrange("p o (a n) -> p (o a) n", a=2),
                               ps[:, 4:6, 0:WH]).then_inc(s.acc_read, 1)

            def exps(h, before):
                for c in range(2 * CH):
                    act.wait_ge(s.d_ready, h * 2 * CH + c + 1)
                    nc.scalar.activation(e_sb[:, c % NE], d_sb[:, c % ND], ACT.Exp).then_inc(s.e_ready, 1)
                    if before is not None:
                        if c == 1:
                            sums_out(before)
                        attend(before, c)

            act.wait_ge(s.in_wqo, 16)
            exps(0, None)
            with act.Fori(0, H - 1) as i:
                exps(i + 1, i)
            sums_out(H - 1)
            for c in range(2 * CH):
                attend(H - 1, c)

            ln_act("lna", HALF_T, (2, 4))
            act.wait_ge(s.fir_w, 1)
            for a in range(2):
                act.wait_ge(ln.out, LN_BASE["lna"] + a + 1)
                nc.scalar.copy(xpad[0:D, 2 * a:2 * a + 2, TAPS:TAPS + T],
                               xl[:, 2 * a * T:(2 * a + 2) * T].rearrange("p (b t) -> p b t", b=2)).then_inc(s.fir_in, 1)
            act.wait_ge(s.fir_tb, 1)
            nc.scalar.activation(tot[:, 2], ps[0:D, 6, 0:NB], ACT.Identity, bias=col("l1_bias")).then_inc(s.fir_tbs, 1)

            ln_act("lnm", HALF_T, (2, 4))
            act.wait_ge(s.moe_nm, 1)
            for f, rows in ((0, TILE), (1, T - TILE)):
                last = nc.scalar.activation(lg[0:rows, 1, f], lg[0:rows, 0, f], ACT.Exp, bias=lsum[0:rows, 0, f:f + 1],
                                            accum_out=lsum[0:rows, 1, f:f + 1])
            last.then_inc(s.moe_le, 1)
            act.wait_ge(s.bn_ready, 1)
            for p in range(EP):
                for l, (done, hid) in enumerate(((s.moe_h1, h1), (s.moe_h2, h2))):
                    act.wait_ge(done, p + 1)
                    if l == 1 and p >= 2:
                        act.wait_ge(s.moe_y, p - 1)
                    nc.scalar.activation(hid[:, p % 2].rearrange("p b t -> p (b t)").rearrange("p (a n) -> p a n", a=2),
                                         ps[:, 2 * l:2 * l + 2, 0:2 * T], ACT.Relu, bias=bn[:, 1, p, l:l + 1],
                                         scale=bn[:, 0, p, l:l + 1]).then_inc((s.moe_a1, s.moe_a2)[l], 1)
                if p == 0:
                    act.wait_ge(s.moe_gt, 1)
                    nc.scalar.copy(gt[:], ps[0:E_, 7, 0:T]).then_inc(s.moe_gts, 1)
                    act.wait_ge(s.moe_gb, 1)
                    nc.scalar.copy(gb.rearrange("p (c a) t -> p c (a t)", c=2), ps[:, 6:8, 0:2 * T]).then_inc(s.moe_gbs, 1)

        @block.vector
        def _(dve_):
            nonlocal dve
            dve = dve_
            dve.wait_ge(s.in_x, 16)
            dve.wait_ge(s.tok_mean, 1)
            nc.vector.tensor_tensor(tk[:, 0], x_sb[:], ps[0:PC, 0, 0:TOK].unsqueeze(1).broadcast_to([PC, 2, TOK]),
                                    ALU.subtract).then_inc(s.tok_xc, 1)
            dve.wait_ge(s.tok_std, 1)
            link(nc.vector.reciprocal(tk[:, 2, 1], tk[:, 2, 0]))
            dve.wait_ge(s.in_tokp, 16)
            for c in range(2):
                link(nc.vector.tensor_tensor(tk[:, 3, c], tk[:, 0, c], tk[:, 2, 1], ALU.mult))
            for c in range(2):
                nc.vector.tensor_scalar(tk[:, 3, c], tk[:, 3, c], tokp_sb[:, c:c + 1], tokp_sb[:, 2 + c:3 + c],
                                        ALU.mult, ALU.add).then_inc(s.tok_xn, 1)
            dve.wait_ge(s.ssm_n2, 1)
            nc.vector.reciprocal(sp_[:, 8:9], sp_[:, 7:8]).then_inc(s.ssm_rn, 1)
            dve.wait_ge(s.in_p64, 16)
            ln_dve("ln2", tz[:, 0], tz[:, 1], [(0, TOK)], (3, 4), (col("ln2_g"), col("ln2_b")))
            dve.wait_ge(s.ssm_r0, 1)
            link(nc.vector.tensor_scalar(sp_[:, 20:21], sp_[:, 13:14], 1e-30, None, ALU.max))
            nc.vector.reciprocal(sp_[:, 14:15], sp_[:, 20:21]).then_inc(s.ssm_rinv, 1)
            ln_dve("lnp", tz[:, 2], tz[:, 3], [(0, TOK)], (6, 7), (col("lnp_g"), col("lnp_b")))
            dve.wait_ge(s.ssm_r, 1)
            link(nc.vector.tensor_scalar(sp_[:, 20:21], sp_[:, 13:14], 1e-30, None, ALU.max))
            nc.vector.reciprocal(sp_[:, 14:15], sp_[:, 20:21]).then_inc(s.ssm_ri2, 1)
            dve.wait_ge(s.silu_e, 1)
            link(nc.vector.tensor_scalar(tz[:, 4], tz[:, 4], 1.0, None, ALU.add))
            link(nc.vector.reciprocal(tz[:, 5], tz[:, 4]))
            nc.vector.tensor_tensor(tz[:, 4], tz[:, 3], tz[:, 5], ALU.mult).then_inc(s.silu_out, 1)
            ln_dve("lns", u_sb, x1, [(0, TOK + 1)], (1, 2))
            dve.wait_ge(s.ssm_bx, 1)
            dve.wait_ge(s.ssm_phase, 1)
            v = vq[:, 0, 0:TIMED].rearrange("p (b t) -> p b t", b=NB)
            bx = ps[:, 0, 0:TOK + 1]
            nc.vector.tensor_scalar(v[:, :, 0], bx[:, TOK:TOK + 1].broadcast_to([128, NB]), pin[:, 0:1], None, ALU.mult)
            for b in range(NB):
                last = nc.vector.tensor_tensor(
                    v[:, b, 1:T].rearrange("p (s j) -> p s j", s=REP),
                    bx[:, b * SEG:(b + 1) * SEG].unsqueeze(1).broadcast_to([128, REP, SEG]),
                    pin[:, 1:T].rearrange("p (s j) -> p s j", s=REP), ALU.mult)
                if b < NB - 1:
                    last.then_inc(s.dve_chain, 1)
                    nlink[0] += 1
            link(last)
            dve.wait_ge(s.ssm_r, 1)
            for b in range(NB):
                nc.vector.tensor_tensor_scan(g_sb[:, b], sp_[:, 13:14].broadcast_to([128, T]), v[:, b], 0.0,
                                             ALU.mult, ALU.add).then_inc(s.ssm_g, 1)
            dve.wait_ge(s.ssm_g, NB)
            nc.vector.tensor_copy(vq[:, 0, CLS:CLS + 1], g_sb[:, 0, 0:1])
            nc.vector.tensor_tensor(vq[:, 0, 0:CLS].rearrange("p (b t) -> p b t", b=NB), g_sb[:, :, 1:T],
                                    ph[:, 0, 1:T].unsqueeze(1).broadcast_to([128, NB, T - 1]),
                                    ALU.mult).then_inc(s.ssm_q, 1)
            for i, (a, b) in enumerate(HALF_F):
                dve.wait_ge(s.ssm_y, i + 1)
                for bb in (2 * i, 2 * i + 1):
                    last = nc.vector.tensor_tensor(
                        res[:, bb * (T - 1):(bb + 1) * (T - 1)].rearrange("p (s j) -> p s j", s=REP),
                        ps[0:D, 1 + i, (bb % 2) * (T - 1):(bb % 2 + 1) * (T - 1)].rearrange("p (s j) -> p s j", s=REP),
                        u_sb[:, bb * SEG:(bb + 1) * SEG].unsqueeze(1).broadcast_to([D, REP, SEG]), ALU.add)
                    if bb == 3:
                        link(last)
                        last = nc.vector.tensor_tensor(res[:, CLS:CLS + 1], ps[0:D, 2, b - 1 - a:b - a],
                                                       u_sb[:, TOK:TOK + 1], ALU.add)
                last.then_inc(s.res_flat, 1)
            ln_dve("lnf", res, x2, HALF_F, (3, 5))
            dve.wait_ge(s.bn_sd, 1)
            nc.vector.reciprocal(bn[:, 0], bn[:, 3]).then_inc(s.bn_rec, 1)

            def shaped(ap):
                return ap.rearrange("p (b t) -> p b t", b=NB)

            dve.wait_ge(ln.out, LN_BASE["lnf"] + 2)
            for dst, src in ((rest, res), (x2t, x2)):
                nc.vector.tensor_copy(shaped(dst[:])[:, :, 1:T], shaped(src[:, 0:CLS]))
                nc.vector.tensor_copy(shaped(dst[:])[:, :, 0], src[:, CLS:FLAT].broadcast_to([D, NB])
                                      ).then_inc(s.timed_ready, 1)

            def best_tile(u, n, rows):
                k = [0]
                sm, tp = sim[0:rows, u], top[0:rows]

                def lk(ins):
                    k[0] += 1
                    ins.then_inc(s.top_chain, 1)
                    dve.wait_ge(s.top_chain, n * TOP_LINKS + k[0])
                    settle(dve)

                dve.wait_ge(s.sims_ready, 2 * n + 2)
                settle(dve)
                for f in range(2 * H):
                    last = nc.vector.max(tp[:, f, 0:8], sm[:, f])
                lk(last)
                for f in range(2 * H):
                    last = nc.vector.match_replace(rest_sims[0:rows, f], tp[:, f, 0:8], sm[:, f], NEG)
                lk(last)
                for f in range(2 * H):
                    last = nc.vector.max(tp[:, f, 8:16], rest_sims[0:rows, f])
                lk(last)
                cd = [cand[0:rows, v] for v in range(2)]
                f0, f1 = tp[:, 0:H], tp[:, H:2 * H]
                at = 0
                a = 0
                while a < TOPK:
                    m = STAIR[a]
                    e = a
                    while e < TOPK and STAIR[e] == m:
                        e += 1
                    shape = [rows, H, e - a, m]
                    last = nc.vector.tensor_tensor(
                        cd[0][:, :, at:at + (e - a) * m].rearrange("p h (x y) -> p h x y", y=m),
                        f0[:, :, a:e].unsqueeze(3).broadcast_to(shape),
                        f1[:, :, 0:m].unsqueeze(2).broadcast_to(shape), ALU.add)
                    at += (e - a) * m
                    a = e
                lk(last)
                for r in range(2):
                    for h in range(H):
                        last = nc.vector.max(best[0:rows, h, 8 * r:8 * r + 8], cd[r][:, h])
                    lk(last)
                    if r < 1:
                        for h in range(H):
                            last = nc.vector.match_replace(cd[r + 1][:, h], best[0:rows, h, 8 * r:8 * r + 8], cd[r][:, h], NEG)
                        lk(last)
                v16 = best[0:rows, :, TOPK - 1]
                stt = nc.vector.scalar_tensor_tensor
                lk(stt(cut[0:rows, 0], f1[:, :, TOPK - 1], -1.0, f1[:, :, 0], ALU.mult, ALU.max))
                lk(stt(cut[0:rows, 1], v16, -1.0, cut[0:rows, 0], ALU.mult, ALU.max))
                lk(nc.vector.tensor_tensor(cut[0:rows, 1], cut[0:rows, 1], v16, ALU.max))
                lk(nc.vector.scalar_tensor_tensor(cut[0:rows, 0], cut[0:rows, 1], -SLACK, v16, ALU.mult, ALU.add))
                lk(nc.vector.scalar_tensor_tensor(cut[0:rows, 2], best[0:rows, :, 0], -GUARD, cut[0:rows, 0], ALU.add, ALU.max))
                nc.vector.tensor_tensor(ez[0:rows, 0], best[0:rows, :, 0:TOPK],
                                        cut[0:rows, 2].unsqueeze(2).broadcast_to([rows, H, TOPK]),
                                        ALU.subtract).then_inc(s.cut_e, 1)
                nc.vector.tensor_tensor(s0p[0:rows, u, :, 0], sm[:, 0:H],
                                        cut[0:rows, 2].unsqueeze(2).broadcast_to([rows, H, NK]),
                                        ALU.subtract).then_inc(s.s0p_ready, 1)
                dve.wait_ge(s.cut_es, n + 1)
                lk(nc.vector.reduce_sum(cut[0:rows, 0], ez[0:rows, 1], AX))
                nc.vector.reciprocal(zinv[0:rows, u], cut[0:rows, 0]).then_inc(s.zinv_ready, 1)
                assert k[0] == TOP_LINKS

            with dve.Fori(0, NTILE // 2) as i:
                for u in range(2):
                    best_tile(u, 2 * i + u, TILE)
            best_tile(0, NTILE, 1)

            dve.sem_inc(s.w_used, NW)
            dve.wait_ge(s.even_ready, 1)
            dve.wait_ge(s.tr0_read, NTILE + 2)

            def add(h, c):
                dve.wait_ge(s.b_ready, h * 2 * CH + c + 1)
                nc.vector.tensor_tensor(d_sb[:, c % ND].rearrange("p (a n) -> p a n", a=2),
                                        ps[:, 2 * (c % 2):2 * (c % 2) + 2, 0:WH],
                                        s0t[:, bass.ds(h, 1), :].rearrange("p o (a n) -> p (o a) n", a=2),
                                        ALU.add).then_inc(s.d_ready, 1)

            def weigh(h, c):
                dve.wait_ge(s.e_ready, h * 2 * CH + c + 1)
                dve.wait_ge(s.w_used, h * 2 * CH + c + 1)
                nc.vector.scalar_tensor_tensor(w_sb[:, c % NW], d_sb[:, c % ND], 0.0, e_sb[:, c % NE],
                                               ALU.is_ge, ALU.mult).then_inc(s.w_ready, 1)

            def mask_scores(h, a):
                n1, b2 = T - TILE, slice(2 * a, 2 * a + 2)
                dve.wait_ge(s.qk_done, 2 * h + a + 1)
                nc.vector.tensor_tensor(a0[:, b2], ps[:, 6, 0:2 * TILE].rearrange("p (b j) -> p b j", b=2),
                                        mask0.unsqueeze(1).broadcast_to([TILE, 2, TILE]), ALU.add)
                nc.vector.tensor_tensor(a1[:, b2], ps[0:n1, 7, 0:2 * T].rearrange("p (b j) -> p b j", b=2),
                                        mask1.unsqueeze(1).broadcast_to([n1, 2, T]), ALU.add).then_inc(s.sc_ready, 1)
                dve.wait_ge(s.sc_ready, 2 * h + a + 1)
                nc.vector.tensor_reduce(amax[:, 0, b2], a0[:, b2], AX, ALU.max, negate=True)
                nc.vector.tensor_reduce(amax[0:n1, 1, b2], a1[:, b2], AX, ALU.max, negate=True).then_inc(s.nm_ready, 1)

            def invert_sums(h, a):
                n1, b2 = T - TILE, slice(2 * a, 2 * a + 2)
                dve.wait_ge(s.p_exp, 2 * h + a + 1)
                nc.vector.reciprocal(arec[:, 0, b2], asum[:, 0, b2])
                nc.vector.reciprocal(arec[0:n1, 1, b2], asum[0:n1, 1, b2]).then_inc(s.rec_ready, 1)

            def to_residual(h, a):
                lo, hi = HALF_T[a]
                dve.wait_ge(s.pv_done, 2 * h + a + 1)
                nc.vector.tensor_tensor(rest[:, lo:hi], rest[:, lo:hi], ps[0:D, 7, 0:2 * T], ALU.add).then_inc(s.res_att, 1)

            def attend(h, c):
                for at, step in ((MASK_AT, mask_scores), (REC_AT, invert_sums), (RES_AT, to_residual)):
                    if c % HALF_CH == at:
                        step(h, c // HALF_CH)

            def head(h, before, last):
                for c in range(2 * CH):
                    if c < 2 * CH - 1:
                        add(h, c + 1)
                    elif not last:
                        add(h + 1, 0)
                    weigh(h, c)
                    if before is not None:
                        attend(before, c)

            add(0, 0)
            head(0, None, False)
            with dve.Fori(0, H - 2) as i:
                head(i + 1, i, False)
            head(H - 1, H - 2, True)
            for c in range(2 * CH):
                attend(H - 1, c)

            ln_dve("lna", rest, xl, HALF_T, (2, 4))
            dve.wait_ge(s.fir_w, 1)
            for a in range(2):
                dve.wait_ge(ln.out, LN_BASE["lna"] + a + 1)
                nc.vector.tensor_copy(xpad[D:128, 2 * a:2 * a + 2, TAPS + 1:TAPS + T],
                                      xl[:, 2 * a * T:(2 * a + 2) * T].rearrange("p (b t) -> p b t", b=2)[:, :, 0:T - 1]
                                      ).then_inc(s.fir_pad, 1)
            link(nc.vector.reduce_sum(tot[:, 0], shaped(xl), AX))
            nc.vector.tensor_scalar(tot[:, 1], tot[:, 0], col("m0"), None, ALU.mult).then_inc(s.fir_tot, 1)
            dve.wait_ge(s.fir_tbs, 1)
            for b in range(NB):
                if b % 2 == 0:
                    dve.wait_ge(s.fir_done, b // 2 + 1)
                r = rest[:, b * T:(b + 1) * T]
                nc.vector.scalar_tensor_tensor(r, ps[0:D, b // 2, (b % 2) * T:(b % 2 + 1) * T], tot[:, 2, b:b + 1], r,
                                               ALU.add, ALU.add).then_inc(s.res_fir, 1)

            ln_dve("lnm", rest, xl, HALF_T, (2, 4))
            dve.wait_ge(ln.out, LN_BASE["lnm"] + 2)
            nc.vector.reduce_sum(feat[:], shaped(xl).rearrange("p b t -> p t b"), AX).then_inc(s.moe_feat, 1)
            dve.wait_ge(s.moe_log, 1)
            for f, rows in ((0, TILE), (1, T - TILE)):
                link(nc.vector.tensor_scalar(lg[0:rows, 0, f], ps[0:rows, 6, f * E_:(f + 1) * E_], 1.0 / NB, None, ALU.mult))
                last = nc.vector.tensor_reduce(lsum[0:rows, 0, f:f + 1], lg[0:rows, 0, f], AX, ALU.max, negate=True)
            last.then_inc(s.moe_nm, 1)
            dve.wait_ge(s.moe_le, 1)
            for f, rows in ((0, TILE), (1, T - TILE)):
                link(nc.vector.reciprocal(lsum[0:rows, 2, f:f + 1], lsum[0:rows, 1, f:f + 1]))
                nc.vector.tensor_scalar(lg[0:rows, 2, f], lg[0:rows, 1, f], lsum[0:rows, 2, f:f + 1], None,
                                        ALU.mult).then_inc(s.moe_gate, 1)
            dve.wait_ge(s.moe_gbs, 1)
            for p in range(EP):
                dve.wait_ge(s.moe_a2, p + 1)
                nc.vector.tensor_tensor(h2[:, p % 2], h2[:, p % 2], gb[:, p].unsqueeze(1).broadcast_to([128, NB, T]),
                                        ALU.mult).then_inc(s.moe_w2g, 1)
            dve.wait_ge(s.moe_y, EP)
            for a, (lo, hi) in enumerate(HALF_T):
                nc.vector.tensor_tensor(rest[:, lo:hi], rest[:, lo:hi], ps[0:D, 4 + a, 0:2 * T], ALU.add
                                        ).then_inc(s.out_ready, 1)

        @block.tensor
        def _(pe_):
            nonlocal pe
            pe = pe_
            mm = nc.tensor.matmul
            pe.wait_ge(s.ones_ready, 1)
            pe.wait_ge(s.in_x, 16)
            for c in range(2):
                last = mm(ps[0:PC, 0, 0:TOK], onesp[:], x_sb[:, c], start=(c == 0), stop=(c == 1))
            last.then_inc(s.tok_mean, 1)
            pe.wait_ge(s.tok_sq, 1)
            for c in range(2):
                last = mm(ps[0:PC, 1, 0:TOK], onesp[:], tk[:, 1, c], start=(c == 0), stop=(c == 1))
            last.then_inc(s.tok_var, 1)
            pe.wait_ge(s.tok_xn, 2)
            for c in range(2):
                last = mm(ps[0:D, 2, 0:TOK], tokp_sb[:, 4 + c * D:4 + (c + 1) * D], tk[:, 3, c],
                          start=(c == 0), stop=(c == 1))
            last.then_inc(s.tok_z, 1)
            ln_pe("ln2", tz[:, 0], s.tok_zb, [1], [(0, TOK)], (3, 4))
            pe.wait_ge(ln.out, LN_BASE["ln2"] + 1)
            mm(ps[0:D, 5, 0:TOK], col("Wp1", D), tz[:, 1], start=True, stop=True).then_inc(s.tok_h, 1)
            ln_pe("lnp", tz[:, 2], s.tok_hb, [1], [(0, TOK)], (6, 7))
            pe.wait_ge(s.silu_out, 1)
            mm(ps[0:D, 0, 0:TOK], col("Wp2", D), tz[:, 4], start=True, stop=True).then_inc(s.tok_o, 1)
            pe.wait_ge(s.cls_ready, 1)
            ln_pe("lns", u_sb, s.tok_ready, [1], [(0, TOK + 1)], (1, 2))
            pe.wait_ge(ln.out, LN_BASE["lns"] + 1)
            mm(ps[:, 0, 0:TOK + 1], col("BT2", 128), x1[:], start=True, stop=True).then_inc(s.ssm_bx, 1)
            pe.wait_ge(s.ssm_wc, 1)
            pe.wait_ge(s.ssm_q, 1)
            pe.wait_ge(s.ssm_q2, 1)
            for i, (a, b) in enumerate(HALF_F):
                mm(ps[0:D, 1 + i, 0:b - a], wcs[:, 0, :], vq[:, 0, a:b], start=True, stop=False)
                mm(ps[0:D, 1 + i, 0:b - a], wcs[:, 1, :], vq[:, 1, a:b], start=False, stop=True).then_inc(s.ssm_y, 1)
            pe.wait_ge(s.in_keys, 16)
            pe.wait_ge(s.silu_out, 1)
            for q in range(4):
                if q == 2:
                    pe.wait_ge(s.res_flat, 2)
                for g in range(4):
                    last = mm(ps[0:D, 4 * (q % 2) + q // 2, g * NK:(g + 1) * NK], pkw_sb[DK * q:DK * q + DK, 0, g],
                              pkw_sb[DK * q:DK * q + DK, 1, g], start=True, stop=True)
                last.then_inc(s.pk_m, 1)
            pe.wait_ge(s.pk_mc, 4)
            ln_pe("lnf", res, s.res_flat, [1, 2], HALF_F, (3, 5))

            def scores(u, n, rows):
                pe.wait_ge(s.xst_ready, n + 1)
                pe.wait_ge(s.sims_ready, 2 * n)
                for k in range(2):
                    last = mm(ps[0:rows, k, :], xst[:, u, 0:rows], m_sb[:, 512 * k:512 * k + 512], start=True, stop=True)
                last.then_inc(s.sim_done, 1)

            def turn(u, n, rows):
                pe.wait_ge(s.s1p_ready, n + 2)
                pe.wait_ge(s.tr1_read, n + 1)
                for f in range(2 * H):
                    last = nc.tensor.transpose(ps[0:3 * JH, 6 + f // 8, :].bitcast(BF16)[:, (f % 8) * 128:(f % 8) * 128 + rows],
                                               s1p[0:rows, u, f].rearrange("p a k -> p (a k)"), identb[0:rows, 0:rows])
                last.then_inc(s.tr1_done, 1)
                pe.wait_ge(s.s0p_ready, n + 1)
                pe.wait_ge(s.s0q_ready, n + 1)
                pe.wait_ge(s.tr0_read, n + 1)
                for h in range(H):
                    last = nc.tensor.transpose(ps[:, 2 + h // 4, (h % 4) * 128:(h % 4) * 128 + rows],
                                               s0p[0:rows, u, h].rearrange("p a k -> p (a k)"),
                                               ident[0:rows, 0:rows])
                last.then_inc(s.tr0_done, 1)
                pe.wait_ge(s.zinv_ready, n + 1)
                pe.wait_ge(s.trz_read, n + 1)
                for h in range(H):
                    last = mm(ps[:, 4 + h // 4, (h % 4) * 128:(h % 4) * 128 + rows],
                              zinv[0:rows, u, h:h + 1].broadcast_to([rows, 128]), ident[0:rows, 0:rows],
                              start=True, stop=True)
                last.then_inc(s.trz_done, 1)

            pe.wait_ge(s.identb_ready, 1)
            for read in (s.tr0_read, s.tr1_read, s.trz_read):
                pe.sem_inc(read, 1)
            scores(0, 0, TILE)
            with pe.Fori(0, NTILE // 2 - 1) as i:
                for u in range(2):
                    scores(1 - u, 2 * i + u + 1, TILE)
                    turn(u, 2 * i + u, TILE)
            scores(1, NTILE - 1, TILE)
            turn(0, NTILE - 2, TILE)
            scores(0, NTILE, 1)
            turn(1, NTILE - 1, TILE)
            turn(0, NTILE, 1)

            pe.wait_ge(s.sel_ready, 1)
            pe.wait_ge(s.even_ready, 1)
            pe.wait_ge(s.trz_read, NTILE + 2)

            def spread(h, c, free):
                if free:
                    pe.wait_ge(s.d_ready, h * 2 * CH + c - 1)
                for a in range(2):
                    last = mm(ps[:, 2 * (c % 2) + a, 0:WH], sel_sb[:, c % CH],
                              s1t[:, bass.ds(2 * h + c // CH, 1), a * WH:(a + 1) * WH], start=True, stop=True)
                last.then_inc(s.b_ready, 1)

            def gather(h, c):
                if c == 0:
                    pe.wait_ge(s.acc_read, h + 1)
                if c % GRP == 0:
                    pe.wait_ge(tab_in[c // GRP], 16 * (h + 1))
                pe.wait_ge(s.w_ready, h * 2 * CH + c + 1)
                for a in range(2):
                    last = mm(ps[:, 4 + a, 0:WH], tab_sb[:, c // GRP, c % GRP], w_sb[:, c % NW, a * WH:(a + 1) * WH],
                              start=(c == 0), stop=(c == 2 * CH - 1))
                last.then_inc(s.w_used, 1)

            n1 = T - TILE

            def queries(h, a):
                if a == 0:
                    pe.wait_ge(s.wst_ready, h + 1)
                    settle(pe)
                lo, hi = HALF_T[a]
                mm(ps[0:D, 6, 0:2 * T], wst[0:D], x2t[:, lo:hi], start=True, stop=True).then_inc(s.q_done, 1)

            def key_scores(h, a):
                pe.wait_ge(s.q_ready, 2 * h + a + 1)
                pe.wait_ge(s.res_att, 2 * h + a + 1)
                if a == 0:
                    pe.wait_ge(s.kvh_ready, h + 1)
                for b in range(2):
                    mm(ps[:, 6, b * TILE:(b + 1) * TILE], q_sb[:, 2 * a + b, 0:TILE], kvh[0:D, 2 * a + b, 0:TILE],
                       start=True, stop=True)
                for b in range(2):
                    last = mm(ps[0:n1, 7, b * T:(b + 1) * T], q_sb[:, 2 * a + b, TILE:T], kvh[0:D, 2 * a + b],
                              start=True, stop=True)
                last.then_inc(s.qk_done, 1)

            def values(h, a):
                pe.wait_ge(s.sc_ready, 2 * h + a + 1)
                for b in range(2):
                    mm(ps[:, 6, b * D:(b + 1) * D], kvh[D:128, 2 * a + b, 0:TILE], wst[D:128], start=True, stop=True)
                for b in range(2):
                    at = 2 * D + b * D
                    last = mm(ps[0:n1, 6, at:at + D], kvh[D:128, 2 * a + b, TILE:T], wst[D:128], start=True, stop=True)
                last.then_inc(s.vw_done, 1)

            def turn_probs(h, a):
                pe.wait_ge(s.vw_ready, 2 * h + a + 1)
                pe.wait_ge(s.p_ready, 2 * h + a + 1)
                for b in range(2):
                    at = 2 * TILE + b * n1
                    nc.tensor.transpose(ps[:, 6, b * TILE:(b + 1) * TILE], a0[:, 2 * a + b], ident)
                    nc.tensor.transpose(ps[:, 6, at:at + n1], a1[:, 2 * a + b, 0:TILE], ident[0:n1, 0:n1])
                    last = nc.tensor.transpose(ps[0:n1, 7, b * n1:(b + 1) * n1], a1[:, 2 * a + b, TILE:T], ident[0:n1, 0:n1])
                last.then_inc(s.pt_done, 1)

            def output(h, a):
                pe.wait_ge(s.pt_ready, 2 * h + a + 1)
                settle(pe)
                for b in range(2):
                    y = ps[0:D, 7, b * T:(b + 1) * T]
                    mm(y[:, 0:TILE], vw0[:, 2 * a + b], pt0[:, 2 * a + b], start=True, stop=True)
                    mm(y[:, TILE:T], vw0[:, 2 * a + b], pt1[:, 2 * a + b], start=True, stop=False)
                    last = mm(y[:, TILE:T], vw1[:, 2 * a + b], pt2[:, 2 * a + b], start=False, stop=True)
                last.then_inc(s.pv_done, 1)

            def attend(h, c):
                for at, step in ((Q_AT, queries), (QK_AT, key_scores), (VW_AT, values), (PT_AT, turn_probs), (Y_AT, output)):
                    if c % HALF_CH == at:
                        step(h, c // HALF_CH)

            def pe_head(h, before, last):
                for c in range(2 * CH):
                    if c < 2 * CH - 3:
                        spread(h, c + 3, True)
                    elif not last:
                        spread(h + 1, c - (2 * CH - 3), True)
                    gather(h, c)
                    if before is not None:
                        attend(before, c)

            pe.wait_ge(s.timed_ready, 2)
            pe.sem_inc(s.acc_read, 1)
            pe.sem_inc(s.res_att, 1)
            pe.sem_inc(s.vw_done, 1)
            spread(0, 0, False)
            spread(0, 1, False)
            spread(0, 2, True)
            pe_head(0, None, False)
            with pe.Fori(0, H - 2) as i:
                pe_head(i + 1, i, False)
            pe_head(H - 1, H - 2, True)
            for c in range(2 * CH):
                attend(H - 1, c)

            ln_pe("lna", rest, s.res_att, [2 * H, 2 * H + 1], HALF_T, (2, 4))
            pe.wait_ge(s.fir_w, 1)
            for a in range(2):
                pe.wait_ge(s.fir_in, a + 1)
                pe.wait_ge(s.fir_pad, a + 1)
                for k in range(PAIRS):
                    last = mm(ps[0:D, a, 0:2 * T], firw[:, k], xpad[:, 2 * a:2 * a + 2, TAPS - 2 * k:TAPS - 2 * k + T],
                              start=(k == 0), stop=(k == PAIRS - 1))
                last.then_inc(s.fir_done, 1)
                if a == 0:
                    pe.wait_ge(s.fir_tot, 1)
                    mm(ps[0:D, 6, 0:NB], col("W2", D), tot[:, 1], start=True, stop=True).then_inc(s.fir_tb, 1)

            ln_pe("lnm", rest, s.res_fir, [2, 4], HALF_T, (2, 4))
            pe.wait_ge(s.in_moe_w, 16)
            pe.wait_ge(ln.out, LN_BASE["lnm"] + 2)

            def layer1(p):
                if p:
                    pe.wait_ge(s.moe_a1, p)
                for a, (lo, hi) in enumerate(HALF_T):
                    last = mm(ps[:, a, 0:2 * T], w1m[:, p * 128:(p + 1) * 128], xl[:, lo:hi], start=True, stop=True)
                last.then_inc(s.moe_h1, 1)

            layer1(0)
            pe.wait_ge(s.moe_feat, 1)
            for f, rows in ((0, TILE), (1, T - TILE)):
                lo = f * TILE
                mm(ps[0:rows, 6, f * E_:(f + 1) * E_], feat[:, lo:lo + rows], col("Wr", E_), start=True, stop=False)
                last = mm(ps[0:rows, 6, f * E_:(f + 1) * E_], four[:, 0:rows], brm, start=False, stop=True)
            last.then_inc(s.moe_log, 1)
            for p in range(EP):
                pe.wait_ge(s.moe_a1, p + 1)
                if p:
                    pe.wait_ge(s.moe_a2, p)
                for a in range(2):
                    last = mm(ps[:, 2 + a, 0:2 * T], w2m[:, p], h1[:, p % 2, 2 * a:2 * a + 2], start=True, stop=True)
                last.then_inc(s.moe_h2, 1)
                if p < EP - 1:
                    layer1(p + 1)
                if p == 0:
                    pe.wait_ge(s.moe_gate, 2)
                    for f, rows in ((0, TILE), (1, T - TILE)):
                        last = nc.tensor.transpose(ps[0:E_, 7, f * TILE:f * TILE + rows], lg[0:rows, 2, f], ident[0:rows, 0:rows])
                    last.then_inc(s.moe_gt, 1)
                    pe.wait_ge(s.moe_gts, 1)
                    for q in range(EP):
                        last = mm(ps[:, 6 + q // 2, (q % 2) * T:(q % 2 + 1) * T], e8m[:, q], gt[:], start=True, stop=True)
                    last.then_inc(s.moe_gb, 1)
                    for a in range(2):
                        mm(ps[0:D, 4 + a, 0:2 * T], bom, gt[:].unsqueeze(1).broadcast_to([E_, 2, T]), start=True, stop=False)
                pe.wait_ge(s.moe_w2g, p + 1)
                for a in range(2):
                    last = mm(ps[0:D, 4 + a, 0:2 * T], wom[:, p, 0:D], h2[:, p % 2, 2 * a:2 * a + 2],
                              start=False, stop=(p == EP - 1))
                last.then_inc(s.moe_y, 1)


def layouts(inp):
    import numpy as np
    f = {k: np.asarray(v) for k, v in inp.items()}
    a = {}
    x = f["x"].reshape(NB, 3, 8, 8, 8, 8)
    a["xT"] = x.transpose(3, 5, 1, 0, 2, 4).reshape(2, PC, TOK).transpose(1, 0, 2)
    two = lambda v: v.reshape(2, PC, -1).transpose(1, 0, 2).reshape(PC, -1)
    a["tokp"] = np.concatenate([two(f["L0_tok_ln1_g"]), two(f["L0_tok_ln1_b"]), two(f["L0_tok_W1"])], axis=1)
    c1 = lambda v: v.reshape(D, 1)
    BT = f["L0_attn_B"].T
    a["p64"] = np.concatenate(
        [c1(f[k]) for k in ("L0_tok_b1", "L0_tok_ln2_g", "L0_tok_ln2_b", "L0_tok_bp1", "L0_tok_lnp_g",
                            "L0_tok_lnp_b", "L0_tok_bp2", "cls_tok", "L1_attn_bias")]
        + [c1(f["L1_attn_memory_weights"][0]), f["L0_tok_Wp1"], f["L0_tok_Wp2"], BT, BT,
           f["L1_attn_W1"], f["L1_attn_W2"], f["L1_ffn_Wr"]], axis=1)
    d2 = lambda v: np.concatenate([v, v]).reshape(128, 1)
    Cr, Ci = f["L0_attn_C_real"].T, f["L0_attn_C_imag"].T
    a["p128"] = np.concatenate([d2(f["L0_attn_log_lambda_real"]), d2(f["L0_attn_lambda_imag"]), d2(f["L0_attn_log_dt"]),
                                np.concatenate([Cr, Ci]), np.concatenate([Ci, Cr])], axis=1)
    const = np.zeros((128, CC["end"]), np.float32)
    const[:, :128] = np.eye(128)
    i, j = np.arange(TILE)[:, None], np.arange(T)[None, :]
    const[:, CC["m0"]:CC["m0"] + TILE] = np.where(j[:, :TILE] <= i, 0.0, NEG)
    const[:T - TILE, CC["m1"]:CC["m1"] + T] = np.where(j <= TILE + i[:T - TILE], 0.0, NEG)
    a["const"] = const
    sel = np.zeros((3, JH, CH, 2, NK), np.float32)
    for n in range(JH):
        sel[:, n, n // 2, n % 2, :] = 1.0
    a["sel"] = sel.reshape(3 * JH, CH, 128)
    wq = f["L0_ffn_Wq_pk"].T.reshape(4, 4, DK, D).transpose(1, 2, 0, 3)
    kk = f["L0_ffn_pk_keys"].transpose(0, 2, 3, 1).reshape(4, 4, DK, NK).transpose(1, 2, 0, 3)
    a["pkw"] = np.stack([wq.reshape(128, 4, D), kk.reshape(128, 4, NK)], axis=1)
    tab = np.concatenate([f["L0_ffn_keys_table"], f["L0_ffn_values_table"]], axis=1)
    a["table"] = tab.reshape(H * 8, GRP, 128, 128).transpose(0, 2, 1, 3)
    a["wqo"] = np.concatenate([f["L0_ffn_Wq"].reshape(D, H, D).transpose(1, 0, 2), f["L0_ffn_Wo"].reshape(H, D, D)],
                              axis=1).transpose(1, 0, 2)
    mw = np.zeros((2 * PAIRS, D), np.float32)
    mw[:TAPS + 1] = f["L1_attn_memory_weights"]
    both = lambda v: np.concatenate([v, v])
    a["fir"] = np.concatenate([mw.reshape(PAIRS, 2, D).transpose(1, 2, 0).reshape(128, PAIRS), d2(f["L1_attn_memory_weights"][0]),
                               both(f["L1_attn_W2"]), both(f["L1_attn_W1"])], axis=1)
    prm = np.stack([f["L1_ffn_" + k] for k in ("b1", "g1", "be1", "m1", "v1", "b2", "g2", "be2", "m2", "v2")])
    a["moe"] = prm.reshape(MOE_P, 4, 128).transpose(2, 1, 0)
    e8 = np.zeros((E_, 4, 2, D), np.float32)
    for e in range(E_):
        e8[e, e // 2, e % 2] = 1.0
    w = np.zeros((5, 128, E_ * D), np.float32)
    w[0, :D] = f["L1_ffn_W1"].transpose(1, 0, 2).reshape(D, E_ * D)
    w2 = f["L1_ffn_W2"].reshape(4, 2, D, D)
    for q in range(2):
        w[1].reshape(128, 4, 128)[q * D:(q + 1) * D, :, q * D:(q + 1) * D] = w2[:, q].transpose(1, 0, 2)
    w[2].reshape(128, 4, 128)[:, :, :D] = f["L1_ffn_Wo"].reshape(4, 128, D).transpose(1, 0, 2)
    w[3, :E_, :D] = f["L1_ffn_bo"]
    w[3, 0, D:D + E_] = f["L1_ffn_br"]
    w[4, :E_] = e8.reshape(E_, 512)
    a["moe_w"] = w.transpose(1, 0, 2)
    return {k: np.ascontiguousarray(v) for k, v in a.items()}


def kernel(**inputs):
    import numpy as _np
    import concourse.bacc as _bacc
    from concourse import mybir as _mybir
    from concourse.bass_utils import run_bass_kernel_spmd as _run

    nc = _bacc.Bacc("TRN2", target_bir_lowering=False, num_devices=1)
    arrays, args = {}, {}
    for name, a in layouts(inputs).items():
        arrays[f"in_{name}"] = a
        args[name] = nc.dram_tensor(f"in_{name}", a.shape, _mybir.dt.from_np(a.dtype), kind="ExternalInput").ap()
    out = nc.dram_tensor("out", (D, TIMED), F32, kind="ExternalOutput").ap()
    tower(nc, out=out, **args)
    r = _run(nc, [arrays], core_ids=[0])
    return _np.ascontiguousarray(r.results[0]["out"].T).reshape(NB, T, D)
```

```python
from collections import namedtuple
from contextlib import ExitStack

import concourse.bass as bass
from concourse import mybir

ALU = mybir.AluOpType
ACT = mybir.ActivationFunctionType
AX = mybir.AxisListType.X
F32 = mybir.dt.float32
BF16 = mybir.dt.bfloat16

NB = 4
D = 64
SEG = 64
REP = 3
T = 1 + REP * SEG
TOK = NB * SEG
FLAT = NB * (T - 1) + 1
CLS = FLAT - 1
TIMED = NB * T
HALF_F = [(0, 2 * (T - 1)), (2 * (T - 1), FLAT)]
HALF_T = [(0, 2 * T), (2 * T, TIMED)]
PATCH = 192
PC = PATCH // 2
EPS = 1e-5
TOP_LINKS = 10
BN_EPS = 1e-3

H = 8
NK = 64
TOPK = 16
DK = 32
GUARD = 104.0
SHIFT = 32.0
SLACK = float(2 ** -22)
NEG = -3.0e38
STAIR = [TOPK // (a + 1) for a in range(TOPK)]
NCAND = sum(STAIR)
WIDE = FLAT + FLAT % 2
WH = WIDE // 2
TILE = 128
NTILE = (FLAT - 1) // TILE
JH = 32
CH = 16
GRP = 4

NTG = 2 * CH // GRP
ND, NE, NW = 4, 2, 4

TAIL_BANK = 6, 0
MEAN_K, VAR_K = 5, 9
POOL_EVERY = 4
PCH = 2 * CH // POOL_EVERY
VCH = 2 * CH - PCH
AHEAD = 4
EVAC_AT = 2
HALF_CH = CH
Q_AT, QK_AT, VW_AT, PT_AT, Y_AT = 0, 3, 7, 11, 13
QS_AT, EXP_AT, VS_AT, PTS_AT = 2, 8, 10, 13
KV_AT, MASK_AT, NORM_AT, RES_AT = 2, 5, 10, 15

TAPS = 40
PAIRS = (TAPS + 2) // 2
FARS = PAIRS // 2
NEARS = PAIRS - FARS
FAR = 2 * NEARS
E_ = 8
EP = E_ // 2

C64 = dict(tok_b1=0, ln2_g=1, ln2_b=2, bp1=3, lnp_g=4, lnp_b=5, bp2=6, cls=7, l1_bias=8, m0=9,
           Wp1=10, Wp2=74, BT2=138, W1=266, W2=330, Wr=394, end=402)
C128 = dict(lr=0, li=1, ldt=2, CriT=3, CirT=67, end=131)
CC = dict(ident=0, m0=TILE, m1=2 * TILE, end=2 * TILE + T)
MOE_P = 10
SEMS = """
in_x in_tokp in_p64 in_p128 in_const in_sel in_keys in_wqo in_moe in_moe_w in_fir
ones_ready pool_chain dve_chain top_chain first_done
tok_mean tok_xc tok_sq tok_var tok_std tok_xn tok_z tok_zb tok_h tok_hb silu_e silu_out tok_o tok_ready cls_ready
ssm_exp ssm_n2 ssm_rn ssm_r2 ssm_r ssm_r0 ssm_rinv ssm_ri2 ssm_phase ssm_wc ssm_bx ssm_g ssm_q ssm_q2 ssm_y res_flat
pk_m pk_mc identb_ready sel_ready xst_ready sim_done sims_ready cut_e cut_es z_sum s0p_ready zinv_ready
s1h s1r s1m s1p_ready settled tr0_done tr0_read trz_done trz_read tr1_done tr1_read even_ready
b_ready bs_ready dp_ready d_ready e_ready w_ready w_used acc0_done acc_read
tab0 tab1 tab2 tab3 tab4 tab5 tab6 tab7
timed_ready wst_ready kvh_ready q_done q_ready qk_done sc_ready nm_ready p_exp rec_ready p_ready pt_done pt_ready
vw_done vw_ready pv_done res_att
fir_w fir_pad fir_in fir_tot fir_tb fir_tbs fir_done res_fir
bn_sd bn_rec bn_ready
moe_feat moe_log moe_nm moe_le moe_gate moe_gt moe_gts moe_gb moe_gbs moe_h1 moe_a1 moe_h2 moe_a2 moe_w2g moe_y out_ready
out_done
""".split()


Semaphores = namedtuple("Semaphores", SEMS)
LN_SEMS = ("mean", "xc", "sq", "var", "std", "out")
LnSemaphores = namedtuple("LnSemaphores", LN_SEMS)


def tower(nc, xT, tokp, p64, p128, const, sel, pkw, table, wqo, fir, moe, moe_w, out):
    with ExitStack() as ctx:
        def sb(name, shape, dt=F32):
            return ctx.enter_context(nc.sbuf_tensor(name, shape, dt))

        ps = ctx.enter_context(nc.psum_tensor("ps", [128, 8, 512], F32))
        s = Semaphores(*[ctx.enter_context(nc.semaphore(n)) for n in SEMS])
        LN_BASE = dict(ln2=0, lnp=1, lns=2, lnf=3, lna=5, lnm=7)
        ln = LnSemaphores(*[ctx.enter_context(nc.semaphore("ln_" + n)) for n in LN_SEMS])

        kv = sb("kv", [128, H, WIDE])
        zbc = sb("zbc", [128, H, WIDE])
        rings = sb("rings", [128, (ND + NE + NW) * WIDE])
        taken = {}

        def part(region, shape, dt=F32, stage=0):
            flat = region.rearrange("p a b -> p (a b)") if region.ndim == 3 else region
            flat = flat if region.dtype == F32 else flat.bitcast(F32)
            n = 1
            for x in shape[1:]:
                n *= x
            words = n if dt == F32 else n // 2
            at = taken.get((region.name, stage), 0)
            taken[region.name, stage] = at + words
            assert at + words <= flat.shape[1]
            v = flat[0:shape[0], at:at + words]
            v = v if dt == F32 else v.bitcast(dt)
            names = "abcde"[:len(shape) - 1]
            if len(names) > 1:
                v = v.rearrange(f"p ({' '.join(names)}) -> p {' '.join(names)}",
                                **dict(zip(names[1:], shape[2:])))
            return v

        x_sb = part(zbc[:], [PC, 2, TOK])
        tokp_sb = sb("tokp_sb", [PC, 4 + 2 * D])
        p64_sb = sb("p64_sb", [D, C64["end"]])
        p128_sb = sb("p128_sb", [128, C128["end"]])
        const_sb = sb("const_sb", [128, CC["end"]])
        sel_sb = sb("sel_sb", [3 * JH, CH, 128], BF16)
        pkw_sb = part(zbc[:], [128, 2, 4, 64])
        fir_sb = sb("fir_sb", [128, PAIRS + 1 + 2 * D])
        moe_sb = sb("moe_sb", [128, 4, MOE_P])
        onesp = sb("onesp", [PC, PC])
        ones64 = sb("ones64", [D, D])
        four = sb("four", [1, 128])
        bn = sb("bn", [128, 4, EP, 2])
        sqrt_sb = sb("sqrt_sb", [128, 1])
        eps_sb = sb("eps_sb", [128, 3])

        def col(name, n=1):
            return p64_sb[:, C64[name]:C64[name] + n]

        def par(name, n=1):
            return p128_sb[:, C128[name]:C128[name] + n]

        ident = const_sb[:, CC["ident"]:CC["ident"] + 128]
        mask0 = const_sb[:, CC["m0"]:CC["m0"] + TILE]
        mask1 = const_sb[0:T - TILE, CC["m1"]:CC["m1"] + T]

        tk = part(kv[:], [PC, 4, 2, TOK])
        u_sb = part(zbc[:], [D, TOK + 1])
        lnw = part(zbc[:], [D, 3, TIMED])
        tz = part(kv[:], [D, 6, TOK])
        sp_ = sb("sp_", [128, 32])
        ph = sb("ph", [128, 2, T])
        pht = part(zbc[:], [128, 2, SEG * 2])
        pin = part(zbc[:], [128, T])
        pin2 = part(zbc[:], [128, T])
        wcs = sb("wcs", [128, 2, D])
        vq = part(kv[:], [128, 2, FLAT + 3])
        g_sb = part(kv[:], [128, NB, T])
        res = sb("res", [D, FLAT])
        x1 = part(zbc[:], [D, TOK + 1])
        x2 = sb("x2", [D, FLAT])

        m_sb = sb("m_sb", [D, 2 * H * NK])
        identb = sb("identb", [128, 128], BF16)
        xz = sb("xz", [D, 2 * H - 1])
        xst = sb("xst", [D, 2, TILE])
        sim = part(rings[:], [128, 2, 2 * H, NK])
        rest_sims = part(kv[:], [128, 2 * H, NK], stage=1)
        top = part(rings[:], [128, 2 * H, TOPK])
        cand = part(kv[:], [128, 2, H, NCAND], stage=1)
        best = sb("best", [128, H, TOPK])
        zsum = sb("zsum", [128, H])
        cut = sb("cut", [128, 3, H])
        ez = sb("ez", [128, 2, H, TOPK])
        zinv = sb("zinv", [128, 2, H])
        s0p = part(rings[:], [128, 2, H, 2, NK])
        s1p = part(rings[:], [128, 2, 2 * H, 3, JH], BF16)
        s1r = part(rings[:], [128, 2 * H, JH])
        s0t = sb("s0t", [128, H, WIDE])
        s1t_all = sb("s1t", [128, 2 * H, WIDE], BF16)
        s1t = s1t_all[0:3 * JH]
        tab_sb = sb("tab_sb", [128, NTG, GRP, 128])
        ring = rings[:].rearrange("p (a n) -> p a n", n=WIDE)
        d_sb, e_sb, w_sb = ring[:, 0:ND], ring[:, ND:ND + NE], ring[:, ND + NE:ND + NE + NW]
        bs_sb = sb("bs_sb", [128, 2, WH])
        tab_in = [s.tab0, s.tab1, s.tab2, s.tab3, s.tab4, s.tab5, s.tab6, s.tab7]
        x2t = sb("x2t", [D, TIMED])
        rest = sb("rest", [D, TIMED])
        wqo_sb = sb("wqo_sb", [128, H, D])
        wst = sb("wst", [128, D])
        kvh = sb("kvh", [128, NB, T])
        q_sb = sb("q_sb", [D, NB, T])
        a0 = sb("a0", [TILE, NB, TILE])
        a1 = sb("a1", [T - TILE, NB, T])
        amax = sb("amax", [TILE, 2, NB])
        asum = sb("asum", [TILE, 2, NB])
        arec = sb("arec", [TILE, 2, NB])
        pt0 = sb("pt0", [TILE, NB, TILE])
        pt1 = sb("pt1", [TILE, NB, T - TILE])
        pt2 = sb("pt2", [T - TILE, NB, T - TILE])
        vw0 = sb("vw0", [TILE, NB, D])
        vw1 = sb("vw1", [T - TILE, NB, D])

        def settle(eng):
            eng.sem_inc(s.settled, 1)

        def pool_adds(c):
            return c % POOL_EVERY == POOL_EVERY - 1

        def spread_at(p):
            r = p % POOL_EVERY
            return p - r + (POOL_EVERY - 1 if r == 0 else r - 1)

        def nth(h, c):
            return h * PCH + c // POOL_EVERY + 1 if pool_adds(c) else h * VCH + c - c // POOL_EVERY + 1

        sel_in = part(rings[:], [3 * JH, CH, 128], stage=1)

        moew = part(s0t[:], [128, 5, E_ * D])
        xpad = part(s0t[:], [128, NB, FAR + T])
        firw = part(s0t[:], [128, NEARS, 2, D])
        firm = part(s0t[:], [128, PAIRS])
        xl = part(s1t_all[:], [D, TIMED])
        h1 = part(s1t_all[:], [128, 2, NB, T])
        h2 = part(s1t_all[:], [128, 2, NB, T])
        gb = part(s1t_all[:], [128, EP, T])
        tot = sb("tot", [D, 3, NB])
        feat = sb("feat", [D, T])
        lg = sb("lg", [TILE, 3, 2, E_])
        lsum = sb("lsum", [TILE, 3, 2])
        gt = sb("gt", [E_, T])
        w1m, w2m, wom = moew[0:D, 0], moew[:, 1].rearrange("p (a k) -> p a k", a=EP), moew[:, 2].rearrange("p (a k) -> p a k", a=EP)
        bom, brm, e8m = moew[0:E_, 3, 0:D], moew[0:1, 3, D:D + E_], moew[0:E_, 4].rearrange("p (a k) -> p a k", a=EP)

        pe = act = dve = None
        nlink = [0]

        def link(ins):
            nlink[0] += 1
            ins.then_inc(s.dve_chain, 1)
            dve.wait_ge(s.dve_chain, nlink[0])

        def ln_mean(src, ready, need, parts, banks, i):
            a, b = parts[i]
            pe.wait_ge(ready, need[i])
            nc.tensor.matmul(ps[0:D, banks[0] + i, 0:b - a], ones64[:], src[:, a:b],
                             start=True, stop=True).then_inc(ln.mean, 1)

        def ln_var(k, parts, banks, i):
            a, b = parts[i]
            pe.wait_ge(ln.sq, LN_BASE[k] + i + 1)
            nc.tensor.matmul(ps[0:D, banks[1] + i, 0:b - a], ones64[:], lnw[:, 1, a:b],
                             start=True, stop=True).then_inc(ln.var, 1)

        def ln_pe(k, src, ready, need, parts, banks):
            for i in range(len(parts)):
                ln_mean(src, ready, need, parts, banks, i)
            for i in range(len(parts)):
                ln_var(k, parts, banks, i)

        def ln_act(k, parts, banks, apart=False):
            steps = [(step, i) for i in range(len(parts)) for step in range(2)]
            for step, i in steps if apart else sorted(steps):
                a, b = parts[i]
                if step == 0:
                    act.wait_ge(ln.xc, LN_BASE[k] + i + 1)
                    nc.scalar.activation(lnw[:, 1, a:b], lnw[:, 0, a:b], ACT.Square).then_inc(ln.sq, 1)
                else:
                    act.wait_ge(ln.var, LN_BASE[k] + i + 1)
                    nc.scalar.activation(lnw[:, 2, a:b], ps[0:D, banks[1] + i, 0:b - a], ACT.Sqrt,
                                         bias=eps_sb[0:D, 0:1]).then_inc(ln.std, 1)

        def ln_centre(k, src, parts, banks, i):
            a, b = parts[i]
            dve.wait_ge(ln.mean, LN_BASE[k] + i + 1)
            nc.vector.tensor_tensor(lnw[:, 0, a:b], src[:, a:b], ps[0:D, banks[0] + i, 0:b - a],
                                    ALU.subtract).then_inc(ln.xc, 1)

        def ln_scale(k, dst, parts, i, affine=None):
            a, b = parts[i]
            dve.wait_ge(ln.std, LN_BASE[k] + i + 1)
            link(nc.vector.reciprocal(lnw[:, 2, a:b], lnw[:, 2, a:b]))
            last = nc.vector.tensor_tensor(dst[:, a:b], lnw[:, 0, a:b], lnw[:, 2, a:b], ALU.mult)
            if affine:
                link(last)
                last = nc.vector.tensor_scalar(dst[:, a:b], dst[:, a:b], affine[0], affine[1],
                                               ALU.mult, ALU.add)
            last.then_inc(ln.out, 1)

        def ln_dve(k, src, dst, parts, banks, affine=None, between=None, after=None):
            for i in range(len(parts)):
                ln_centre(k, src, parts, banks, i)
            if between:
                between()
            for i in range(len(parts)):
                ln_scale(k, dst, parts, i, affine)
                if after:
                    after(i)

        block = ctx.enter_context(nc.Block())

        @block.sync
        def _(sp):
            for dst, src, done in (
                (x_sb[:], xT, s.in_x), (tokp_sb[:], tokp, s.in_tokp), (p64_sb[:], p64, s.in_p64),
                (p128_sb[:], p128, s.in_p128), (const_sb[:], const, s.in_const), (pkw_sb[:], pkw, s.in_keys),
                (sel_in, sel, s.in_sel), (wqo_sb[:], wqo, s.in_wqo),
                (moe_sb[:], moe, s.in_moe), (fir_sb[:], fir, s.in_fir),
            ):
                sp.dma_start(dst, src).then_inc(done, 16)
            for g in range(NTG):
                sp.dma_start(tab_sb[:, g], table[g]).then_inc(tab_in[g], 16)
            with sp.Fori(0, H - 1) as h:
                for g in range(NTG):
                    sp.wait_ge(s.w_used, NW + h * 2 * CH + (g + 1) * GRP)
                    sp.dma_start(tab_sb[:, g], table[bass.ds((h + 1) * NTG + g, 1)]
                                 .rearrange("o p c k -> (o p) c k")).then_inc(tab_in[g], 16)
            sp.wait_ge(s.w_used, NW + H * 2 * CH)
            sp.dma_start(moew, moe_w).then_inc(s.in_moe_w, 16)
            for a, (lo, hi) in enumerate(HALF_T):
                sp.wait_ge(s.out_ready, a + 1)
                sp.dma_start(out[:, lo:hi], rest[:, lo:hi]).then_inc(s.out_done, 16)
            sp.wait_ge(s.out_done, 32)

        @block.gpsimd
        def _(pool):
            n = [0]

            def pl(ins):
                n[0] += 1
                ins.then_inc(s.pool_chain, 1)
                pool.wait_ge(s.pool_chain, n[0])

            nc.gpsimd.memset(xz[:], 0.0)
            nc.gpsimd.memset(onesp[:], 1.0 / PATCH)
            nc.gpsimd.memset(ones64[:], 1.0 / D)
            nc.gpsimd.memset(four[:], float(NB))
            nc.gpsimd.memset(eps_sb[:, 2:3], -SHIFT)
            nc.gpsimd.memset(eps_sb[:, 1:2], BN_EPS)
            nc.gpsimd.memset(eps_sb[:, 0:1], EPS).then_inc(s.ones_ready, 1)

            EL, DT, AR, AI, OM, AI2, AR2, N2, RN, T1, ARE, AIM, R2, R, RI, C1, S1, BRE, BIM, P2 = range(20)

            def c(k):
                return sp_[:, k:k + 1]

            tt, ts, stt = nc.gpsimd.tensor_tensor, nc.gpsimd.tensor_scalar, nc.gpsimd.scalar_tensor_tensor
            pool.wait_ge(s.in_p128, 16)
            pool.wait_ge(s.ssm_exp, 2)
            pl(ts(c(DT), c(DT), 0.005, 0.1, ALU.max, ALU.min))
            pl(tt(c(AR), c(DT), c(EL), ALU.mult))
            pl(ts(c(AR), c(AR), -0.5, None, ALU.mult))
            pl(tt(c(AI), c(DT), par("li"), ALU.mult))
            pl(ts(c(AI), c(AI), 0.5, None, ALU.mult))
            pl(ts(c(OM), c(AR), -1.0, 1.0, ALU.mult, ALU.add))
            pl(tt(c(AI2), c(AI), c(AI), ALU.mult))
            pl(tt(c(AR2), c(AR), c(AR), ALU.mult))
            pl(tt(c(N2), c(OM), c(OM), ALU.mult))
            tt(c(N2), c(N2), c(AI2), ALU.add).then_inc(s.ssm_n2, 1)
            pl(tt(c(T1), c(AR2), c(AI2), ALU.add))
            pl(ts(c(T1), c(T1), -1.0, 1.0, ALU.mult, ALU.add))
            pl(tt(c(BRE), c(DT), c(OM), ALU.mult))
            pl(tt(c(BIM), c(DT), c(AI), ALU.mult))
            pool.wait_ge(s.ssm_rn, 1)
            pl(tt(c(ARE), c(T1), c(RN), ALU.mult))
            pl(tt(c(AIM), c(AI), c(RN), ALU.mult))
            pl(ts(c(AIM), c(AIM), 2.0, None, ALU.mult))
            pl(tt(c(BRE), c(BRE), c(RN), ALU.mult))
            pl(tt(c(BIM), c(BIM), c(RN), ALU.mult))
            pl(tt(c(R2), c(ARE), c(ARE), ALU.mult))
            pl(tt(c(T1), c(AIM), c(AIM), ALU.mult))
            tt(c(R2), c(R2), c(T1), ALU.add).then_inc(s.ssm_r2, 1)
            pool.wait_ge(s.ssm_rinv, 1)
            pl(tt(c(T1), c(R2), c(RI), ALU.mult))
            pl(tt(c(R), c(R), c(T1), ALU.add))
            ts(c(R), c(R), 0.5, None, ALU.mult).then_inc(s.ssm_r, 1)
            pool.wait_ge(s.ssm_ri2, 1)
            pl(nc.gpsimd.memset(ph[:, 0, 0:1], 1.0))
            pl(nc.gpsimd.memset(ph[:, 1, 0:1], 0.0))
            pl(tt(ph[:, 0, 1:2], c(ARE), c(RI), ALU.mult))
            pl(tt(ph[:, 1, 1:2], c(AIM), c(RI), ALU.mult))
            m = 1
            while m < T - 1:
                w = min(m, T - 1 - m)
                cm, sm = ph[:, 0, m:m + 1], ph[:, 1, m:m + 1]
                cs, ss = ph[:, 0, 1:1 + w], ph[:, 1, 1:1 + w]
                ts(pht[:, 0, 0:w], ss, sm, None, ALU.mult)
                pl(ts(pht[:, 1, 0:w], ss, cm, None, ALU.mult))
                ts(ph[:, 0, m + 1:m + 1 + w], cs, cm, None, ALU.mult)
                pl(ts(ph[:, 1, m + 1:m + 1 + w], cs, sm, None, ALU.mult))
                tt(ph[:, 0, m + 1:m + 1 + w], ph[:, 0, m + 1:m + 1 + w], pht[:, 0, 0:w], ALU.subtract)
                pl(tt(ph[:, 1, m + 1:m + 1 + w], ph[:, 1, m + 1:m + 1 + w], pht[:, 1, 0:w], ALU.add))
                m += w
            for lo, a, b, neg in ((0, BRE, BIM, False), (D, BIM, BRE, True)):
                q = slice(lo, lo + D)
                pl(ts(pin[q, :], ph[q, 0, :], sp_[q, a:a + 1], None, ALU.mult))
                pl(ts(pin2[q, :], ph[q, 1, :], sp_[q, b:b + 1], None, ALU.mult))
                last = tt(pin[q, :], pin[q, :], pin2[q, :], ALU.subtract if neg else ALU.add)
                pl(last) if lo == 0 else last.then_inc(s.ssm_phase, 1)
            pool.wait_ge(s.ssm_phase, 1)
            pl(ts(wcs[0:D, 0, :], p128_sb[0:D, C128["CriT"]:C128["CriT"] + D], 1.0, None, ALU.mult))
            pl(ts(wcs[D:128, 0, :], p128_sb[D:128, C128["CriT"]:C128["CriT"] + D], -1.0, None, ALU.mult))
            ts(wcs[:, 1, :], par("CirT", D), -1.0, None, ALU.mult).then_inc(s.ssm_wc, 1)
            pool.wait_ge(s.ssm_g, NB)
            nc.gpsimd.memset(vq[:, 1, CLS:CLS + 1], 0.0)
            tt(vq[:, 1, 0:CLS].rearrange("p (b t) -> p b t", b=NB), g_sb[:, :, 1:T],
               ph[:, 1, 1:T].unsqueeze(1).broadcast_to([128, NB, T - 1]), ALU.mult).then_inc(s.ssm_q2, 1)
            nc.gpsimd.memset(s0t[:, :, FLAT:WIDE], -1.0)
            nc.gpsimd.memset(s1t[:, :, FLAT:WIDE], 0.0).then_inc(s.even_ready, 1)

            def pieces(u, n, rows, nh=H):
                pool.wait_ge(s.s1h, n + 1)
                pool.wait_ge(s.s1p_ready, n + 1)
                tt(s1r[0:rows, 0:2 * nh], sim[0:rows, u, nh:2 * nh].rearrange("p h (j k) -> p (h j) k", j=2),
                   s1p[0:rows, u, 0:2 * nh, 0], ALU.subtract).then_inc(s.s1r, 1)
                pool.wait_ge(s.s1m, n + 1)
                tt(s1p[0:rows, u, 0:2 * nh, 2], s1r[0:rows, 0:2 * nh], s1p[0:rows, u, 0:2 * nh, 1], ALU.subtract).then_inc(s.s1p_ready, 1)
                pool.wait_ge(s.cut_e, n + 1)
                shape = [rows, nh, 2, NK]
                tt(s0p[0:rows, u, 0:nh], sim[0:rows, u, 0:nh].unsqueeze(2).broadcast_to(shape),
                   cut[0:rows, 2, 0:nh].unsqueeze(2).unsqueeze(3).broadcast_to(shape), ALU.subtract).then_inc(s.s0p_ready, 1)

            pool.sem_inc(s.s1p_ready, 1)
            with pool.Fori(0, NTILE // 2) as i:
                for u in range(2):
                    pieces(u, 2 * i + u, TILE)
            pieces(0, NTILE, H, 1)
            def pool_add(h, c):
                pool.wait_ge(s.bs_ready, nth(h, c))
                pool.wait_ge(s.w_ready, h * 2 * CH + c - ND + 2)
                settle(pool)
                tt(d_sb[:, c % ND], bs_sb[:].rearrange("p a n -> p (a n)").unsqueeze(1), s0t[:, bass.ds(h, 1), :],
                   ALU.add).then_inc(s.dp_ready, 1)

            with pool.Fori(0, H) as h:
                for c in range(POOL_EVERY - 1, 2 * CH, POOL_EVERY):
                    pool_add(h, c)
            pool.wait_ge(s.bn_rec, 1)
            prm = moe_sb[:].rearrange("p a (l k) -> p a l k", l=2)
            pl(tt(bn[:, 0], prm[:, :, :, 1], bn[:, 0], ALU.mult))
            pl(tt(bn[:, 2], prm[:, :, :, 0], prm[:, :, :, 3], ALU.subtract))
            pl(tt(bn[:, 2], bn[:, 2], bn[:, 0], ALU.mult))
            tt(bn[:, 1], bn[:, 2], prm[:, :, :, 2], ALU.add).then_inc(s.bn_ready, 1)
            pool.wait_ge(s.in_fir, 16)
            pool.wait_ge(s.w_used, NW + H * 2 * CH)
            nc.gpsimd.memset(xpad[:, :, 0:FAR + 1], 0.0)
            pl(ts(firm, fir_sb[:, 0:PAIRS], fir_sb[:, PAIRS:PAIRS + 1], None, ALU.subtract))
            for side, (k0, n_) in enumerate(((0, NEARS), (NEARS, FARS))):
                pl(tt(firw[:, 0:n_, side], firm[:, k0:k0 + n_].unsqueeze(2).broadcast_to([128, n_, D]),
                      fir_sb[:, PAIRS + 1:PAIRS + 1 + D].unsqueeze(1).broadcast_to([128, n_, D]), ALU.mult))
            pl(nc.gpsimd.memset(firw[D:128, FARS - 1, 1], 0.0))
            pl(nc.gpsimd.memset(firw[:, FARS:NEARS, 1], 0.0))
            nc.gpsimd.tensor_copy(firw[0:D, 0, 0], fir_sb[0:D, PAIRS + 1 + D:PAIRS + 1 + 2 * D]).then_inc(s.fir_w, 1)

        @block.scalar
        def _(act_):
            nonlocal act
            act = act_
            def preload_sqrt():
                nc.scalar.activation(sqrt_sb[:], eps_sb[:, 0:1], ACT.Sqrt)

            act.wait_ge(s.ones_ready, 1)
            act.wait_ge(s.tok_xc, 1)
            nc.scalar.activation(tk[:, 1], tk[:, 0], ACT.Square).then_inc(s.tok_sq, 1)
            act.wait_ge(s.in_p128, 16)
            nc.scalar.activation(sp_[:, 0:1], par("lr"), ACT.Exp).then_inc(s.ssm_exp, 1)
            nc.scalar.activation(sp_[:, 1:2], par("ldt"), ACT.Exp).then_inc(s.ssm_exp, 1)
            act.wait_ge(s.tok_var, 1)
            nc.scalar.activation(tk[:, 2, 0], ps[0:PC, 1, 0:TOK], ACT.Sqrt, bias=eps_sb[0:PC, 0:1]).then_inc(s.tok_std, 1)
            act.wait_ge(s.in_p64, 16)
            act.wait_ge(s.tok_z, 1)
            nc.scalar.activation(tz[:, 0], ps[0:D, 2, 0:TOK], ACT.Identity, bias=col("tok_b1")).then_inc(s.tok_zb, 1)
            nc.scalar.copy(u_sb[:, TOK:TOK + 1], col("cls")).then_inc(s.cls_ready, 1)
            act.wait_ge(s.ssm_r2, 1)
            nc.scalar.activation(sp_[:, 13:14], sp_[:, 12:13], ACT.Sqrt).then_inc(s.ssm_r0, 1)
            ln_act("ln2", [(0, TOK)], (3, 4))
            act.wait_ge(s.tok_h, 1)
            nc.scalar.activation(tz[:, 2], ps[0:D, 5, 0:TOK], ACT.Identity, bias=col("bp1")).then_inc(s.tok_hb, 1)
            ln_act("lnp", [(0, TOK)], (6, 7))
            act.wait_ge(ln.out, LN_BASE["lnp"] + 1)
            nc.scalar.activation(tz[:, 4], tz[:, 3], ACT.Exp, scale=-1.0).then_inc(s.silu_e, 1)
            preload_sqrt()
            act.wait_ge(s.tok_o, 1)
            nc.scalar.activation(u_sb[:, 0:TOK], ps[0:D, 0, 0:TOK], ACT.Identity, bias=col("bp2")).then_inc(s.tok_ready, 1)
            ln_act("lns", [(0, TOK + 1)], (1, 2))
            act.wait_ge(s.in_sel, 16)
            nc.scalar.copy(sel_sb[:], sel_in).then_inc(s.sel_ready, 1)
            act.wait_ge(s.in_moe, 16)
            nc.scalar.activation(bn[:, 3], moe_sb[:].rearrange("p a (l k) -> p a l k", l=2)[:, :, :, 4], ACT.Sqrt,
                                 bias=eps_sb[:, 1:2]).then_inc(s.bn_sd, 1)
            act.wait_ge(s.in_const, 16)
            nc.scalar.copy(identb[:], ident).then_inc(s.identb_ready, 1)
            mv = m_sb[:].rearrange("p (g q k) -> p g q k", g=4, q=4)
            for q in range(4):
                act.wait_ge(s.pk_m, q + 1)
                nc.scalar.copy(mv[:, :, q], ps[0:D, 4 + q, 0:4 * NK].rearrange("p (g k) -> p g k", g=4)
                               ).then_inc(s.pk_mc, 1)

            ln_act("lnf", HALF_F, (3, 5))

            def stage_tile(u, lo, rows):
                nc.scalar.copy(xst[:, u, 0:rows], x2[:, lo]).then_inc(s.xst_ready, 1)

            def stage_class():
                nc.scalar.copy(xz[:, H - 1:H], x2[:, CLS:FLAT]).then_inc(s.xst_ready, 1)

            def scores_out(u, n, rows, nh=H):
                act.wait_ge(s.sim_done, n + 1)
                for k in range(2):
                    src = ps[0:rows, k, :] if nh == H else ps[0:rows, 0, k * NK:(k + 1) * NK]
                    nc.scalar.copy(sim[0:rows, u, nh * k:nh * k + nh], src.rearrange("p (h k) -> p h k", k=NK)
                                   ).then_inc(s.sims_ready, 1)
                act.wait_ge(s.sims_ready, 2 * n + 2)
                nc.scalar.copy(s1p[0:rows, u, 0:2 * nh, 0], sim[0:rows, u, nh:2 * nh].rearrange("p h (j k) -> p (h j) k", j=2)
                               ).then_inc(s.s1h, 1)

            def middle_out(u, n, rows, nh=H):
                act.wait_ge(s.s1r, n + 1)
                nc.scalar.copy(s1p[0:rows, u, 0:2 * nh, 1], s1r[0:rows, 0:2 * nh]).then_inc(s.s1m, 1)

            def best_exps(n, rows, nh=H):
                act.wait_ge(s.cut_e, n + 1)
                nc.scalar.activation(ez[0:rows, 1, 0:nh], ez[0:rows, 0, 0:nh], ACT.Exp, bias=eps_sb[0:rows, 2:3]).then_inc(s.cut_es, 1)

            def turned_out(n, lo, rows):
                act.wait_ge(s.tr0_done, n + 1)
                nc.scalar.copy(s0t[:, :, lo], ps[:, 2:4, :].rearrange("p a (h k) -> p (a h) k", h=4)[:, :, 0:rows]
                               ).then_inc(s.tr0_read, 1)
                act.wait_ge(s.tr1_done, n + 1)
                nc.scalar.copy(s1t[:, :, lo], ps[0:3 * JH, 6:8, :].bitcast(BF16).rearrange("p a (h k) -> p (a h) k", h=8)[:, :, 0:rows]
                               ).then_inc(s.tr1_read, 1)
                act.wait_ge(s.trz_done, n + 1)
                nc.scalar.copy(zbc[:, :, lo], ps[:, 4:6, :].rearrange("p a (h k) -> p (a h) k", h=4)[:, :, 0:rows]
                               ).then_inc(s.trz_read, 1)

            def class_turned_out(n):
                act.wait_ge(s.tr1_done, n + 1)
                nc.scalar.copy(s1t[:, :, CLS].rearrange("p (h j) -> p j h", j=2),
                               ps[0:3 * JH, 6, :].bitcast(BF16)[:, 0:256].rearrange("p (j h) -> p j h", j=2)[:, :, 0:H]
                               ).then_inc(s.tr1_read, 1)
                act.wait_ge(s.tr0_done, n + 1)
                nc.scalar.copy(s0t[:, :, CLS], ps[:, 2, 0:H]).then_inc(s.tr0_read, 1)
                act.wait_ge(s.trz_done, n + 1)
                nc.scalar.copy(zbc[:, :, CLS], ps[:, 4, 0:H]).then_inc(s.trz_read, 1)

            act.wait_ge(ln.out, LN_BASE["lnf"] + 1)
            for u in range(2):
                stage_tile(u, slice(u * TILE, (u + 1) * TILE), TILE)
            scores_out(0, 0, TILE)
            middle_out(0, 0, TILE)
            act.wait_ge(ln.out, LN_BASE["lnf"] + 2)
            with act.Fori(0, NTILE // 2 - 1) as i:
                for u in range(2):
                    n = 2 * i + u
                    scores_out(1 - u, n + 1, TILE)
                    stage_tile(u, bass.ds((n + 2) * TILE, TILE), TILE)
                    best_exps(n, TILE)
                    middle_out(1 - u, n + 1, TILE)
                    turned_out(n, bass.ds(n * TILE, TILE), TILE)
            n = NTILE - 2
            scores_out(1, n + 1, TILE)
            stage_class()
            best_exps(n, TILE)
            middle_out(1, n + 1, TILE)
            turned_out(n, slice(n * TILE, n * TILE + TILE), TILE)
            scores_out(0, NTILE, H, 1)
            best_exps(n + 1, TILE)
            middle_out(0, NTILE, H, 1)
            turned_out(n + 1, slice(n * TILE + TILE, CLS), TILE)
            best_exps(NTILE, H, 1)
            class_turned_out(NTILE)

            def head_weights(h):
                act.wait_ge(s.vw_done, 2 * h + 1)
                nc.scalar.copy(wst[:].unsqueeze(1), wqo_sb[:, bass.ds(h, 1), :]).then_inc(s.wst_ready, 1)

            def queries_out(h, a, q=6):
                act.wait_ge(s.q_done, 2 * h + a + 1)
                nc.scalar.mul(q_sb[:, 2 * a:2 * a + 2].rearrange("p b t -> p (b t)"), ps[0:D, q, 0:2 * T],
                              float(D) ** -0.5).then_inc(s.q_ready, 1)

            def values_out(h, a, q=6):
                act.wait_ge(s.vw_done, 2 * h + a + 2)
                nc.scalar.copy(vw0[:, 2 * a:2 * a + 2], ps[:, q, 0:2 * D].rearrange("p (b e) -> p b e", b=2))
                nc.scalar.copy(vw1[:, 2 * a:2 * a + 2],
                               ps[0:T - TILE, q, 2 * D:4 * D].rearrange("p (b e) -> p b e", b=2)
                               ).then_inc(s.vw_ready, 1)

            def prob_exps(h, a, q=6):
                act.wait_ge(s.nm_ready, 2 * h + a + 1)
                for b in range(2 * a, 2 * a + 2):
                    nc.scalar.activation(a0[:, b], a0[:, b], ACT.Exp, bias=amax[:, 0, b:b + 1],
                                         accum_out=asum[:, 0, b:b + 1])
                    last = nc.scalar.activation(a1[:, b], a1[:, b], ACT.Exp, bias=amax[0:T - TILE, 1, b:b + 1],
                                                accum_out=asum[0:T - TILE, 1, b:b + 1])
                last.then_inc(s.p_exp, 1)

            def probs_out(h, a, q=6):
                n1, b2 = T - TILE, slice(2 * a, 2 * a + 2)
                act.wait_ge(s.pt_done, 2 * h + a + 1)
                nc.scalar.copy(pt0[:, b2], ps[:, q, 0:2 * TILE].rearrange("p (b i) -> p b i", b=2))
                nc.scalar.copy(pt1[:, b2], ps[:, q, 2 * TILE:2 * T].rearrange("p (b i) -> p b i", b=2))
                nc.scalar.copy(pt2[:, b2], ps[0:n1, q + 1, 0:2 * n1].rearrange("p (b i) -> p b i", b=2)
                               ).then_inc(s.pt_ready, 1)

            def attend(h, c):
                a, k = c // HALF_CH, c % HALF_CH
                if c == 0:
                    head_weights(h)
                for at, step in ((QS_AT, queries_out), (EXP_AT, prob_exps), (VS_AT, values_out), (PTS_AT, probs_out)):
                    if k == at:
                        step(h, a)

            def sums_out(h):
                act.wait_ge(s.acc0_done, h + 1)
                nc.scalar.copy(kv[:, bass.ds(h, 1), 0:WH], ps[:, 4, 0:WH].unsqueeze(1)).then_inc(s.acc_read, 1)
                act.wait_ge(s.w_used, NW + (h + 1) * 2 * CH)
                nc.scalar.copy(kv[:, bass.ds(h, 1), WH:WIDE], ps[:, 5, 0:WH].unsqueeze(1)).then_inc(s.acc_read, 1)

            def pool_scores_out(h, p, later):
                act.wait_ge(s.b_ready, h * 2 * CH + p + 1)
                if later:
                    act.wait_ge(s.dp_ready, h * PCH + p // POOL_EVERY)
                nc.scalar.copy(bs_sb[:], ps[:, 0:2, 0:WH]).then_inc(s.bs_ready, 1)

            def exps(h, before, last):
                for c in range(2 * CH):
                    act.wait_ge(s.dp_ready if pool_adds(c) else s.d_ready, nth(h, c))
                    if pool_adds(c):
                        act.wait_ge(s.w_ready, h * 2 * CH + c)
                    nc.scalar.activation(e_sb[:, c % NE], d_sb[:, c % ND], ACT.Exp, bias=eps_sb[:, 2:3]).then_inc(s.e_ready, 1)
                    if c % POOL_EVERY == EVAC_AT:
                        if c + POOL_EVERY < 2 * CH:
                            pool_scores_out(h, c + POOL_EVERY - EVAC_AT, True)
                        elif not last:
                            pool_scores_out(h + 1, 0, True)
                    if before is not None:
                        if c == 1:
                            sums_out(before)
                        attend(before, c)

            act.wait_ge(s.in_wqo, 16)
            pool_scores_out(0, 0, False)
            exps(0, None, False)
            with act.Fori(0, H - 2) as i:
                exps(i + 1, i, False)
            exps(H - 1, H - 2, True)
            sums_out(H - 1)
            head_weights(H - 1)
            for step in (queries_out, prob_exps, values_out, probs_out):
                for a in range(2):
                    step(H - 1, a, TAIL_BANK[a])

            preload_sqrt()
            ln_act("lna", HALF_T, (2, 4))
            act.wait_ge(s.fir_w, 1)
            for a in range(2):
                act.wait_ge(ln.out, LN_BASE["lna"] + a + 1)
                nc.scalar.copy(xpad[0:D, 2 * a:2 * a + 2, FAR:FAR + T],
                               xl[:, 2 * a * T:(2 * a + 2) * T].rearrange("p (b t) -> p b t", b=2)).then_inc(s.fir_in, 1)
            act.wait_ge(s.fir_tb, 1)
            nc.scalar.activation(tot[:, 2], ps[0:D, 6, 0:NB], ACT.Identity, bias=col("l1_bias")).then_inc(s.fir_tbs, 1)

            ln_act("lnm", HALF_T, (2, 4), apart=True)
            def rectify(p, l):
                done, hid = (s.moe_h1, s.moe_h2)[l], (h1, h2)[l]
                act.wait_ge(done, p + 1)
                if l == 1 and p >= 2:
                    act.wait_ge(s.moe_y, p - 1)
                nc.scalar.activation(hid[:, p % 2].rearrange("p b t -> p (b t)").rearrange("p (a n) -> p a n", a=2),
                                     ps[:, 2 * l:2 * l + 2, 0:2 * T], ACT.Relu, bias=bn[:, 1, p, l:l + 1],
                                     scale=bn[:, 0, p, l:l + 1]).then_inc((s.moe_a1, s.moe_a2)[l], 1)

            act.wait_ge(s.bn_ready, 1)
            rectify(0, 0)
            act.wait_ge(s.moe_nm, 1)
            for f, rows in ((0, TILE), (1, T - TILE)):
                last = nc.scalar.activation(lg[0:rows, 1, f], lg[0:rows, 0, f], ACT.Exp, bias=lsum[0:rows, 0, f:f + 1],
                                            accum_out=lsum[0:rows, 1, f:f + 1])
            last.then_inc(s.moe_le, 1)
            for p in range(EP):
                if p:
                    rectify(p, 0)
                rectify(p, 1)
                if p == 0:
                    act.wait_ge(s.moe_gt, 1)
                    nc.scalar.copy(gt[:], ps[0:E_, 7, 0:T]).then_inc(s.moe_gts, 1)
                    act.wait_ge(s.moe_gb, 1)
                    nc.scalar.copy(gb.rearrange("p (c a) t -> p c (a t)", c=2), ps[:, 6:8, 0:2 * T]).then_inc(s.moe_gbs, 1)

        @block.vector
        def _(dve_):
            nonlocal dve
            dve = dve_
            dve.wait_ge(s.in_x, 16)
            dve.wait_ge(s.tok_mean, 1)
            nc.vector.tensor_tensor(tk[:, 0], x_sb[:], ps[0:PC, 0, 0:TOK].unsqueeze(1).broadcast_to([PC, 2, TOK]),
                                    ALU.subtract).then_inc(s.tok_xc, 1)
            dve.wait_ge(s.tok_std, 1)
            link(nc.vector.reciprocal(tk[:, 2, 1], tk[:, 2, 0]))
            dve.wait_ge(s.in_tokp, 16)
            for c in range(2):
                link(nc.vector.tensor_tensor(tk[:, 3, c], tk[:, 0, c], tk[:, 2, 1], ALU.mult))
            for c in range(2):
                nc.vector.tensor_scalar(tk[:, 3, c], tk[:, 3, c], tokp_sb[:, c:c + 1], tokp_sb[:, 2 + c:3 + c],
                                        ALU.mult, ALU.add).then_inc(s.tok_xn, 1)
            dve.wait_ge(s.ssm_n2, 1)
            nc.vector.reciprocal(sp_[:, 8:9], sp_[:, 7:8]).then_inc(s.ssm_rn, 1)
            dve.wait_ge(s.in_p64, 16)

            def invert_r(ready, done):
                dve.wait_ge(ready, 1)
                link(nc.vector.tensor_scalar(sp_[:, 20:21], sp_[:, 13:14], 1e-30, None, ALU.max))
                nc.vector.reciprocal(sp_[:, 14:15], sp_[:, 20:21]).then_inc(done, 1)

            invert_r(s.ssm_r0, s.ssm_rinv)
            ln_dve("ln2", tz[:, 0], tz[:, 1], [(0, TOK)], (3, 4), (col("ln2_g"), col("ln2_b")),
                   between=lambda: invert_r(s.ssm_r, s.ssm_ri2))
            ln_dve("lnp", tz[:, 2], tz[:, 3], [(0, TOK)], (6, 7), (col("lnp_g"), col("lnp_b")))
            dve.wait_ge(s.silu_e, 1)
            link(nc.vector.tensor_scalar(tz[:, 4], tz[:, 4], 1.0, None, ALU.add))
            link(nc.vector.reciprocal(tz[:, 5], tz[:, 4]))
            nc.vector.tensor_tensor(tz[:, 4], tz[:, 3], tz[:, 5], ALU.mult).then_inc(s.silu_out, 1)
            ln_dve("lns", u_sb, x1, [(0, TOK + 1)], (1, 2))
            dve.wait_ge(s.ssm_bx, 1)
            dve.wait_ge(s.ssm_phase, 1)
            v = vq[:, 0, 0:TIMED].rearrange("p (b t) -> p b t", b=NB)
            bx = ps[:, 0, 0:TOK + 1]
            nc.vector.tensor_scalar(v[:, :, 0], bx[:, TOK:TOK + 1].broadcast_to([128, NB]), pin[:, 0:1], None, ALU.mult)
            for b in range(NB):
                last = nc.vector.tensor_tensor(
                    v[:, b, 1:T].rearrange("p (s j) -> p s j", s=REP),
                    bx[:, b * SEG:(b + 1) * SEG].unsqueeze(1).broadcast_to([128, REP, SEG]),
                    pin[:, 1:T].rearrange("p (s j) -> p s j", s=REP), ALU.mult)
                if b < NB - 1:
                    last.then_inc(s.dve_chain, 1)
                    nlink[0] += 1
            link(last)
            dve.wait_ge(s.ssm_r, 1)
            for b in range(NB):
                nc.vector.tensor_tensor_scan(g_sb[:, b], sp_[:, 13:14].broadcast_to([128, T]), v[:, b], 0.0,
                                             ALU.mult, ALU.add).then_inc(s.ssm_g, 1)
            dve.wait_ge(s.ssm_g, NB)
            nc.vector.tensor_copy(vq[:, 0, CLS:CLS + 1], g_sb[:, 0, 0:1])
            nc.vector.tensor_tensor(vq[:, 0, 0:CLS].rearrange("p (b t) -> p b t", b=NB), g_sb[:, :, 1:T],
                                    ph[:, 0, 1:T].unsqueeze(1).broadcast_to([128, NB, T - 1]),
                                    ALU.mult).then_inc(s.ssm_q, 1)
            for i, (a, b) in enumerate(HALF_F):
                dve.wait_ge(s.ssm_y, i + 1)
                for bb in (2 * i, 2 * i + 1):
                    last = nc.vector.tensor_tensor(
                        res[:, bb * (T - 1):(bb + 1) * (T - 1)].rearrange("p (s j) -> p s j", s=REP),
                        ps[0:D, 1 + i, (bb % 2) * (T - 1):(bb % 2 + 1) * (T - 1)].rearrange("p (s j) -> p s j", s=REP),
                        u_sb[:, bb * SEG:(bb + 1) * SEG].unsqueeze(1).broadcast_to([D, REP, SEG]), ALU.add)
                    if bb == 3:
                        link(last)
                        last = nc.vector.tensor_tensor(res[:, CLS:CLS + 1], ps[0:D, 2, b - 1 - a:b - a],
                                                       u_sb[:, TOK:TOK + 1], ALU.add)
                last.then_inc(s.res_flat, 1)
            ln_dve("lnf", res, x2, HALF_F, (3, 5))
            dve.wait_ge(s.bn_sd, 1)
            nc.vector.reciprocal(bn[:, 0], bn[:, 3]).then_inc(s.bn_rec, 1)

            def shaped(ap):
                return ap.rearrange("p (b t) -> p b t", b=NB)

            dve.wait_ge(ln.out, LN_BASE["lnf"] + 2)
            for dst, src in ((rest, res), (x2t, x2)):
                nc.vector.tensor_copy(shaped(dst[:])[:, :, 1:T], shaped(src[:, 0:CLS]))
                nc.vector.tensor_copy(shaped(dst[:])[:, :, 0], src[:, CLS:FLAT].broadcast_to([D, NB])
                                      ).then_inc(s.timed_ready, 1)

            def denominator(u, n, rows, nh=H):
                dve.wait_ge(s.cut_es, n + 1)
                nc.vector.reduce_sum(zsum[0:rows, 0:nh], ez[0:rows, 1, 0:nh], AX).then_inc(s.z_sum, 1)
                dve.wait_ge(s.z_sum, n + 1)
                nc.vector.reciprocal(zinv[0:rows, u, 0:nh], zsum[0:rows, 0:nh]).then_inc(s.zinv_ready, 1)

            def top_link(n, k, last, between=lambda: None):
                last.then_inc(s.top_chain, 1)
                between()
                dve.wait_ge(s.top_chain, n * TOP_LINKS + k)
                settle(dve)

            def first_best(u, rows, nh, part):
                last = None
                lo, hi = (0, 2 * nh) if part is None else (2 * nh * part // 4, 2 * nh * (part + 1) // 4)
                for f in range(lo, hi):
                    last = nc.vector.max(top[0:rows, f, 0:8], sim[0:rows, u, f])
                return last

            def best_sums(u, n, rows, nh=H, first=False):
                sm, tp = sim[0:rows, u], top[0:rows]
                dve.wait_ge(s.first_done, n + 1)
                settle(dve)
                for f in range(2 * nh):
                    last = nc.vector.match_replace(rest_sims[0:rows, f], tp[:, f, 0:8], sm[:, f], NEG)
                top_link(n, 1, last)
                if not first:
                    denominator(1 - u, n - 1, TILE)
                    settle(dve)
                for f in range(2 * nh):
                    last = nc.vector.max(tp[:, f, 8:16], rest_sims[0:rows, f])
                top_link(n, 2, last)
                cd = [cand[0:rows, v, 0:nh] for v in range(2)]
                f0, f1 = tp[:, 0:nh], tp[:, nh:2 * nh]
                nc.vector.scalar_tensor_tensor(cut[0:rows, 0, 0:nh], f1[:, :, TOPK - 1], -1.0, f1[:, :, 0], ALU.mult, ALU.max)
                at = 0
                a = 0
                while a < TOPK:
                    m = STAIR[a]
                    e = a
                    while e < TOPK and STAIR[e] == m:
                        e += 1
                    shape = [rows, nh, e - a, m]
                    last = nc.vector.tensor_tensor(
                        cd[0][:, :, at:at + (e - a) * m].rearrange("p h (x y) -> p h x y", y=m),
                        f0[:, :, a:e].unsqueeze(3).broadcast_to(shape),
                        f1[:, :, 0:m].unsqueeze(2).broadcast_to(shape), ALU.add)
                    at += (e - a) * m
                    a = e
                top_link(n, 3, last)
                for h in range(nh):
                    last = nc.vector.max(best[0:rows, h, 0:8], cd[0][:, h])
                top_link(n, 4, last)
                for h in range(nh):
                    last = nc.vector.match_replace(cd[1][:, h], best[0:rows, h, 0:8], cd[0][:, h], NEG)
                top_link(n, 5, last)
                for h in range(nh):
                    last = nc.vector.max(best[0:rows, h, 8:16], cd[1][:, h])
                top_link(n, 6, last)

            def cut_sums(u, n, rows, nh=H, after=None, first=False):
                stt = nc.vector.scalar_tensor_tensor
                c0, c1, c2 = (cut[0:rows, v, 0:nh] for v in range(3))
                v16 = best[0:rows, 0:nh, TOPK - 1]
                last = stt(c1, v16, -1.0, c0, ALU.mult, ALU.max)
                top_link(n, 7, last)
                if after:
                    dve.wait_ge(s.sims_ready, 2 * n + 4)
                last = nc.vector.tensor_tensor(c1, c1, v16, ALU.max)
                top_link(n, 8, last, lambda: after and first_best(1 - u, *after, 0))
                last = stt(c0, c1, -SLACK, v16, ALU.mult, ALU.add)
                top_link(n, 9, last, lambda: after and first_best(1 - u, *after, 1))
                if not first:
                    dve.wait_ge(s.s0p_ready, n)
                last = stt(c2, best[0:rows, 0:nh, 0], -GUARD, c0, ALU.add, ALU.max)
                if after:
                    settle(dve)
                top_link(n, 10, last, lambda: after and first_best(1 - u, *after, 2))
                if after:
                    last = first_best(1 - u, *after, 3)
                    last.then_inc(s.first_done, 1)
                nc.vector.tensor_tensor(ez[0:rows, 0, 0:nh], best[0:rows, 0:nh, 0:TOPK],
                                        c2.unsqueeze(2).broadcast_to([rows, nh, TOPK]), ALU.subtract).then_inc(s.cut_e, 1)

            dve.wait_ge(s.sims_ready, 2)
            first_best(0, TILE, H, None).then_inc(s.first_done, 1)
            best_sums(0, 0, TILE, first=True)
            cut_sums(0, 0, TILE, after=(TILE, H), first=True)
            with dve.Fori(0, NTILE // 2 - 1) as i:
                for k in range(2):
                    best_sums(1 - k, 2 * i + 1 + k, TILE)
                    cut_sums(1 - k, 2 * i + 1 + k, TILE, after=(TILE, H))
            best_sums(1, NTILE - 1, TILE)
            cut_sums(1, NTILE - 1, TILE, after=(H, 1))
            best_sums(0, NTILE, H, 1)
            cut_sums(0, NTILE, H, 1)
            denominator(0, NTILE, H, 1)

            dve.sem_inc(s.w_used, NW)
            dve.sem_inc(s.w_ready, 1)
            dve.wait_ge(s.even_ready, 1)
            dve.wait_ge(s.tr0_read, NTILE + 2)

            def add(h, c):
                dve.wait_ge(s.b_ready, h * 2 * CH + c + 2)
                nc.vector.tensor_tensor(d_sb[:, c % ND].rearrange("p (a n) -> p a n", a=2),
                                        ps[:, 2 * ((c + 1) % 2):2 * ((c + 1) % 2) + 2, 0:WH],
                                        s0t[:, bass.ds(h, 1), :].rearrange("p o (a n) -> p (o a) n", a=2),
                                        ALU.add).then_inc(s.d_ready, 1)

            def weigh(h, c):
                dve.wait_ge(s.e_ready, h * 2 * CH + c + 1)
                dve.wait_ge(s.w_used, h * 2 * CH + c + 1)
                nc.vector.scalar_tensor_tensor(w_sb[:, c % NW], d_sb[:, c % ND], 0.0, e_sb[:, c % NE],
                                               ALU.is_ge, ALU.mult).then_inc(s.w_ready, 1)

            def normed_kv(h, a, q=6):
                if a:
                    return
                dve.wait_ge(s.acc_read, 2 * h + 4)
                dve.wait_ge(s.vw_done, 2 * h + 1)
                kh, zh = kv[:, bass.ds(h, 1), :], zbc[:, bass.ds(h, 1), :]
                nc.vector.tensor_tensor(kvh[:, :, 1:T], kh[:, :, 0:CLS].rearrange("p o (b t) -> p (o b) t", b=NB),
                                        zh[:, :, 0:CLS].rearrange("p o (b t) -> p (o b) t", b=NB), ALU.mult)
                nc.vector.tensor_tensor(kvh[:, :, 0:1], kh[:, :, CLS:FLAT].broadcast_to([128, NB, 1]),
                                        zh[:, :, CLS:FLAT].broadcast_to([128, NB, 1]), ALU.mult).then_inc(s.kvh_ready, 1)

            def mask_scores(h, a, q=6):
                n1, b2 = T - TILE, slice(2 * a, 2 * a + 2)
                dve.wait_ge(s.qk_done, 2 * h + a + 1)
                nc.vector.tensor_tensor(a0[:, b2], ps[:, q, 0:2 * TILE].rearrange("p (b j) -> p b j", b=2),
                                        mask0.unsqueeze(1).broadcast_to([TILE, 2, TILE]), ALU.add)
                nc.vector.tensor_tensor(a1[:, b2], ps[0:n1, q + 1, 0:2 * T].rearrange("p (b j) -> p b j", b=2),
                                        mask1.unsqueeze(1).broadcast_to([n1, 2, T]), ALU.add).then_inc(s.sc_ready, 1)
                dve.wait_ge(s.sc_ready, 2 * h + a + 1)
                nc.vector.tensor_reduce(amax[:, 0, b2], a0[:, b2], AX, ALU.max, negate=True)
                nc.vector.tensor_reduce(amax[0:n1, 1, b2], a1[:, b2], AX, ALU.max, negate=True).then_inc(s.nm_ready, 1)

            def normed_probs(h, a, q=6):
                n1, b2 = T - TILE, slice(2 * a, 2 * a + 2)
                dve.wait_ge(s.p_exp, 2 * h + a + 1)
                nc.vector.reciprocal(arec[:, 0, b2], asum[:, 0, b2])
                nc.vector.reciprocal(arec[0:n1, 1, b2], asum[0:n1, 1, b2]).then_inc(s.rec_ready, 1)
                dve.wait_ge(s.rec_ready, 2 * h + a + 1)
                nc.vector.tensor_tensor(a0[:, b2], a0[:, b2], arec[:, 0, b2].unsqueeze(2).broadcast_to([TILE, 2, TILE]), ALU.mult)
                nc.vector.tensor_tensor(a1[:, b2], a1[:, b2], arec[0:n1, 1, b2].unsqueeze(2).broadcast_to([n1, 2, T]),
                                        ALU.mult).then_inc(s.p_ready, 1)

            def to_residual(h, a, q=6):
                dve.wait_ge(s.pv_done, 2 * h + a + 1)
                for b in range(2):
                    r = rest[:, (2 * a + b) * T:(2 * a + b + 1) * T]
                    last = nc.vector.tensor_tensor(r, r, ps[b * D:(b + 1) * D, q + 1, b * T:(b + 1) * T], ALU.add)
                last.then_inc(s.res_att, 1)

            def attend(h, c):
                for at, step in ((KV_AT, normed_kv), (MASK_AT, mask_scores), (NORM_AT, normed_probs), (RES_AT, to_residual)):
                    if c % HALF_CH == at:
                        step(h, c // HALF_CH)

            def head(h, before, last):
                for c in range(2 * CH):
                    if c < 2 * CH - 1:
                        if not pool_adds(c + 1):
                            add(h, c + 1)
                    elif not last:
                        add(h + 1, 0)
                    weigh(h, c)
                    if before is not None:
                        attend(before, c)

            add(0, 0)
            head(0, None, False)
            with dve.Fori(0, H - 2) as i:
                head(i + 1, i, False)
            head(H - 1, H - 2, True)
            for step in (normed_kv, mask_scores, normed_probs, to_residual):
                for a in range(2):
                    step(H - 1, a, TAIL_BANK[a])

            def shift_half(a):
                if a == 0:
                    dve.wait_ge(s.fir_w, 1)
                dve.wait_ge(ln.out, LN_BASE["lna"] + a + 1)
                nc.vector.tensor_copy(xpad[D:128, 2 * a:2 * a + 2, FAR + 1:FAR + T],
                                      xl[:, 2 * a * T:(2 * a + 2) * T].rearrange("p (b t) -> p b t", b=2)[:, :, 0:T - 1]
                                      ).then_inc(s.fir_pad, 1)

            ln_dve("lna", rest, xl, HALF_T, (2, 4), after=shift_half)
            link(nc.vector.reduce_sum(tot[:, 0], shaped(xl), AX))
            nc.vector.tensor_scalar(tot[:, 1], tot[:, 0], col("m0"), None, ALU.mult).then_inc(s.fir_tot, 1)
            dve.wait_ge(s.fir_tbs, 1)
            for b in range(NB):
                if b == 2:
                    ln_centre("lnm", rest, HALF_T, (2, 4), 0)
                    ln_scale("lnm", xl, HALF_T, 0)
                if b % 2 == 0:
                    dve.wait_ge(s.fir_done, b // 2 + 1)
                r = rest[:, b * T:(b + 1) * T]
                nc.vector.scalar_tensor_tensor(r, ps[0:D, b // 2, (b % 2) * T:(b % 2 + 1) * T], tot[:, 2, b:b + 1], r,
                                               ALU.add, ALU.add).then_inc(s.res_fir, 1)
                dve.wait_ge(s.res_fir, 2 * b + 1)
                nc.vector.tensor_tensor(r[:, FAR:T], r[:, FAR:T], ps[D:128, b // 2, (b % 2) * T:(b % 2 + 1) * T - FAR], ALU.add
                                        ).then_inc(s.res_fir, 1)

            ln_centre("lnm", rest, HALF_T, (2, 4), 1)
            ln_scale("lnm", xl, HALF_T, 1)
            dve.wait_ge(ln.out, LN_BASE["lnm"] + 2)
            nc.vector.reduce_sum(feat[:], shaped(xl).rearrange("p b t -> p t b"), AX).then_inc(s.moe_feat, 1)
            dve.wait_ge(s.moe_log, 1)
            for f, rows in ((0, TILE), (1, T - TILE)):
                link(nc.vector.tensor_scalar(lg[0:rows, 0, f], ps[0:rows, 6, f * E_:(f + 1) * E_], 1.0 / NB, None, ALU.mult))
                last = nc.vector.tensor_reduce(lsum[0:rows, 0, f:f + 1], lg[0:rows, 0, f], AX, ALU.max, negate=True)
            last.then_inc(s.moe_nm, 1)
            dve.wait_ge(s.moe_le, 1)
            for f, rows in ((0, TILE), (1, T - TILE)):
                link(nc.vector.reciprocal(lsum[0:rows, 2, f:f + 1], lsum[0:rows, 1, f:f + 1]))
                nc.vector.tensor_scalar(lg[0:rows, 2, f], lg[0:rows, 1, f], lsum[0:rows, 2, f:f + 1], None,
                                        ALU.mult).then_inc(s.moe_gate, 1)
            dve.wait_ge(s.moe_gbs, 1)
            for p in range(EP):
                dve.wait_ge(s.moe_a2, p + 1)
                nc.vector.tensor_tensor(h2[:, p % 2], h2[:, p % 2], gb[:, p].unsqueeze(1).broadcast_to([128, NB, T]),
                                        ALU.mult).then_inc(s.moe_w2g, 1)
            dve.wait_ge(s.moe_y, EP)
            for a, (lo, hi) in enumerate(HALF_T):
                nc.vector.tensor_tensor(rest[:, lo:hi], rest[:, lo:hi], ps[0:D, 4 + a, 0:2 * T], ALU.add
                                        ).then_inc(s.out_ready, 1)

        @block.tensor
        def _(pe_):
            nonlocal pe
            pe = pe_
            mm = nc.tensor.matmul
            pe.wait_ge(s.ones_ready, 1)
            pe.wait_ge(s.in_x, 16)
            for c in range(2):
                last = mm(ps[0:PC, 0, 0:TOK], onesp[:], x_sb[:, c], start=(c == 0), stop=(c == 1))
            last.then_inc(s.tok_mean, 1)
            pe.wait_ge(s.tok_sq, 1)
            for c in range(2):
                last = mm(ps[0:PC, 1, 0:TOK], onesp[:], tk[:, 1, c], start=(c == 0), stop=(c == 1))
            last.then_inc(s.tok_var, 1)
            pe.wait_ge(s.tok_xn, 2)
            for c in range(2):
                last = mm(ps[0:D, 2, 0:TOK], tokp_sb[:, 4 + c * D:4 + (c + 1) * D], tk[:, 3, c],
                          start=(c == 0), stop=(c == 1))
            last.then_inc(s.tok_z, 1)
            ln_pe("ln2", tz[:, 0], s.tok_zb, [1], [(0, TOK)], (3, 4))
            pe.wait_ge(ln.out, LN_BASE["ln2"] + 1)
            mm(ps[0:D, 5, 0:TOK], col("Wp1", D), tz[:, 1], start=True, stop=True).then_inc(s.tok_h, 1)
            ln_pe("lnp", tz[:, 2], s.tok_hb, [1], [(0, TOK)], (6, 7))
            pe.wait_ge(s.silu_out, 1)
            mm(ps[0:D, 0, 0:TOK], col("Wp2", D), tz[:, 4], start=True, stop=True).then_inc(s.tok_o, 1)
            pe.wait_ge(s.cls_ready, 1)
            ln_pe("lns", u_sb, s.tok_ready, [1], [(0, TOK + 1)], (1, 2))
            pe.wait_ge(ln.out, LN_BASE["lns"] + 1)
            mm(ps[:, 0, 0:TOK + 1], col("BT2", 128), x1[:], start=True, stop=True).then_inc(s.ssm_bx, 1)
            pe.wait_ge(s.in_keys, 16)
            for q in range(4):
                for g in range(4):
                    last = mm(ps[0:D, 4 + q, g * NK:(g + 1) * NK], pkw_sb[DK * q:DK * q + DK, 0, g],
                              pkw_sb[DK * q:DK * q + DK, 1, g], start=True, stop=True)
                last.then_inc(s.pk_m, 1)
            pe.wait_ge(s.ssm_wc, 1)
            pe.wait_ge(s.ssm_q, 1)
            pe.wait_ge(s.ssm_q2, 1)
            for i, (a, b) in enumerate(HALF_F):
                mm(ps[0:D, 1 + i, 0:b - a], wcs[:, 0, :], vq[:, 0, a:b], start=True, stop=False)
                mm(ps[0:D, 1 + i, 0:b - a], wcs[:, 1, :], vq[:, 1, a:b], start=False, stop=True).then_inc(s.ssm_y, 1)
            pe.wait_ge(s.pk_mc, 4)
            ln_pe("lnf", res, s.res_flat, [1, 2], HALF_F, (3, 5))

            def scores(u, n, rows):
                pe.wait_ge(s.xst_ready, n + 1)
                pe.wait_ge(s.sims_ready, 2 * n)
                for k in range(2):
                    last = mm(ps[0:rows, k, :], xst[:, u, 0:rows], m_sb[:, 512 * k:512 * k + 512], start=True, stop=True)
                last.then_inc(s.sim_done, 1)

            def class_scores(n):
                pe.wait_ge(s.xst_ready, n + 1)
                pe.wait_ge(s.sims_ready, 2 * n)
                for f in range(2):
                    for h in range(H):
                        at = (f * H + h) * NK
                        last = mm(ps[0:H, 0, f * NK:(f + 1) * NK], xz[:, H - 1 - h:2 * H - 1 - h], m_sb[:, at:at + NK],
                                  start=(h == 0), stop=(h == H - 1))
                last.then_inc(s.sim_done, 1)

            def turn(u, n, rows, nh=H):
                pe.wait_ge(s.s1p_ready, n + 2)
                pe.wait_ge(s.tr1_read, n + 1)
                for f in range(2 * nh):
                    last = nc.tensor.transpose(ps[0:3 * JH, 6 + f // 8, :].bitcast(BF16)[:, (f % 8) * 128:(f % 8) * 128 + rows],
                                               s1p[0:rows, u, f].rearrange("p a k -> p (a k)"), identb[0:rows, 0:rows])
                last.then_inc(s.tr1_done, 1)
                pe.wait_ge(s.s0p_ready, n + 1)
                pe.wait_ge(s.tr0_read, n + 1)
                for h in range(nh):
                    last = nc.tensor.transpose(ps[:, 2 + h // 4, (h % 4) * 128:(h % 4) * 128 + rows],
                                               s0p[0:rows, u, h].rearrange("p a k -> p (a k)"),
                                               ident[0:rows, 0:rows])
                last.then_inc(s.tr0_done, 1)
                pe.wait_ge(s.zinv_ready, n + 1)
                pe.wait_ge(s.trz_read, n + 1)
                for h in range(nh):
                    last = mm(ps[:, 4 + h // 4, (h % 4) * 128:(h % 4) * 128 + rows],
                              zinv[0:rows, u, h:h + 1].broadcast_to([rows, 128]), ident[0:rows, 0:rows],
                              start=True, stop=True)
                last.then_inc(s.trz_done, 1)

            pe.wait_ge(s.identb_ready, 1)
            for read in (s.tr0_read, s.tr1_read, s.trz_read):
                pe.sem_inc(read, 1)
            scores(0, 0, TILE)
            scores(1, 1, TILE)
            with pe.Fori(0, NTILE // 2 - 1) as i:
                for u in range(2):
                    scores(u, 2 * i + u + 2, TILE)
                    turn(u, 2 * i + u, TILE)
            class_scores(NTILE)
            turn(0, NTILE - 2, TILE)
            turn(1, NTILE - 1, TILE)
            turn(0, NTILE, H, 1)

            pe.wait_ge(s.sel_ready, 1)
            pe.wait_ge(s.even_ready, 1)
            pe.wait_ge(s.trz_read, NTILE + 2)

            def spread(h, p, free):
                c = spread_at(p)
                if free:
                    before = spread_at(p - 2)
                    pe.wait_ge(s.bs_ready if pool_adds(before) else s.d_ready, nth(h, before))
                for a in range(2):
                    last = mm(ps[:, 2 * (p % 2) + a, 0:WH], sel_sb[:, c % CH],
                              s1t[:, bass.ds(2 * h + c // CH, 1), a * WH:(a + 1) * WH], start=True, stop=True)
                last.then_inc(s.b_ready, 1)

            def gather(h, c):
                if c % GRP == 0:
                    pe.wait_ge(tab_in[c // GRP], 16 * (h + 1))
                pe.wait_ge(s.w_ready, h * 2 * CH + c + 2)
                for a in range(2):
                    if c == 0:
                        pe.wait_ge(s.acc_read, 2 * h + a + 1)
                    last = mm(ps[:, 4 + a, 0:WH], tab_sb[:, c // GRP, c % GRP], w_sb[:, c % NW, a * WH:(a + 1) * WH],
                              start=(c == 0), stop=(c == 2 * CH - 1))
                    if c == 2 * CH - 1 and a == 0:
                        last.then_inc(s.acc0_done, 1)
                last.then_inc(s.w_used, 1)

            n1 = T - TILE

            def queries(h, a, q=6):
                if a == 0:
                    pe.wait_ge(s.wst_ready, h + 1)
                    settle(pe)
                lo, hi = HALF_T[a]
                mm(ps[0:D, q, 0:2 * T], wst[0:D], x2t[:, lo:hi], start=True, stop=True).then_inc(s.q_done, 1)

            def key_scores(h, a, q=6):
                pe.wait_ge(s.q_ready, 2 * h + a + 1)
                if a == 0 or q == 6:
                    pe.wait_ge(s.res_att, 2 * h + a + 1)
                if a == 0:
                    pe.wait_ge(s.kvh_ready, h + 1)
                for b in range(2):
                    mm(ps[:, q, b * TILE:(b + 1) * TILE], q_sb[:, 2 * a + b, 0:TILE], kvh[0:D, 2 * a + b, 0:TILE],
                       start=True, stop=True)
                for b in range(2):
                    last = mm(ps[0:n1, q + 1, b * T:(b + 1) * T], q_sb[:, 2 * a + b, TILE:T], kvh[0:D, 2 * a + b],
                              start=True, stop=True)
                last.then_inc(s.qk_done, 1)

            def values(h, a, q=6):
                pe.wait_ge(s.sc_ready, 2 * h + a + 1)
                for b in range(2):
                    mm(ps[:, q, b * D:(b + 1) * D], kvh[D:128, 2 * a + b, 0:TILE], wst[D:128], start=True, stop=True)
                for b in range(2):
                    at = 2 * D + b * D
                    last = mm(ps[0:n1, q, at:at + D], kvh[D:128, 2 * a + b, TILE:T], wst[D:128], start=True, stop=True)
                last.then_inc(s.vw_done, 1)

            def turn_probs(h, a, q=6):
                pe.wait_ge(s.vw_ready, 2 * h + a + 1)
                pe.wait_ge(s.p_ready, 2 * h + a + 1)
                for b in range(2):
                    at = 2 * TILE + b * n1
                    nc.tensor.transpose(ps[:, q, b * TILE:(b + 1) * TILE], a0[:, 2 * a + b], ident)
                    nc.tensor.transpose(ps[:, q, at:at + n1], a1[:, 2 * a + b, 0:TILE], ident[0:n1, 0:n1])
                    last = nc.tensor.transpose(ps[0:n1, q + 1, b * n1:(b + 1) * n1], a1[:, 2 * a + b, TILE:T], ident[0:n1, 0:n1])
                last.then_inc(s.pt_done, 1)

            def output(h, a, q=6):
                pe.wait_ge(s.pt_ready, 2 * h + a + 1)
                settle(pe)
                y = [ps[b * D:(b + 1) * D, q + 1, b * T:(b + 1) * T] for b in range(2)]
                for b in range(2):
                    mm(y[b][:, 0:TILE], vw0[:, 2 * a + b], pt0[:, 2 * a + b], start=True, stop=True)
                for b in range(2):
                    mm(y[b][:, TILE:T], vw0[:, 2 * a + b], pt1[:, 2 * a + b], start=True, stop=False)
                for b in range(2):
                    last = mm(y[b][:, TILE:T], vw1[:, 2 * a + b], pt2[:, 2 * a + b], start=False, stop=True)
                last.then_inc(s.pv_done, 1)

            def attend(h, c):
                for at, step in ((Q_AT, queries), (QK_AT, key_scores), (VW_AT, values), (PT_AT, turn_probs), (Y_AT, output)):
                    if c % HALF_CH == at:
                        step(h, c // HALF_CH)

            def pe_head(h, before, last):
                for c in range(2 * CH):
                    if c < 2 * CH - AHEAD:
                        spread(h, c + AHEAD, True)
                    elif not last:
                        spread(h + 1, c - (2 * CH - AHEAD), True)
                    gather(h, c)
                    if before is not None:
                        attend(before, c)

            pe.wait_ge(s.timed_ready, 2)
            pe.sem_inc(s.acc_read, 2)
            pe.sem_inc(s.res_att, 1)
            pe.sem_inc(s.vw_done, 1)
            for p in range(AHEAD):
                spread(0, p, p >= 2)
            pe_head(0, None, False)
            with pe.Fori(0, H - 2) as i:
                pe_head(i + 1, i, False)
            pe_head(H - 1, H - 2, True)
            for step in (queries, key_scores, values, turn_probs, output):
                for a in range(2):
                    step(H - 1, a, TAIL_BANK[a])

            ln_pe("lna", rest, s.res_att, [2 * H, 2 * H + 1], HALF_T, (2, 4))
            pe.wait_ge(s.fir_w, 1)
            for a in range(2):
                pe.wait_ge(s.fir_in, a + 1)
                pe.wait_ge(s.fir_pad, a + 1)
                for k in range(NEARS):
                    if a == 1 and k == MEAN_K:
                        ln_mean(rest, s.res_fir, [4, 8], HALF_T, (2, 4), 0)
                    if a == 1 and k == VAR_K:
                        ln_var("lnm", HALF_T, (2, 4), 0)
                    last = mm(ps[:, a, 0:2 * T], firw[:, k].rearrange("p s d -> p (s d)"),
                              xpad[:, 2 * a:2 * a + 2, FAR - 2 * k:FAR - 2 * k + T], start=(k == 0), stop=(k == NEARS - 1))
                last.then_inc(s.fir_done, 1)
                if a == 0:
                    pe.wait_ge(s.fir_tot, 1)
                    mm(ps[0:D, 6, 0:NB], col("W2", D), tot[:, 1], start=True, stop=True).then_inc(s.fir_tb, 1)

            ln_mean(rest, s.res_fir, [4, 8], HALF_T, (2, 4), 1)
            ln_var("lnm", HALF_T, (2, 4), 1)
            pe.wait_ge(s.in_moe_w, 16)
            pe.wait_ge(ln.out, LN_BASE["lnm"] + 2)

            def layer1(p):
                if p:
                    pe.wait_ge(s.moe_a1, p)
                for a, (lo, hi) in enumerate(HALF_T):
                    last = mm(ps[:, a, 0:2 * T], w1m[:, p * 128:(p + 1) * 128], xl[:, lo:hi], start=True, stop=True)
                last.then_inc(s.moe_h1, 1)

            layer1(0)
            pe.wait_ge(s.moe_feat, 1)
            for f, rows in ((0, TILE), (1, T - TILE)):
                lo = f * TILE
                mm(ps[0:rows, 6, f * E_:(f + 1) * E_], feat[:, lo:lo + rows], col("Wr", E_), start=True, stop=False)
                last = mm(ps[0:rows, 6, f * E_:(f + 1) * E_], four[:, 0:rows], brm, start=False, stop=True)
            last.then_inc(s.moe_log, 1)
            for p in range(EP):
                pe.wait_ge(s.moe_a1, p + 1)
                if p:
                    pe.wait_ge(s.moe_a2, p)
                for a in range(2):
                    last = mm(ps[:, 2 + a, 0:2 * T], w2m[:, p], h1[:, p % 2, 2 * a:2 * a + 2], start=True, stop=True)
                last.then_inc(s.moe_h2, 1)
                if p < EP - 1:
                    layer1(p + 1)
                if p == 0:
                    pe.wait_ge(s.moe_gate, 2)
                    for f, rows in ((0, TILE), (1, T - TILE)):
                        last = nc.tensor.transpose(ps[0:E_, 7, f * TILE:f * TILE + rows], lg[0:rows, 2, f], ident[0:rows, 0:rows])
                    last.then_inc(s.moe_gt, 1)
                    pe.wait_ge(s.moe_gts, 1)
                    for q in range(EP):
                        last = mm(ps[:, 6 + q // 2, (q % 2) * T:(q % 2 + 1) * T], e8m[:, q], gt[:], start=True, stop=True)
                    last.then_inc(s.moe_gb, 1)
                    for a in range(2):
                        mm(ps[0:D, 4 + a, 0:2 * T], bom, gt[:].unsqueeze(1).broadcast_to([E_, 2, T]), start=True, stop=False)
                pe.wait_ge(s.moe_w2g, p + 1)
                for a in range(2):
                    last = mm(ps[0:D, 4 + a, 0:2 * T], wom[:, p, 0:D], h2[:, p % 2, 2 * a:2 * a + 2],
                              start=False, stop=(p == EP - 1))
                last.then_inc(s.moe_y, 1)


def layouts(inp):
    import numpy as np
    f = {k: np.asarray(v) for k, v in inp.items()}
    a = {}
    x = f["x"].reshape(NB, 3, 8, 8, 8, 8)
    a["xT"] = x.transpose(3, 5, 1, 0, 2, 4).reshape(2, PC, TOK).transpose(1, 0, 2)
    two = lambda v: v.reshape(2, PC, -1).transpose(1, 0, 2).reshape(PC, -1)
    a["tokp"] = np.concatenate([two(f["L0_tok_ln1_g"]), two(f["L0_tok_ln1_b"]), two(f["L0_tok_W1"])], axis=1)
    c1 = lambda v: v.reshape(D, 1)
    BT = f["L0_attn_B"].T
    a["p64"] = np.concatenate(
        [c1(f[k]) for k in ("L0_tok_b1", "L0_tok_ln2_g", "L0_tok_ln2_b", "L0_tok_bp1", "L0_tok_lnp_g",
                            "L0_tok_lnp_b", "L0_tok_bp2", "cls_tok", "L1_attn_bias")]
        + [c1(f["L1_attn_memory_weights"][0]), f["L0_tok_Wp1"], f["L0_tok_Wp2"], BT, BT,
           f["L1_attn_W1"], f["L1_attn_W2"], f["L1_ffn_Wr"]], axis=1)
    d2 = lambda v: np.concatenate([v, v]).reshape(128, 1)
    Cr, Ci = f["L0_attn_C_real"].T, f["L0_attn_C_imag"].T
    a["p128"] = np.concatenate([d2(f["L0_attn_log_lambda_real"]), d2(f["L0_attn_lambda_imag"]), d2(f["L0_attn_log_dt"]),
                                np.concatenate([Cr, Ci]), np.concatenate([Ci, Cr])], axis=1)
    const = np.zeros((128, CC["end"]), np.float32)
    const[:, :128] = np.eye(128)
    i, j = np.arange(TILE)[:, None], np.arange(T)[None, :]
    const[:, CC["m0"]:CC["m0"] + TILE] = np.where(j[:, :TILE] <= i, 0.0, NEG)
    const[:T - TILE, CC["m1"]:CC["m1"] + T] = np.where(j <= TILE + i[:T - TILE], 0.0, NEG)
    a["const"] = const
    sel = np.zeros((3, JH, CH, 2, NK), np.float32)
    for n in range(JH):
        sel[:, n, n // 2, n % 2, :] = 1.0
    a["sel"] = sel.reshape(3 * JH, CH, 128)
    wq = f["L0_ffn_Wq_pk"].T.reshape(4, 4, DK, D).transpose(1, 2, 0, 3)
    kk = f["L0_ffn_pk_keys"].transpose(0, 2, 3, 1).reshape(4, 4, DK, NK).transpose(1, 2, 0, 3)
    a["pkw"] = np.stack([wq.reshape(128, 4, D), kk.reshape(128, 4, NK)], axis=1)
    tab = np.concatenate([f["L0_ffn_keys_table"], f["L0_ffn_values_table"]], axis=1)
    a["table"] = tab.reshape(H * 8, GRP, 128, 128).transpose(0, 2, 1, 3)
    a["wqo"] = np.concatenate([f["L0_ffn_Wq"].reshape(D, H, D).transpose(1, 0, 2), f["L0_ffn_Wo"].reshape(H, D, D)],
                              axis=1).transpose(1, 0, 2)
    mw = np.zeros((2 * PAIRS, D), np.float32)
    mw[:TAPS + 1] = f["L1_attn_memory_weights"]
    both = lambda v: np.concatenate([v, v])
    a["fir"] = np.concatenate([mw.reshape(PAIRS, 2, D).transpose(1, 2, 0).reshape(128, PAIRS), d2(f["L1_attn_memory_weights"][0]),
                               both(f["L1_attn_W2"]), both(f["L1_attn_W1"])], axis=1)
    prm = np.stack([f["L1_ffn_" + k] for k in ("b1", "g1", "be1", "m1", "v1", "b2", "g2", "be2", "m2", "v2")])
    a["moe"] = prm.reshape(MOE_P, 4, 128).transpose(2, 1, 0)
    e8 = np.zeros((E_, 4, 2, D), np.float32)
    for e in range(E_):
        e8[e, e // 2, e % 2] = 1.0
    w = np.zeros((5, 128, E_ * D), np.float32)
    w[0, :D] = f["L1_ffn_W1"].transpose(1, 0, 2).reshape(D, E_ * D)
    w2 = f["L1_ffn_W2"].reshape(4, 2, D, D)
    for q in range(2):
        w[1].reshape(128, 4, 128)[q * D:(q + 1) * D, :, q * D:(q + 1) * D] = w2[:, q].transpose(1, 0, 2)
    w[2].reshape(128, 4, 128)[:, :, :D] = f["L1_ffn_Wo"].reshape(4, 128, D).transpose(1, 0, 2)
    w[3, :E_, :D] = f["L1_ffn_bo"]
    w[3, 0, D:D + E_] = f["L1_ffn_br"]
    w[4, :E_] = e8.reshape(E_, 512)
    a["moe_w"] = w.transpose(1, 0, 2)
    return {k: np.ascontiguousarray(v) for k, v in a.items()}


def kernel(**inputs):
    import numpy as _np
    import concourse.bacc as _bacc
    from concourse import mybir as _mybir
    from concourse.bass_utils import run_bass_kernel_spmd as _run

    nc = _bacc.Bacc("TRN2", target_bir_lowering=False, num_devices=1)
    arrays, args = {}, {}
    for name, a in layouts(inputs).items():
        arrays[f"in_{name}"] = a
        args[name] = nc.dram_tensor(f"in_{name}", a.shape, _mybir.dt.from_np(a.dtype), kind="ExternalInput").ap()
    out = nc.dram_tensor("out", (D, TIMED), F32, kind="ExternalOutput").ap()
    tower(nc, out=out, **args)
    r = _run(nc, [arrays], core_ids=[0])
    return _np.ascontiguousarray(r.results[0]["out"].T).reshape(NB, T, D)
```
